# Optimizing a Trainium2 kernel written in Bass

```python
import numpy as np
import jax
import jax.numpy as jnp

def _softmax(x, axis=-1):
    return jax.nn.softmax(x, axis=axis)

def _gelu(x):
    return jax.nn.gelu(x, approximate=True)

def _silu(x):
    return jax.nn.silu(x)

def _sigmoid(x):
    return jax.nn.sigmoid(x)

def _layernorm(x, axis=-1, eps=1e-05):
    m = jnp.mean(x, axis=axis, keepdims=True)
    v = jnp.var(x, axis=axis, keepdims=True)
    return (x - m) / jnp.sqrt(v + eps)

def _scatter_add(tgt, idx, src, axis=0):
    return tgt.at[idx].add(src)

def _segment_sum(src, seg, n):
    return jax.ops.segment_sum(src, seg, n)
kernel_name = 'mk_decoder_preln_d2_seqx_r4_adc63c'

def setup_inputs(seed: int=0):
    np.random.seed(seed)
    _w = jnp.asarray

    def _rec_inputs():
        import jax
        import jax.numpy as jnp
        _rk = jax.random.key(seed)
        x = 0.002226 + 0.9996 * jax.random.normal(jax.random.fold_in(_rk, 1), (32, 112, 256), jnp.float32)
        _lenS = 112 - jax.random.randint(jax.random.fold_in(_rk, 7), (32,), 0, max(1, 112 // 4) + 1, jnp.int32)
        _lenS2 = 375 - jax.random.randint(jax.random.fold_in(_rk, 8), (32,), 0, max(1, 375 // 4) + 1, jnp.int32)
        _ctx_1024P = jax.random.normal(jax.random.fold_in(_rk, 11), (32, 16, 256), jnp.float32)
        _ctx_1024c = jax.random.dirichlet(jax.random.fold_in(_rk, 511), 0.3 * jnp.ones((16,), jnp.float32), (32, 375))
        _ctx_1024t = jnp.einsum('bsk,bkd->bsd', _ctx_1024c, _ctx_1024P)
        _ctx_1024t = _ctx_1024t * jax.lax.rsqrt(jnp.mean(jnp.square(_ctx_1024t)) + 1e-12) * 0.953939
        ctx_1024 = -0.000125008 + 0.999885 * (_ctx_1024t + 0.3 * jax.random.normal(jax.random.fold_in(_rk, 611), (32, 375, 256), jnp.float32))
        _validS = jnp.arange(112)[None, :] < _lenS[:, None]
        _validS2 = jnp.arange(375)[None, :] < _lenS2[:, None]
        _causal = jnp.tril(jnp.ones((112, 112), dtype=bool))
        mask_BxS2_bk1 = jnp.broadcast_to(_validS2[:, :], (32, 375))
        return (x, ctx_1024, mask_BxS2_bk1)
    x, ctx_1024, mask_BxS2_bk1 = _rec_inputs()

    def _L0_attn_setup():
        import jax, jax.numpy as jnp
        import numpy as np
        B, T, D, H, R = (1, 1024, 256, 16, 64)
        HD = D // H
        STD = 0.02

        def _low_rank_proj(x, a, b):
            mid = jnp.einsum('btd,hdr->bhtr', x, a)
            return jnp.einsum('bhtr,hrd->bhtd', mid, b)
        key = jax.random.key(seed)
        ks = jax.random.split(key, 8)
        return {'hidden_states': jax.random.normal(ks[0], (B, T, D), jnp.float32), 'q_a': STD * jax.random.normal(ks[1], (H, D, R), jnp.float32), 'q_b': STD * jax.random.normal(ks[2], (H, R, HD), jnp.float32), 'k_a': STD * jax.random.normal(ks[3], (H, D, R), jnp.float32), 'k_b': STD * jax.random.normal(ks[4], (H, R, HD), jnp.float32), 'v_w': STD * jax.random.normal(ks[5], (D, D), jnp.float32), 'v_b': jnp.zeros((D,), jnp.float32), 'o_w': STD * jax.random.normal(ks[6], (D, D), jnp.float32), 'o_b': jnp.zeros((D,), jnp.float32)}
    _L0_attn_all = _L0_attn_setup()
    _L0_attn_in = {k: v for k, v in _L0_attn_all.items() if k in ('q_a', 'q_b', 'k_a', 'k_b', 'v_w', 'v_b', 'o_w', 'o_b')}
    del _L0_attn_all

    def _L0_xattn_setup():
        import jax, jax.numpy as jnp
        import numpy as np
        DIM = 256
        DIM_HEAD = 64
        HEADS = 8
        INNER = DIM_HEAD * HEADS
        EPS = 1e-05

        def layernorm(x, g, b):
            mu = jnp.mean(x, axis=-1, keepdims=True)
            var = jnp.var(x, axis=-1, keepdims=True)
            return (x - mu) * jax.lax.rsqrt(var + EPS) * g + b
        key = jax.random.key(seed)
        ks = jax.random.split(key, 8)
        b, n, m = (8, 1024, 64)
        x = jax.random.normal(ks[0], (b, n, DIM), dtype=jnp.float32)
        latents = jax.random.normal(ks[1], (b, m, DIM), dtype=jnp.float32)
        mask = jax.random.bernoulli(ks[2], 0.9, (b, n))
        s = DIM ** (-0.5)
        Wq = jax.random.normal(ks[3], (DIM, INNER), dtype=jnp.float32) * s
        Wkv = jax.random.normal(ks[4], (DIM, 2 * INNER), dtype=jnp.float32) * s
        Wo = jax.random.normal(ks[5], (INNER, DIM), dtype=jnp.float32) * INNER ** (-0.5)
        ln_x_g = jnp.ones((DIM,), jnp.float32)
        ln_x_b = jnp.zeros((DIM,), jnp.float32)
        ln_l_g = jnp.ones((DIM,), jnp.float32)
        ln_l_b = jnp.zeros((DIM,), jnp.float32)
        ln_o_g = jnp.ones((DIM,), jnp.float32)
        ln_o_b = jnp.zeros((DIM,), jnp.float32)
        return {'x': x, 'latents': latents, 'mask': mask, 'Wq': Wq, 'Wkv': Wkv, 'Wo': Wo, 'ln_x_g': ln_x_g, 'ln_x_b': ln_x_b, 'ln_l_g': ln_l_g, 'ln_l_b': ln_l_b, 'ln_o_g': ln_o_g, 'ln_o_b': ln_o_b}
    _L0_xattn_all = _L0_xattn_setup()
    _L0_xattn_in = {k: v for k, v in _L0_xattn_all.items() if k in ('Wq', 'Wkv', 'Wo', 'ln_x_g', 'ln_x_b', 'ln_l_g', 'ln_l_b', 'ln_o_g', 'ln_o_b')}
    del _L0_xattn_all

    def _L0_ffn_setup():
        import jax, jax.numpy as jnp
        import numpy as np
        D_MODEL = 256
        D_FF = 1024
        N_EXPERTS = 8
        TOP_K = 2
        D_FF_PER = D_FF // N_EXPERTS
        B, T = (4, 512)
        key = jax.random.key(seed)
        ks = jax.random.split(key, 7)
        b1_bound = 1.0 / np.sqrt(D_MODEL)
        b2_bound = 1.0 / np.sqrt(D_FF_PER)
        return {'x': jax.random.normal(ks[0], (B, T, D_MODEL), dtype=jnp.float32), 'router_w': jax.random.uniform(ks[1], (D_MODEL, N_EXPERTS), minval=-b1_bound, maxval=b1_bound, dtype=jnp.float32), 'router_b': jax.random.uniform(ks[2], (N_EXPERTS,), minval=-b1_bound, maxval=b1_bound, dtype=jnp.float32), 'W1': jax.random.uniform(ks[3], (N_EXPERTS, D_MODEL, D_FF_PER), minval=-b1_bound, maxval=b1_bound, dtype=jnp.float32), 'b1': jax.random.uniform(ks[4], (N_EXPERTS, D_FF_PER), minval=-b1_bound, maxval=b1_bound, dtype=jnp.float32), 'W2': jax.random.uniform(ks[5], (N_EXPERTS, D_FF_PER, D_MODEL), minval=-b2_bound, maxval=b2_bound, dtype=jnp.float32), 'b2': jax.random.uniform(ks[6], (N_EXPERTS, D_MODEL), minval=-b2_bound, maxval=b2_bound, dtype=jnp.float32)}
    _L0_ffn_all = _L0_ffn_setup()
    _L0_ffn_in = {k: v for k, v in _L0_ffn_all.items() if k in ('router_w', 'router_b', 'W1', 'b1', 'W2', 'b2')}
    del _L0_ffn_all

    def _L1_attn_setup():
        import jax, jax.numpy as jnp
        import numpy as np
        D_MODEL, N_HEADS = (256, 16)
        D_H = D_MODEL // N_HEADS
        D_HR = D_H // 2
        D_LATENT = 64
        THETA = 10000.0

        def rope(x, theta=THETA):
            S, d = (x.shape[-2], x.shape[-1])
            inv = theta ** (-jnp.arange(0, d, 2, dtype=jnp.float32) / d)
            ang = jnp.arange(S, dtype=jnp.float32)[:, None] * inv
            cos, sin = (jnp.cos(ang), jnp.sin(ang))
            x1, x2 = (x[..., 0::2], x[..., 1::2])
            r1 = x1 * cos - x2 * sin
            r2 = x1 * sin + x2 * cos
            return jnp.stack([r1, r2], axis=-1).reshape(x.shape)
        key = jax.random.key(seed)
        ks = jax.random.split(key, 9)
        s = lambda fan_in: 1.0 / np.sqrt(fan_in)
        return {'x': jax.random.normal(ks[0], (4, 512, D_MODEL), jnp.float32), 'W_DQ': jax.random.normal(ks[1], (D_MODEL, D_LATENT), jnp.float32) * s(D_MODEL), 'W_UQ': jax.random.normal(ks[2], (D_LATENT, N_HEADS * D_H), jnp.float32) * s(D_LATENT), 'W_QR': jax.random.normal(ks[3], (D_LATENT, N_HEADS * D_HR), jnp.float32) * s(D_LATENT), 'W_DKV': jax.random.normal(ks[4], (D_MODEL, D_LATENT), jnp.float32) * s(D_MODEL), 'W_UK': jax.random.normal(ks[5], (D_LATENT, N_HEADS * D_H), jnp.float32) * s(D_LATENT), 'W_UV': jax.random.normal(ks[6], (D_LATENT, N_HEADS * D_H), jnp.float32) * s(D_LATENT), 'W_KR': jax.random.normal(ks[7], (D_MODEL, D_HR), jnp.float32) * s(D_MODEL), 'W_O': jax.random.normal(ks[8], (N_HEADS * D_H, D_MODEL), jnp.float32) * s(N_HEADS * D_H)}
    _L1_attn_all = _L1_attn_setup()
    _L1_attn_in = {k: v for k, v in _L1_attn_all.items() if k in ('W_DQ', 'W_UQ', 'W_QR', 'W_DKV', 'W_UK', 'W_UV', 'W_KR', 'W_O')}
    del _L1_attn_all

    def _L1_xattn_setup():
        import jax, jax.numpy as jnp
        import numpy as np
        B, T, D = (2, 512, 256)
        H = 16
        HD = D // H
        ROPE_BASE = 10000.0

        def _apply_rope(x):
            t = x.shape[2]
            hd = x.shape[3]
            inv_freq = 1.0 / ROPE_BASE ** (jnp.arange(0, hd, 2, dtype=jnp.float32) / hd)
            pos = jnp.arange(t, dtype=jnp.float32)
            freqs = pos[:, None] * inv_freq[None, :]
            cos = jnp.cos(freqs)[None, None, :, :]
            sin = jnp.sin(freqs)[None, None, :, :]
            x1, x2 = (x[..., :hd // 2], x[..., hd // 2:])
            return jnp.concatenate([x1 * cos - x2 * sin, x1 * sin + x2 * cos], axis=-1)
        key = jax.random.key(seed)
        ks = jax.random.split(key, 8)
        s = 1.0 / np.sqrt(D)
        return {'query': jax.random.normal(ks[0], (B, T, D), dtype=jnp.float32), 'key': jax.random.normal(ks[1], (B, T, D), dtype=jnp.float32), 'value': jax.random.normal(ks[2], (B, T, D), dtype=jnp.float32), 'Wq': jax.random.normal(ks[3], (D, D), dtype=jnp.float32) * s, 'Wk': jax.random.normal(ks[4], (D, D), dtype=jnp.float32) * s, 'Wv': jax.random.normal(ks[5], (D, D), dtype=jnp.float32) * s, 'Wo': jax.random.normal(ks[6], (D, D), dtype=jnp.float32) * s, 'bo': jax.random.normal(ks[7], (D,), dtype=jnp.float32) * 0.01}
    _L1_xattn_all = _L1_xattn_setup()
    _L1_xattn_in = {k: v for k, v in _L1_xattn_all.items() if k in ('Wq', 'Wk', 'Wv', 'Wo', 'bo')}
    del _L1_xattn_all

    def _L1_ffn_setup():
        import jax, jax.numpy as jnp
        import numpy as np
        D = 256
        H = 16
        HD = D // H
        E = 32
        ES = 128
        K = 4
        B, S = (2, 256)
        ROPE_BASE = 10000.0

        def _layernorm(x, g, b):
            m = x.mean(-1, keepdims=True)
            v = ((x - m) ** 2).mean(-1, keepdims=True)
            return (x - m) * jax.lax.rsqrt(v + 1e-05) * g + b

        def _forward(src, wq, wk, wv, wp, wo, ln1_g, ln1_b, ln2_g, ln2_b, sel_w, keys, values):
            Bs, Ss, Ds = src.shape
            scale = 1.0 / jnp.sqrt(jnp.array(HD, dtype=src.dtype))
            x = _layernorm(src, ln1_g, ln1_b)
            q = (x @ wq).reshape(Bs, Ss, H, HD)
            k = (x @ wk).reshape(Bs, Ss, H, HD)
            v = (x @ wv).reshape(Bs, Ss, H, HD)
            pos = jnp.arange(Ss - 1, -Ss, -1, dtype=src.dtype)
            inv_freq = 1.0 / ROPE_BASE ** (jnp.arange(0, Ds, 2, dtype=src.dtype) / Ds)
            ang = pos[:, None] * inv_freq[None, :]
            pe = jnp.concatenate([jnp.sin(ang), jnp.cos(ang)], axis=-1)
            p = (pe @ wp).reshape(2 * Ss - 1, H, HD)
            ac = jnp.einsum('bihd,bjhd->bhij', q, k)
            bd_full = jnp.einsum('bihd,phd->bhip', q, p)
            rel = jnp.arange(Ss)[:, None] - jnp.arange(Ss)[None, :] + (Ss - 1)
            bd = bd_full[:, :, jnp.arange(Ss)[:, None], rel]
            att = jax.nn.softmax((ac + bd) * scale, axis=-1)
            attn_out = jnp.einsum('bhij,bjhd->bihd', att, v).reshape(Bs, Ss, Ds) @ wo
            src = src + attn_out
            x2 = _layernorm(src, ln2_g, ln2_b)
            sel = jax.nn.sigmoid(x2 @ sel_w)
            scores, idx = jax.lax.top_k(sel, K)
            gate = (jax.nn.one_hot(idx, E, dtype=sel.dtype) * scores[..., None]).sum(-2)
            h = jax.nn.relu(jnp.einsum('bsd,edh->bseh', x2, keys))
            moe_out = jnp.einsum('bseh,ehd,bse->bsd', h, values, gate)
            return src + moe_out
        key = jax.random.key(seed)
        ks = jax.random.split(key, 10)
        std_scale = np.sqrt(2.0 / 18)
        w_std = std_scale / np.sqrt(D)
        return {'src': jax.random.normal(ks[0], (B, S, D), jnp.float32), 'wq': jax.random.normal(ks[1], (D, H * HD), jnp.float32) * w_std, 'wk': jax.random.normal(ks[2], (D, H * HD), jnp.float32) * w_std, 'wv': jax.random.normal(ks[3], (D, H * HD), jnp.float32) * w_std, 'wp': jax.random.normal(ks[4], (D, H * HD), jnp.float32) * w_std, 'wo': jax.random.normal(ks[5], (H * HD, D), jnp.float32) * w_std, 'ln1_g': jnp.ones((D,), jnp.float32), 'ln1_b': jnp.zeros((D,), jnp.float32), 'ln2_g': jnp.ones((D,), jnp.float32), 'ln2_b': jnp.zeros((D,), jnp.float32), 'sel_w': jax.random.normal(ks[6], (D, E), jnp.float32) / np.sqrt(D), 'keys': jax.random.normal(ks[7], (E, D, ES), jnp.float32) * w_std, 'values': jax.random.normal(ks[8], (E, ES, D), jnp.float32) * (std_scale / np.sqrt(ES))}
    _L1_ffn_all = _L1_ffn_setup()
    _L1_ffn_in = {k: v for k, v in _L1_ffn_all.items() if k in ('wq', 'wk', 'wv', 'wp', 'wo', 'ln1_g', 'ln1_b', 'ln2_g', 'ln2_b', 'sel_w', 'keys', 'values')}
    del _L1_ffn_all
    return {'x': x, 'ctx_1024': ctx_1024, 'mask_BxS2_bk1': mask_BxS2_bk1, 'L0_attn_q_a': _L0_attn_in['q_a'], 'L0_attn_q_b': _L0_attn_in['q_b'], 'L0_attn_k_a': _L0_attn_in['k_a'], 'L0_attn_k_b': _L0_attn_in['k_b'], 'L0_attn_v_w': _L0_attn_in['v_w'], 'L0_attn_v_b': _L0_attn_in['v_b'], 'L0_attn_o_w': _L0_attn_in['o_w'], 'L0_attn_o_b': _L0_attn_in['o_b'], 'L0_xattn_Wq': _L0_xattn_in['Wq'], 'L0_xattn_Wkv': _L0_xattn_in['Wkv'], 'L0_xattn_Wo': _L0_xattn_in['Wo'], 'L0_xattn_ln_x_g': _L0_xattn_in['ln_x_g'], 'L0_xattn_ln_x_b': _L0_xattn_in['ln_x_b'], 'L0_xattn_ln_l_g': _L0_xattn_in['ln_l_g'], 'L0_xattn_ln_l_b': _L0_xattn_in['ln_l_b'], 'L0_xattn_ln_o_g': _L0_xattn_in['ln_o_g'], 'L0_xattn_ln_o_b': _L0_xattn_in['ln_o_b'], 'L0_ffn_router_w': _L0_ffn_in['router_w'], 'L0_ffn_router_b': _L0_ffn_in['router_b'], 'L0_ffn_W1': _L0_ffn_in['W1'], 'L0_ffn_b1': _L0_ffn_in['b1'], 'L0_ffn_W2': _L0_ffn_in['W2'], 'L0_ffn_b2': _L0_ffn_in['b2'], 'L1_attn_W_DQ': _L1_attn_in['W_DQ'], 'L1_attn_W_UQ': _L1_attn_in['W_UQ'], 'L1_attn_W_QR': _L1_attn_in['W_QR'], 'L1_attn_W_DKV': _L1_attn_in['W_DKV'], 'L1_attn_W_UK': _L1_attn_in['W_UK'], 'L1_attn_W_UV': _L1_attn_in['W_UV'], 'L1_attn_W_KR': _L1_attn_in['W_KR'], 'L1_attn_W_O': _L1_attn_in['W_O'], 'L1_xattn_Wq': _L1_xattn_in['Wq'], 'L1_xattn_Wk': _L1_xattn_in['Wk'], 'L1_xattn_Wv': _L1_xattn_in['Wv'], 'L1_xattn_Wo': _L1_xattn_in['Wo'], 'L1_xattn_bo': _L1_xattn_in['bo'], 'L1_ffn_wq': _L1_ffn_in['wq'], 'L1_ffn_wk': _L1_ffn_in['wk'], 'L1_ffn_wv': _L1_ffn_in['wv'], 'L1_ffn_wp': _L1_ffn_in['wp'], 'L1_ffn_wo': _L1_ffn_in['wo'], 'L1_ffn_ln1_g': _L1_ffn_in['ln1_g'], 'L1_ffn_ln1_b': _L1_ffn_in['ln1_b'], 'L1_ffn_ln2_g': _L1_ffn_in['ln2_g'], 'L1_ffn_ln2_b': _L1_ffn_in['ln2_b'], 'L1_ffn_sel_w': _L1_ffn_in['sel_w'], 'L1_ffn_keys': _L1_ffn_in['keys'], 'L1_ffn_values': _L1_ffn_in['values']}

def reference(x, ctx_1024, mask_BxS2_bk1, L0_attn_q_a, L0_attn_q_b, L0_attn_k_a, L0_attn_k_b, L0_attn_v_w, L0_attn_v_b, L0_attn_o_w, L0_attn_o_b, L0_xattn_Wq, L0_xattn_Wkv, L0_xattn_Wo, L0_xattn_ln_x_g, L0_xattn_ln_x_b, L0_xattn_ln_l_g, L0_xattn_ln_l_b, L0_xattn_ln_o_g, L0_xattn_ln_o_b, L0_ffn_router_w, L0_ffn_router_b, L0_ffn_W1, L0_ffn_b1, L0_ffn_W2, L0_ffn_b2, L1_attn_W_DQ, L1_attn_W_UQ, L1_attn_W_QR, L1_attn_W_DKV, L1_attn_W_UK, L1_attn_W_UV, L1_attn_W_KR, L1_attn_W_O, L1_xattn_Wq, L1_xattn_Wk, L1_xattn_Wv, L1_xattn_Wo, L1_xattn_bo, L1_ffn_wq, L1_ffn_wk, L1_ffn_wv, L1_ffn_wp, L1_ffn_wo, L1_ffn_ln1_g, L1_ffn_ln1_b, L1_ffn_ln2_g, L1_ffn_ln2_b, L1_ffn_sel_w, L1_ffn_keys, L1_ffn_values):
    import jax
    import jax.numpy as jnp

    def _L0_attn_ref(hidden_states, q_a, q_b, k_a, k_b, v_w, v_b, o_w, o_b):
        import jax, jax.numpy as jnp
        import numpy as np
        B, T, D, H, R = (1, 1024, 256, 16, 64)
        HD = D // H
        STD = 0.02

        def _low_rank_proj(x, a, b):
            mid = jnp.einsum('btd,hdr->bhtr', x, a)
            return jnp.einsum('bhtr,hrd->bhtd', mid, b)
        Bc, Tc, Dc = hidden_states.shape
        q = _low_rank_proj(hidden_states, q_a, q_b)
        k = _low_rank_proj(hidden_states, k_a, k_b)
        v = hidden_states @ v_w.T + v_b
        v = v.reshape(Bc, Tc, H, HD).transpose(0, 2, 1, 3)
        scale = 1.0 / np.sqrt(HD).astype(np.float32)
        att = jnp.einsum('bhtd,bhsd->bhts', q, k) * scale
        causal = jnp.tril(jnp.ones((Tc, Tc), dtype=bool))
        att = jnp.where(causal[None, None], att, jnp.finfo(att.dtype).min)
        att = jax.nn.softmax(att, axis=-1)
        y = jnp.einsum('bhts,bhsd->bhtd', att, v)
        y = y.transpose(0, 2, 1, 3).reshape(Bc, Tc, Dc)
        return y @ o_w.T + o_b

    def _L0_xattn_ref(x, latents, mask, Wq, Wkv, Wo, ln_x_g, ln_x_b, ln_l_g, ln_l_b, ln_o_g, ln_o_b):
        import jax, jax.numpy as jnp
        import numpy as np
        DIM = 256
        DIM_HEAD = 64
        HEADS = 8
        INNER = DIM_HEAD * HEADS
        EPS = 1e-05

        def layernorm(x, g, b):
            mu = jnp.mean(x, axis=-1, keepdims=True)
            var = jnp.var(x, axis=-1, keepdims=True)
            return (x - mu) * jax.lax.rsqrt(var + EPS) * g + b
        scale = DIM_HEAD ** (-0.5)
        b, m = (latents.shape[0], latents.shape[1])
        xn = layernorm(x, ln_x_g, ln_x_b)
        ln = layernorm(latents, ln_l_g, ln_l_b)
        q = ln @ Wq
        kv_in = jnp.concatenate([xn, ln], axis=1)
        kv = kv_in @ Wkv
        k, v = jnp.split(kv, 2, axis=-1)
        q = q.reshape(b, m, HEADS, DIM_HEAD).transpose(0, 2, 1, 3)
        k = k.reshape(b, k.shape[1], HEADS, DIM_HEAD).transpose(0, 2, 1, 3)
        v = v.reshape(b, v.shape[1], HEADS, DIM_HEAD).transpose(0, 2, 1, 3)
        sim = jnp.einsum('bhid,bhjd->bhij', q * scale, k) * scale
        full_mask = jnp.concatenate([mask, jnp.ones((b, m), dtype=bool)], axis=1)
        max_neg = -jnp.finfo(sim.dtype).max
        sim = jnp.where(full_mask[:, None, None, :], sim, max_neg)
        attn = jax.nn.softmax(sim.astype(jnp.float32), axis=-1).astype(sim.dtype)
        out = jnp.einsum('bhij,bhjd->bhid', attn, v)
        out = out.transpose(0, 2, 1, 3).reshape(b, m, INNER)
        out = out @ Wo
        return layernorm(out, ln_o_g, ln_o_b)

    def _L0_ffn_ref(x, router_w, router_b, W1, b1, W2, b2):
        import jax, jax.numpy as jnp
        import numpy as np
        D_MODEL = 256
        D_FF = 1024
        N_EXPERTS = 8
        TOP_K = 2
        D_FF_PER = D_FF // N_EXPERTS
        B, T = (4, 512)
        router_logits = x @ router_w + router_b
        routing_weights = jax.nn.softmax(router_logits, axis=-1)
        top_k_weights, top_k_indices = jax.lax.top_k(routing_weights, TOP_K)
        top_k_weights = top_k_weights / jnp.sum(top_k_weights, axis=-1, keepdims=True)
        routing_mask = jnp.zeros_like(routing_weights)
        routing_mask = jnp.take_along_axis(routing_mask, top_k_indices, axis=-1)
        b_idx = jnp.arange(x.shape[0])[:, None, None]
        t_idx = jnp.arange(x.shape[1])[None, :, None]
        routing_mask = jnp.zeros_like(routing_weights).at[b_idx, t_idx, top_k_indices].set(top_k_weights)
        h1 = jnp.einsum('btd,nde->btne', x, W1) + b1
        h1 = jax.nn.gelu(h1, approximate=False)
        out_per_expert = jnp.einsum('btne,nef->btnf', h1, W2) + b2
        output = jnp.sum(out_per_expert * routing_mask[..., None], axis=-2)
        return output

    def _L1_attn_ref(x, W_DQ, W_UQ, W_QR, W_DKV, W_UK, W_UV, W_KR, W_O):
        import jax, jax.numpy as jnp
        import numpy as np
        D_MODEL, N_HEADS = (256, 16)
        D_H = D_MODEL // N_HEADS
        D_HR = D_H // 2
        D_LATENT = 64
        THETA = 10000.0

        def rope(x, theta=THETA):
            S, d = (x.shape[-2], x.shape[-1])
            inv = theta ** (-jnp.arange(0, d, 2, dtype=jnp.float32) / d)
            ang = jnp.arange(S, dtype=jnp.float32)[:, None] * inv
            cos, sin = (jnp.cos(ang), jnp.sin(ang))
            x1, x2 = (x[..., 0::2], x[..., 1::2])
            r1 = x1 * cos - x2 * sin
            r2 = x1 * sin + x2 * cos
            return jnp.stack([r1, r2], axis=-1).reshape(x.shape)
        B, S, _ = x.shape
        d_qk = D_H + D_HR
        c_q = x @ W_DQ
        Qc = (c_q @ W_UQ).reshape(B, S, N_HEADS, D_H).transpose(0, 2, 1, 3)
        Qr = (c_q @ W_QR).reshape(B, S, N_HEADS, D_HR).transpose(0, 2, 1, 3)
        Qr = rope(Qr)
        c_kv = x @ W_DKV
        Kc = (c_kv @ W_UK).reshape(B, S, N_HEADS, D_H).transpose(0, 2, 1, 3)
        Kr = rope((x @ W_KR)[:, None, :, :])
        Kr = jnp.broadcast_to(Kr, (B, N_HEADS, S, D_HR))
        V = (c_kv @ W_UV).reshape(B, S, N_HEADS, D_H).transpose(0, 2, 1, 3)
        Q = jnp.concatenate([Qc, Qr], axis=-1)
        K = jnp.concatenate([Kc, Kr], axis=-1)
        scores = jnp.einsum('bhqd,bhkd->bhqk', Q, K)
        scores = jnp.clip(scores, -80.0, 80.0)
        causal = jnp.tril(jnp.ones((S, S), dtype=bool))
        scores = jnp.where(causal, scores, -jnp.inf)
        weights = jax.nn.softmax(scores / jnp.sqrt(jnp.float32(d_qk)), axis=-1)
        attn = jnp.einsum('bhqk,bhkd->bhqd', weights, V)
        attn = attn.transpose(0, 2, 1, 3).reshape(B, S, N_HEADS * D_H)
        return attn @ W_O

    def _L1_xattn_ref(query, key, value, Wq, Wk, Wv, Wo, bo):
        import jax, jax.numpy as jnp
        import numpy as np
        B, T, D = (2, 512, 256)
        H = 16
        HD = D // H
        ROPE_BASE = 10000.0

        def _apply_rope(x):
            t = x.shape[2]
            hd = x.shape[3]
            inv_freq = 1.0 / ROPE_BASE ** (jnp.arange(0, hd, 2, dtype=jnp.float32) / hd)
            pos = jnp.arange(t, dtype=jnp.float32)
            freqs = pos[:, None] * inv_freq[None, :]
            cos = jnp.cos(freqs)[None, None, :, :]
            sin = jnp.sin(freqs)[None, None, :, :]
            x1, x2 = (x[..., :hd // 2], x[..., hd // 2:])
            return jnp.concatenate([x1 * cos - x2 * sin, x1 * sin + x2 * cos], axis=-1)
        b, t, d = query.shape

        def split_heads(x):
            return x.reshape(b, -1, H, HD).transpose(0, 2, 1, 3)
        q = split_heads(query @ Wq.T)
        k = split_heads(key @ Wk.T)
        v = split_heads(value @ Wv.T)
        q = _apply_rope(q)
        k = _apply_rope(k)
        scale = 1.0 / jnp.sqrt(jnp.asarray(HD, dtype=q.dtype))
        logits = jnp.einsum('bhqd,bhkd->bhqk', q, k) * scale
        attn = jax.nn.softmax(logits, axis=-1)
        out = jnp.einsum('bhqk,bhkd->bhqd', attn, v)
        out = out.transpose(0, 2, 1, 3).reshape(b, t, d)
        return out @ Wo.T + bo

    def _L1_ffn_ref(src, wq, wk, wv, wp, wo, ln1_g, ln1_b, ln2_g, ln2_b, sel_w, keys, values):
        import jax, jax.numpy as jnp
        import numpy as np
        D = 256
        H = 16
        HD = D // H
        E = 32
        ES = 128
        K = 4
        B, S = (2, 256)
        ROPE_BASE = 10000.0

        def _layernorm(x, g, b):
            m = x.mean(-1, keepdims=True)
            v = ((x - m) ** 2).mean(-1, keepdims=True)
            return (x - m) * jax.lax.rsqrt(v + 1e-05) * g + b

        def _forward(src, wq, wk, wv, wp, wo, ln1_g, ln1_b, ln2_g, ln2_b, sel_w, keys, values):
            Bs, Ss, Ds = src.shape
            scale = 1.0 / jnp.sqrt(jnp.array(HD, dtype=src.dtype))
            x = _layernorm(src, ln1_g, ln1_b)
            q = (x @ wq).reshape(Bs, Ss, H, HD)
            k = (x @ wk).reshape(Bs, Ss, H, HD)
            v = (x @ wv).reshape(Bs, Ss, H, HD)
            pos = jnp.arange(Ss - 1, -Ss, -1, dtype=src.dtype)
            inv_freq = 1.0 / ROPE_BASE ** (jnp.arange(0, Ds, 2, dtype=src.dtype) / Ds)
            ang = pos[:, None] * inv_freq[None, :]
            pe = jnp.concatenate([jnp.sin(ang), jnp.cos(ang)], axis=-1)
            p = (pe @ wp).reshape(2 * Ss - 1, H, HD)
            ac = jnp.einsum('bihd,bjhd->bhij', q, k)
            bd_full = jnp.einsum('bihd,phd->bhip', q, p)
            rel = jnp.arange(Ss)[:, None] - jnp.arange(Ss)[None, :] + (Ss - 1)
            bd = bd_full[:, :, jnp.arange(Ss)[:, None], rel]
            att = jax.nn.softmax((ac + bd) * scale, axis=-1)
            attn_out = jnp.einsum('bhij,bjhd->bihd', att, v).reshape(Bs, Ss, Ds) @ wo
            src = src + attn_out
            x2 = _layernorm(src, ln2_g, ln2_b)
            sel = jax.nn.sigmoid(x2 @ sel_w)
            scores, idx = jax.lax.top_k(sel, K)
            gate = (jax.nn.one_hot(idx, E, dtype=sel.dtype) * scores[..., None]).sum(-2)
            h = jax.nn.relu(jnp.einsum('bsd,edh->bseh', x2, keys))
            moe_out = jnp.einsum('bseh,ehd,bse->bsd', h, values, gate)
            return src + moe_out
        return _forward(src, wq, wk, wv, wp, wo, ln1_g, ln1_b, ln2_g, ln2_b, sel_w, keys, values)
    x = x + _L0_attn_ref(_layernorm(x, axis=-1), L0_attn_q_a, L0_attn_q_b, L0_attn_k_a, L0_attn_k_b, L0_attn_v_w, L0_attn_v_b, L0_attn_o_w, L0_attn_o_b)
    x = x + _L0_xattn_ref(ctx_1024, _layernorm(x, axis=-1), mask_BxS2_bk1, L0_xattn_Wq, L0_xattn_Wkv, L0_xattn_Wo, L0_xattn_ln_x_g, L0_xattn_ln_x_b, L0_xattn_ln_l_g, L0_xattn_ln_l_b, L0_xattn_ln_o_g, L0_xattn_ln_o_b)
    x = x + _L0_ffn_ref(_layernorm(x, axis=-1), L0_ffn_router_w, L0_ffn_router_b, L0_ffn_W1, L0_ffn_b1, L0_ffn_W2, L0_ffn_b2)
    x = x + _L1_attn_ref(_layernorm(x, axis=-1), L1_attn_W_DQ, L1_attn_W_UQ, L1_attn_W_QR, L1_attn_W_DKV, L1_attn_W_UK, L1_attn_W_UV, L1_attn_W_KR, L1_attn_W_O)
    x = x + _L1_xattn_ref(_layernorm(x, axis=-1), ctx_1024, ctx_1024, L1_xattn_Wq, L1_xattn_Wk, L1_xattn_Wv, L1_xattn_Wo, L1_xattn_bo)
    x = x + _L1_ffn_ref(_layernorm(x, axis=-1), L1_ffn_wq, L1_ffn_wk, L1_ffn_wv, L1_ffn_wp, L1_ffn_wo, L1_ffn_ln1_g, L1_ffn_ln1_b, L1_ffn_ln2_g, L1_ffn_ln2_b, L1_ffn_sel_w, L1_ffn_keys, L1_ffn_values)
    return x

_drawn_inputs = setup_inputs


def setup_inputs(seed=0):
    import zlib

    import numpy as np

    out = dict(_drawn_inputs(seed))
    spreads = {'L0_attn_v_b': (0.0, 0.28),
     'L0_attn_o_b': (0.0, 0.1),
     'L0_xattn_ln_x_g': (1.0, 0.2),
     'L0_xattn_ln_x_b': (0.0, 0.1),
     'L0_xattn_ln_l_g': (1.0, 0.6),
     'L0_xattn_ln_l_b': (0.0, 0.1),
     'L0_xattn_ln_o_g': (1.0, 0.2),
     'L0_xattn_ln_o_b': (0.0, 0.1),
     'L1_ffn_ln1_g': (1.0, 0.6),
     'L1_ffn_ln1_b': (0.0, 0.8),
     'L1_ffn_ln2_g': (1.0, 0.6),
     'L1_ffn_ln2_b': (0.0, 0.368)}
    factors = {'L0_attn_q_a': 8.0,
     'L0_attn_q_b': 8.0,
     'L0_attn_k_a': 8.0,
     'L0_attn_k_b': 8.0,
     'L0_ffn_router_b': 3.072,
     'L0_ffn_b1': 8.0,
     'L1_xattn_bo': 8.0,
     'L1_ffn_wq': 8.0,
     'L1_ffn_wk': 8.0,
     'L1_ffn_wp': 8.0}
    for name, (base, spread) in spreads.items():
        noise = np.random.default_rng([zlib.crc32(name.encode()), seed]).standard_normal(out[name].shape)
        drawn = base * np.exp(spread * noise) if base else spread * noise
        out[name] = jnp.asarray(drawn.astype(out[name].dtype))
    for name, factor in factors.items():
        out[name] = (out[name] * factor).astype(out[name].dtype)
    return out
```

```python
from contextlib import ExitStack

import numpy as np

import concourse.bass as bass
from concourse import mybir

F32 = mybir.dt.float32
U8 = mybir.dt.uint8
ACT = mybir.ActivationFunctionType
ALU = mybir.AluOpType
AX_X = mybir.AxisListType.X

P = 128
T = 112
D = 256
DC = D // P
H = 16
HD = D // H
SLOT = 32
HS = P // SLOT
HG = H // HS
S2 = 375
CC = 3
CK = S2 // CC
XH, XD = 8, 64
XK = 488
XC = 4
XCK = XK // XC
RP = 2 * T - 1
RPW = RP + 1
EPS = 1e-5
BIG = 1.5e38

CONST = {}
_at = 0
for _name, _width in (("ident", P), ("mask8", 8), ("mask4", 4), ("keep0", T), ("keep1", T), ("pick", P),
                      ("turnX", P), ("cosX", S2), ("sinX", S2), ("turnA", P), ("cosA", T), ("sinA", T),
                      ("restart", 128), ("pe", DC * RPW)):
    CONST[_name] = (_at, _width)
    _at += _width
CONST_W = _at


def constants():
    c = np.zeros((P, CONST_W), np.float32)

    def put(name, a):
        at, width = CONST[name]
        c[:a.shape[0], at:at + width] = a

    put("ident", np.eye(P, dtype=np.float32))
    put("mask8", np.kron(np.eye(8), np.ones((16, 1))))
    put("mask4", np.kron(np.eye(4), np.ones((32, 1))))
    causal = np.tril(np.ones((T, T), bool))
    put("keep0", np.where(causal, BIG, -BIG))
    put("keep1", np.where(causal, 80.0, -1e30))
    pick = np.zeros((P, P))
    for a in range(HS):
        pick[SLOT * a + HD, SLOT * a:SLOT * (a + 1)] = 1.0
    put("pick", pick)
    inv = (1.0 / np.float32(10000.0) ** (np.arange(0, HD, 2, dtype=np.float32) / np.float32(HD))).astype(np.float32)
    ang = (np.arange(S2, dtype=np.float32)[:, None] * inv[None, :]).astype(np.float32)
    put("cosX", np.tile(np.concatenate([np.cos(ang), np.cos(ang)], 1).T, (P // HD, 1)))
    put("sinX", np.tile(np.concatenate([np.sin(ang), np.sin(ang)], 1).T, (P // HD, 1)))
    turn = np.zeros((P, P))
    for h in range(P // HD):
        for d in range(HD // 2):
            turn[HD * h + d + 8, HD * h + d] = -1.0
            turn[HD * h + d, HD * h + d + 8] = 1.0
    put("turnX", turn)
    inv = (np.float32(10000.0) ** (-np.arange(0, 8, 2, dtype=np.float32) / np.float32(8))).astype(np.float32)
    ang = (np.arange(T, dtype=np.float32)[:, None] * inv[None, :]).astype(np.float32)
    cos, sin, turn = np.ones((P, T)), np.zeros((P, T)), np.zeros((P, P))
    for a in range(HS):
        for r in range(8):
            cos[SLOT * a + 16 + r] = np.cos(ang[:, r // 2])
            sin[SLOT * a + 16 + r] = np.sin(ang[:, r // 2])
        for r in range(0, 8, 2):
            turn[SLOT * a + 17 + r, SLOT * a + 16 + r] = -1.0
            turn[SLOT * a + 16 + r, SLOT * a + 17 + r] = 1.0
    put("cosA", cos)
    put("sinA", sin)
    put("turnA", turn)
    restart = np.ones((P, 128))
    put("restart", restart)
    pos = np.arange(-(T - 1), T, dtype=np.float32)
    inv = (1.0 / np.float32(10000.0) ** (np.arange(0, D, 2, dtype=np.float32) / np.float32(D))).astype(np.float32)
    ang = (pos[None, :] * inv[:, None]).astype(np.float32)
    pe = np.zeros((P, DC, RPW))
    pe[:, 0, :RP] = np.sin(ang)
    pe[:, 1, :RP] = np.cos(ang)
    put("pe", pe.reshape(P, -1))
    return c


def bc(ap, axis, n):
    v = ap.unsqueeze(axis)
    shape = list(v.shape)
    shape[axis] = n
    return v.to_broadcast(shape)


class Chain:

    def __init__(self, eng, sem, per=0, first=1, once=None):
        self.eng, self.sem, self.per, self.first = eng, sem, per, first
        self.base = self.n = self.k = 0
        self.once = once

    def start(self, b):
        if isinstance(b, int):
            self.base = self.n
        else:
            if self.k != self.per or self.n == 0:
                pass
            self.base = self.loop + (b - self.first) * self.per
        self.k = 0

    def enter(self):
        self.loop = self.n

    def leave(self, bodies):
        self.n = self.loop + bodies * self.per

    def inc(self, ins):
        ins.then_inc(self.sem, 1)
        self.k += 1
        self.n += 1
        return self.base + self.k

    def link(self, ins):
        self.eng.wait_ge(self.sem, self.inc(ins))

    def link_apart(self, ins):
        ins.then_inc(self.once, 1)
        self.eng.wait_ge(self.once, 1)
        self.eng.sem_clear(self.once)


def over(eng, n, body, chain=None):
    if chain:
        chain.start(0)
    body(0, 0)
    if chain:
        chain.enter()
    with eng.Fori(0, (n - 2) // 2) as it:
        for k in (0, 1):
            b = it * 2 + (1 + k)
            if chain:
                chain.start(b)
            body(b, (1 + k) % 2)
            if chain:
                assert chain.k == chain.per, (chain.k, chain.per)
    if chain:
        chain.leave(n - 2)
        chain.start(n - 1)
    body(n - 1, (n - 1) % 2)


def at_least(eng, sem, n):
    if not isinstance(n, int) or n > 0:
        eng.wait_ge(sem, n)


class Ring:

    def __init__(self, banks, full, free, la, lo):
        assert (la + lo) % 2 == 0
        self.banks, self.full, self.free, self.la, self.lo = banks, full, free, la, lo

    def count(self, c, b):
        return c // 2 + b * ((self.la + self.lo) // 2)

    def claim(self, pe, c, b):
        at_least(pe, self.free[c % 2], self.count(c, b))
        return self.banks[c % 2]

    def filled(self, ins, c):
        ins.then_inc(self.full[c % 2], 1)

    def take(self, eng, c, b):
        eng.wait_ge(self.full[c % 2], self.count(c, b) + 1)
        return self.banks[c % 2]

    def freed(self, ins, c):
        ins.then_inc(self.free[c % 2], 1)

    def emptied(self, eng, c, b):
        eng.wait_ge(self.free[c % 2], self.count(c, b) + 1)


def decoder(nc, t, stop=99, start=0):
    NB = t["x"].shape[0]
    whole = ExitStack()
    with whole:
        def allocators(stack, tag):
            def sb(name, shape, dt=F32):
                return stack.enter_context(nc.sbuf_tensor(f"{tag}_{name}", shape, dt))

            def psum(name, shape=(P, 512)):
                return stack.enter_context(nc.psum_tensor(f"{tag}_{name}", list(shape), F32))

            sems = []

            def release():
                if sems:
                    nc.clear_and_free_semaphores(sems)
                    nc.all_engine_barrier()

            stack.callback(release)

            def sem(name):
                sems.append(nc.alloc_semaphore(f"{tag}_{name}"))
                return sems[-1]
            return sb, psum, sem

        sb, _, _ = allocators(whole, "g")
        X = sb("residual", [P, NB, D])
        C = sb("constants", [P, CONST_W])
        half = sb("minus_half", [P, 4])

        def const(name, parts=P):
            at, width = CONST[name]
            return C[0:parts, at:at + width]

        G = dict(NB=NB, X=X, const=const, half=half, alloc=allocators, t=t)

        with ExitStack() as layer:
            W = load_layer0(nc, G, layer)
            if stop > 0 and start < 1:
                run_attention(nc, G, CausalAttention, W)
            if stop > 1 and start < 2:
                run_attention(nc, G, LatentAttention, W)
        if stop > 2 and start < 3:
            with ExitStack() as layer:
                experts(nc, G, load_experts(nc, G, layer, 0))
        if stop > 3:
            with ExitStack() as layer:
                W = load_layer1(nc, G, layer)
                if start < 4:
                    run_attention(nc, G, RotaryAttention, W)
                if stop > 4 and start < 5:
                    run_attention(nc, G, ContextAttention, W)
                if stop > 5:
                    G["S2"] = allocators(layer, "l1")[0]("stream2", [P, NB, D])
                    run_attention(nc, G, RelativeAttention, W)
                if stop > 6:
                    with ExitStack() as last:
                        experts(nc, G, load_experts(nc, G, last, 1))
        store(nc, G)


def store(nc, G):
    with ExitStack() as stack:
        sem = G["alloc"](stack, "st")[2]
        stored = sem("stored")
        block = stack.enter_context(nc.Block())

        @block.sync
        def _(sp):
            sp.dma_start(G["t"]["out"].rearrange("b t d -> t b d"), G["X"][0:T, :, :]).then_inc(stored, 16)
            sp.wait_ge(stored, 16)


def rows_in_slots(w):
    return w.rearrange("(g a d) n -> a d g n", g=HG, a=HS)


def load_layer0(nc, G, stack):
    t, NB = G["t"], G["NB"]
    sb, _, _ = G["alloc"](stack, "w0")
    W = dict(wq=sb("wq", [P, DC, D]), wk=sb("wk", [P, DC, D]), wv=sb("wv", [P, DC, D]),
             wo=sb("wo", [P, HG, D]), vb=sb("vb", [P, D]),
             xq=sb("xq", [P, DC, 512]), xkv=sb("xkv", [P, DC, 1024]), xo=sb("xo", [P, 4, D]),
             lnx=sb("lnx", [P, 2, DC]), lnl=sb("lnl", [P, 2, DC]), lno=sb("lno", [P, 2, D]))
    with ExitStack() as own:
        sbt, psum, sem = G["alloc"](own, "p0")
        low = {n: (sbt(f"{n}a", [64, H, D]), sbt(f"{n}b", [64, H, HD])) for n in ("q", "k")}
        bank = [psum(f"bank{i}") for i in range(4)]
        zeroed, loaded, folded, copied = sem("zeroed"), sem("loaded"), sem("folded"), sem("copied")
        small = sem("small")
        block = own.enter_context(nc.Block())

        @block.sync
        def _(sp):
            for n in ("q", "k"):
                sp.dma_start(low[n][0][:], t[f"{n}_aT"].rearrange("h r d -> r h d")).then_inc(loaded, 16)
                sp.dma_start(low[n][1][:], t[f"L0_attn_{n}_b"].rearrange("h r d -> r h d")).then_inc(loaded, 16)
            q = NB // 4
            for i in range(4):
                sp.dma_start(G["X"][0:T, i * q:(i + 1) * q, :],
                             t["x"].rearrange("b t d -> t b d")[:, i * q:(i + 1) * q, :]).then_inc(small, 16)
            sp.wait_ge(small, 64)

        @block.scalar
        def _(act):
            n = 0
            for dst, src in ((G["const"]("ident", P), None),):
                at = CONST["ident"][0]
                act.dma_start(whole_constants(G), t["constants"]).then_inc(copied, 16)
                n += 16
            loads = [
                (W["wv"][:], t["v_wT"].rearrange("(c p) n -> p c n", p=P)),
                (W["vb"][:], t["L0_attn_v_b"].partition_broadcast(P)),
                (W["xq"][:], t["L0_xattn_Wq"].rearrange("(c p) n -> p c n", p=P)),
                (W["xkv"][:], t["L0_xattn_Wkv"].rearrange("(c p) n -> p c n", p=P)),
                (W["xo"][:], t["L0_xattn_Wo"].rearrange("(c p) n -> p c n", p=P)),
            ]
            for key, name in (("lnx", "ln_x"), ("lnl", "ln_l")):
                for i, gb in enumerate("gb"):
                    for c in range(DC):
                        loads.append((W[key][:, i, c:c + 1],
                                      t[f"L0_xattn_{name}_{gb}"].rearrange("(c p a) -> c p a", p=P, a=1)[c]))
            for i, gb in enumerate("gb"):
                loads.append((W["lno"][:, i, :], t[f"L0_xattn_ln_o_{gb}"].partition_broadcast(P)))
            for dst, src in loads:
                act.dma_start(dst, src).then_inc(copied, 16)
                n += 16
            act.wait_ge(zeroed, 1)
            for a in range(HS):
                act.dma_start(W["wo"][SLOT * a:SLOT * a + HD, :, :], rows_in_slots(t["o_wT"])[a]).then_inc(copied, 16)
                n += 16
            act.dma_start(W["wo"][HD:HD + 1, 0, :], t["L0_attn_o_b"].rearrange("(a n) -> a n", a=1)).then_inc(copied, 16)
            n += 16
            act.wait_ge(copied, n)

        @block.gpsimd
        def _(pool):
            pool.memset(W["wo"][:], 0.0).then_inc(zeroed, 1)
            pool.memset(G["half"][:], -0.5).then_inc(zeroed, 1)
            pool.wait_ge(zeroed, 2)

        @block.tensor
        def _(pe):
            pe.wait_ge(loaded, 64)
            for i, n in enumerate("qk"):
                for c in range(DC):
                    for h in range(H):
                        last = nc.tensor.matmul(bank[2 * i + c][:, h * HD:(h + 1) * HD],
                                                low[n][0][:, h, c * P:(c + 1) * P], low[n][1][:, h, :],
                                                start=True, stop=True)
                    last.then_inc(folded, 1)

        @block.vector
        def _(dve):
            for i, n in enumerate("qk"):
                for c in range(DC):
                    dve.wait_ge(folded, 2 * i + c + 1)
                    nc.vector.tensor_copy(W["w" + n][:, c, :], bank[2 * i + c][:, 0:D])
    return W


def whole_constants(G):
    first = CONST["ident"][0]
    ap = G["const"]("ident")
    return bass.AP(ap.tensor, ap.offset, [ap.ap[0], (1, CONST_W)])


class Plan:

    def __init__(self, units, finish, prepare, normalise):
        self.units = units
        self.finish, self.prepare, self.normalise = finish, prepare, normalise
        self.f_names = [n for s in sorted(finish) for n in finish[s]]
        self.p_names = [n for s in sorted(prepare) for n in prepare[s]]
        self.la, self.lo = len(self.p_names), len(self.f_names)

    def first(self):
        return [(n, j) for j, n in enumerate(self.p_names)]

    def finish_at(self, s):
        return [(n, self.la - self.lo + self.f_names.index(n)) for n in self.finish.get(s, ())]

    def prepare_at(self, s):
        return [(n, self.la + self.p_names.index(n)) for n in self.prepare.get(s, ())]

    def last(self):
        return [(n, j - self.lo) for j, n in enumerate(self.f_names)]

    def spot_of(self, name, b):
        j = self.p_names.index(name)
        if isinstance(b, int) and b == 0:
            return j, 0
        return self.la + j, b - 1


def attention(nc, G, stack, cfg):
    NB, X, const = G["NB"], G["X"], G["const"]
    plan = cfg.plan
    U = plan.units
    sb, psum, sem = G["alloc"](stack, cfg.tag)
    scores = [psum("scores0"), psum("scores1")]
    flipped = [psum("flipped0"), psum("flipped1")]
    heads_out = psum("heads_out")
    denominators = psum("denominators")
    ring_banks = [psum("ring0"), psum("ring1")]
    ring = Ring(ring_banks, [sem("ring_full0"), sem("ring_full1")], [sem("ring_free0"), sem("ring_free1")],
                plan.la, plan.lo)
    cfg.ring = ring
    width, ck, nt = cfg.width, cfg.ck, cfg.nt
    shifted = [sb("shifted0", [P, width]), sb("shifted1", [P, width])]
    top = sb("top", [P, 2, cfg.heads])
    probs = [sb("probs0", [P, nt * T]), sb("probs1", [P, nt * T])]
    out_sb = sb("out_sb", [P, 4 * T])
    inverse = sb("inverse", [P, 4 * T])
    normed = sb("normed", [P, 4 * T])
    if cfg.apart:
        key_sums = [sb("key_sums0", [P, T]), sb("key_sums1", [P, T])]
        summed, sums_done = cfg.summed, cfg.sums_done = sem("summed"), sem("sums_done")
    cfg.normed, cfg.inverse, cfg.out_sb, cfg.denominators = normed, inverse, out_sb, denominators

    scored, scores_free = sem("scored"), sem("scores_free")
    maxed, shifted_ready = sem("maxed"), sem("shifted_ready")
    turned, exped, valued = sem("turned"), sem("exped"), sem("valued")
    heads_read = sem("heads_read")
    dve_chain, dve_once, pool_chain = sem("dve_chain"), sem("dve_once"), sem("pool_chain")
    cfg.scores_free, cfg.valued, cfg.heads_read = scores_free, valued, heads_read
    cfg.allocate(sb, sem)
    block = stack.enter_context(nc.Block())

    def unit(b, u):
        return b * U + u

    def first(b):
        return isinstance(b, int) and b == 0

    def last(b):
        return isinstance(b, int) and b == NB - 1

    @block.sync
    def _(sp):
        cfg.sync(sp)

    @block.gpsimd
    def _(pool):
        chain = Chain(pool, pool_chain, cfg.pool_per_body)
        cfg.pool_start(pool, chain)
        for name in sum((plan.normalise[s] for s in sorted(plan.normalise)), []):
            cfg.pool(pool, name, 0, 0, chain)
        for name, c in plan.first():
            cfg.pool(pool, name, 0, 0, chain)

        def body(b, par):
            for s in range(U + 2):
                if not last(b):
                    for name in plan.normalise.get(s, ()):
                        cfg.pool(pool, name, b + 1, 1 - par, chain)
                if not first(b):
                    for name, c in plan.finish_at(s):
                        cfg.pool(pool, name, b - 1, 1 - par, chain)
                if not last(b):
                    for name, c in plan.prepare_at(s):
                        cfg.pool(pool, name, b + 1, 1 - par, chain)

        if cfg.pool_works:
            over(pool, NB, body, chain)
            for name, c in plan.last():
                cfg.pool(pool, name, NB - 1, 1, chain)

    @block.tensor
    def _(pe):
        for name, c in plan.first():
            cfg.pe(pe, name, 0, 0, c, 0)

        def body(b, par):
            for s in range(U + 2):
                if s < U:
                    at_least(pe, scores_free if cfg.bounds else shifted_ready, unit(b, s) - 1)
                    cfg.pe_scores(pe, b, s, par, scores[s % 2]).then_inc(scored, 1)
                if 1 <= s <= U:
                    u = s - 1
                    pe.wait_ge(shifted_ready, unit(b, u) + 1)
                    at_least(pe, exped, unit(b, u) - 1)
                    for i in range(nt):
                        ins = nc.tensor.transpose(flipped[u % 2][0:ck, i * T:(i + 1) * T],
                                                  shifted[u % 2][0:T, i * ck:(i + 1) * ck], const("ident", T)[:, 0:T])
                    ins.then_inc(turned, 1)
                if s >= 2:
                    u = s - 2
                    pe.wait_ge(exped, unit(b, u) + 1)
                    if u == 0:
                        at_least(pe, heads_read, b)
                    cfg.pe_values(pe, b, u, par, probs[u % 2], heads_out).then_inc(valued, 1)
                if cfg.apart and s >= 2:
                    u = s - 2
                    pe.wait_ge(summed, unit(b, u) + 1)
                    if u == 0:
                        at_least(pe, cfg.sums_read, b)
                    nc.tensor.matmul(denominators[XD * (u % 2):XD * (u % 2) + XD, (u // 2) * T:(u // 2 + 1) * T],
                                     cfg.ones[0:ck, 0:XD], key_sums[u % 2][0:ck, :],
                                     start=True, stop=True).then_inc(sums_done, 1)
                if not first(b):
                    for name, c in plan.finish_at(s):
                        cfg.pe(pe, name, b - 1, 1 - par, c, b)
                if not last(b):
                    for name, c in plan.prepare_at(s):
                        cfg.pe(pe, name, b + 1, 1 - par, c, b)

        over(pe, NB, body)
        for name, c in plan.last():
            cfg.pe(pe, name, NB - 1, 1, c, NB)

    @block.scalar
    def _(act):
        cfg.act_start(act)
        for name, c in plan.first():
            cfg.act(act, name, 0, 0, c, 0)

        def heads(b):
            act.wait_ge(valued, b * U)
            nc.scalar.activation(out_sb[:, :], heads_out[:, 0:4 * T], ACT.Copy).then_inc(heads_read, 1)

        def body(b, par):
            for s in range(U + 2):
                if s == 0 and not first(b):
                    heads(b)
                if 1 <= s <= U:
                    u = s - 1
                    act.wait_ge(turned, unit(b, u) + 1)
                    at_least(act, valued, unit(b, u) - 1)
                    if cfg.apart:
                        at_least(act, summed, unit(b, u) - 1)
                    nc.scalar.activation(probs[u % 2][0:ck, :], flipped[u % 2][0:ck, 0:nt * T], ACT.Exp,
                                         scale=cfg.scale).then_inc(exped, 1)
                if not first(b):
                    for name, c in plan.finish_at(s):
                        cfg.act(act, name, b - 1, 1 - par, c, b)
                if not last(b):
                    for name, c in plan.prepare_at(s):
                        cfg.act(act, name, b + 1, 1 - par, c, b)

        over(act, NB, body)
        heads(NB)
        for name, c in plan.last():
            cfg.act(act, name, NB - 1, 1, c, NB)

    @block.vector
    def _(dve):
        chain = Chain(dve, dve_chain, cfg.dve_per_body, once=dve_once)
        cfg.dve_start(dve, chain)
        for name in sum((plan.normalise[s] for s in sorted(plan.normalise)), []):
            cfg.dve(dve, name, 0, 0, None, 0, chain)
        for name, c in plan.first():
            cfg.dve(dve, name, 0, 0, c, 0, chain)

        def key_sum(b, u):
            dve.wait_ge(exped, unit(b, u) + 1)
            at_least(dve, sums_done, unit(b, u) - 1)
            nc.vector.tensor_reduce(key_sums[u % 2][0:ck, :],
                                    probs[u % 2][0:ck, :].rearrange("p (c t) -> p t c", t=T),
                                    AX_X, ALU.add).then_inc(summed, 1)

        def body(b, par):
            for s in range(U + 2):
                if cfg.apart and s == 0 and not first(b):
                    cfg.dve_finish(dve, b - 1)
                if s < U:
                    nh = cfg.heads
                    hold = shifted[s % 2][0:T, :].rearrange("p (h k) -> p h k", h=nh)
                    bank = scores[s % 2][0:T, 0:width].rearrange("p (h k) -> p h k", h=nh)
                    dve.wait_ge(scored, unit(b, s) + 1)
                    at_least(dve, turned, unit(b, s) - 1)
                    if cfg.bounds:
                        cfg.dve_bound(dve, s, par, b, hold, bank).then_inc(scores_free, 1)
                        dve.wait_ge(scores_free, unit(b, s) + 1)
                    src = hold if cfg.bounds else bank
                    nc.vector.tensor_reduce(top[0:T, s % 2, :], src, AX_X, ALU.max).then_inc(maxed, 1)
                    dve.wait_ge(maxed, unit(b, s) + 1)
                    ins = nc.vector.tensor_tensor(hold, src, bc(top[0:T, s % 2, :], 2, width // nh), ALU.subtract)
                    ins.then_inc(shifted_ready, 1)
                if cfg.apart and s >= 1 and s <= U:
                    key_sum(b, s - 1)
                if not last(b):
                    for name in plan.normalise.get(s, ()):
                        cfg.dve(dve, name, b + 1, 1 - par, None, b, chain)
                if not first(b):
                    for name, c in plan.finish_at(s):
                        cfg.dve(dve, name, b - 1, 1 - par, c, b, chain)
                if not last(b):
                    for name, c in plan.prepare_at(s):
                        cfg.dve(dve, name, b + 1, 1 - par, c, b, chain)

        over(dve, NB, body, chain)
        if cfg.apart:
            cfg.dve_finish(dve, NB - 1)
        for name, c in plan.last():
            cfg.dve(dve, name, NB - 1, 1, c, NB, chain)


class Phase:
    apart = False
    bounds = True
    dve_per_body = pool_per_body = 0
    pool_works = True
    scale = 1.0

    def __init__(self, nc, G, W):
        self.nc, self.G, self.W = nc, G, W
        self.X, self.const = G["X"], G["const"]
        self.NB = G["NB"]

    def sync(self, sp):
        pass

    def pool_start(self, pool, chain):
        pass

    def dve_start(self, dve, chain):
        pass

    def act_start(self, act):
        pass

    def allocate_norm(self, sb, sem, tag=""):
        n = type("Norm", (), {})()
        n.stats, n.mv, n.var, n.rstd = sb(f"stats{tag}", [P, 6]), sb(f"mv{tag}", [P, 2]), sb(f"var{tag}", [P, 1]), sb(f"rstd{tag}", [P, 1])
        n.var_ready, n.rstd_ready = sem(f"var_ready{tag}"), sem(f"rstd_ready{tag}")
        return n

    def norm_stats(self, n, src, chain):
        nc = self.nc
        chain.link_apart(nc.vector.bn_stats(n.stats[0:T, :], src))
        chain.link(nc.vector.bn_aggr(n.mv[0:T, :], n.stats[0:T, :]))
        nc.vector.tensor_scalar(n.var[0:T, :], n.mv[0:T, 1:2], EPS, None, ALU.add).then_inc(n.var_ready, 1)

    def norm_power(self, pool, n, b):
        pool.wait_ge(n.var_ready, b + 1)
        self.nc.gpsimd.tensor_tensor(n.rstd[0:T, :], n.var[0:T, :], self.G["half"][0:T, 0:1],
                                     ALU.pow).then_inc(n.rstd_ready, 1)

    def norm_scale(self, dve, n, b, dst, src):
        dve.wait_ge(n.rstd_ready, b + 1)
        return self.nc.vector.tensor_scalar(dst, src, n.mv[0:T, 0:1], n.rstd[0:T, :], ALU.subtract, ALU.mult)

    def end_pe(self, pe, name, b, par, c, body, wo):
        nc, ring = self.nc, self.ring
        if name == "denominators":
            bank = ring.claim(pe, c, body)
            pe.wait_ge(self.heads_read, b + 1)
            ring.filled(nc.tensor.matmul(bank[:, 0:4 * T], self.const("pick"), self.out_sb[:, :],
                                         start=True, stop=True), c)
        elif name == "project":
            bank = ring.claim(pe, c, body)
            pe.wait_ge(self.normed_ready, b + 1)
            for g in range(HG):
                ins = nc.tensor.matmul(bank[0:T, 0:D], self.normed[:, g * T:(g + 1) * T], wo[:, g, :],
                                       start=(g == 0), stop=(g == HG - 1))
            ring.filled(ins, c)

    def end_dve(self, dve, name, b, par, c, body, chain):
        nc, ring = self.nc, self.ring
        if name == "denominators":
            bank = ring.take(dve, c, body)
            ring.freed(nc.vector.reciprocal(self.inverse[:, :], bank[:, 0:4 * T]), c)
            ring.emptied(dve, c, body)
            nc.vector.tensor_tensor(self.normed[:, :], self.out_sb[:, :], self.inverse[:, :],
                                    ALU.mult).then_inc(self.normed_ready, 1)
        elif name == "project":
            bank = ring.take(dve, c, body)
            ring.freed(nc.vector.tensor_tensor(self.X[0:T, b, :], bank[0:T, 0:D], self.X[0:T, b, :], ALU.add), c)

    def widen(self, dst, src, mask, groups, heads, width):
        return self.nc.vector.tensor_tensor(
            dst, bc(src.rearrange("p (g t) -> p g t", g=groups), 2, heads),
            bc(bc(mask, 1, groups), 3, width), ALU.mult)

    def ready(self, eng, name, b, claimed=None):
        c, body = self.plan.spot_of(name, b)
        if claimed is None or (claimed - c) % 2:
            self.ring.emptied(eng, c, body)

    def pe_values(self, pe, b, u, par, probs, out):
        if u == 0:
            self.ready(pe, "v", b)
        for a in range(HS):
            h = HS * u + a
            ins = self.nc.tensor.matmul(out[SLOT * a:SLOT * (a + 1), u * T:(u + 1) * T], self.v[par][0:T, h, :],
                                        probs[0:T, a * T:(a + 1) * T], start=True, stop=True)
        return ins

    def pe_transpose(self, pe, name, b, c, body, src, ready, n):
        bank = self.ring.claim(pe, c, body)
        pe.wait_ge(ready, n)
        for f in range(DC):
            ins = self.nc.tensor.transpose(bank[:, f * T:(f + 1) * T], src[0:T, f * P:(f + 1) * P],
                                           self.const("ident", T)[:, 0:T])
        self.ring.filled(ins, c)

    def pe_columns(self, pe, c, body, w, xT, b, wait):
        bank = self.ring.claim(pe, c, body)
        if wait:
            self.ready(pe, wait, b, c)
        for g in range(DC):
            for f in range(DC):
                ins = self.nc.tensor.matmul(bank[:, g * T:(g + 1) * T], w[:, f, g * P:(g + 1) * P], xT[:, f, :],
                                            start=(f == 0), stop=(f == DC - 1))
        self.ring.filled(ins, c)

    def pe_rows(self, pe, c, body, xT, w, rows):
        bank = self.ring.claim(pe, c, body)
        for f in range(DC):
            ins = self.nc.tensor.matmul(bank[0:rows, 0:w.shape[2]], xT[:, f, :], w[:, f, :],
                                        start=(f == 0), stop=(f == DC - 1))
        self.ring.filled(ins, c)

    def copy_out(self, act, c, body, dst, src_of):
        bank = self.ring.take(act, c, body)
        self.ring.freed(self.nc.scalar.activation(dst, src_of(bank), ACT.Copy), c)


class CausalAttention(Phase):
    tag = "a0"
    width, ck, nt, heads = HS * T, T, HS, HS
    scale = HD ** -0.5
    dve_per_body = 1

    def __init__(self, nc, G, W):
        super().__init__(nc, G, W)
        self.plan = Plan(4, {1: ["denominators"], 2: ["project"]},
                         {2: ["xT"], 3: ["q"], 4: ["k"], 5: ["v"]}, {0: ["stats"], 1: ["scale"]})

    def allocate(self, sb, sem):
        self.norm = self.allocate_norm(sb, sem)
        self.xn, self.xT = sb("xn", [P, D]), sb("xT", [P, DC, T])
        self.q = [sb(f"q{i}", [P, DC, 8, T]) for i in range(2)]
        self.k = [sb(f"k{i}", [P, DC, T]) for i in range(2)]
        self.v = [sb(f"v{i}", [P, H, SLOT]) for i in range(2)]
        self.xn_ready, self.normed_ready = sem("xn_ready"), sem("normed_ready")

    def dve_start(self, dve, chain):
        for i in range(2):
            chain.link(self.nc.vector.memset(self.v[i][:], 1.0))

    def pool(self, pool, name, b, par, chain):
        if name == "stats":
            self.norm_power(pool, self.norm, b)

    def pe(self, pe, name, b, par, c, body):
        W = self.W
        if name == "xT":
            self.pe_transpose(pe, name, b, c, body, self.xn, self.xn_ready, b + 1)
        elif name in ("q", "k"):
            self.pe_columns(pe, c, body, W["w" + name], self.xT, b, "xT")
        elif name == "v":
            self.pe_rows(pe, c, body, self.xT, W["wv"], T)
        else:
            self.end_pe(pe, name, b, par, c, body, W["wo"])

    def pe_scores(self, pe, b, u, par, bank):
        if u == 0:
            self.ready(pe, "q", b)
            self.ready(pe, "k", b)
        for a in range(HS):
            h = HS * u + a
            ins = self.nc.tensor.matmul(bank[0:T, a * T:(a + 1) * T], self.q[par][:, h // 8, h % 8, :],
                                        self.k[par][:, h // 8, :], start=True, stop=True)
        return ins

    def act(self, act, name, b, par, c, body):
        if name == "xT":
            self.copy_out(act, c, body, self.xT[:].rearrange("p f t -> p (f t)"), lambda bank: bank[:, 0:DC * T])
        elif name == "k":
            self.copy_out(act, c, body, self.k[par][:].rearrange("p f t -> p (f t)"), lambda bank: bank[:, 0:DC * T])

    def dve_bound(self, dve, u, par, b, hold, bank):
        return self.nc.vector.scalar_tensor_tensor(hold, bank, -BIG, bc(self.const("keep0", T), 1, HS),
                                                   ALU.max, ALU.min)

    def dve(self, dve, name, b, par, c, body, chain):
        nc, ring, X = self.nc, self.ring, self.X
        if name == "stats":
            self.norm_stats(self.norm, X[0:T, b, :], chain)
        elif name == "scale":
            self.norm_scale(dve, self.norm, b, self.xn[0:T, :], X[0:T, b, :]).then_inc(self.xn_ready, 1)
        elif name == "q":
            bank = ring.take(dve, c, body)
            ring.freed(self.widen(self.q[par][:], bank[:, 0:DC * T], self.const("mask8"), DC, 8, T), c)
        elif name == "v":
            bank = ring.take(dve, c, body)
            ring.freed(nc.vector.tensor_tensor(self.v[par][0:T, :, 0:HD],
                                               bank[0:T, 0:D].rearrange("t (h d) -> t h d", h=H),
                                               self.W["vb"][0:T, :].rearrange("t (h d) -> t h d", h=H), ALU.add), c)
        else:
            self.end_dve(dve, name, b, par, c, body, chain)


class LatentAttention(Phase):
    tag = "x0"
    apart = True
    width, ck, nt, heads = XK, XCK, XC, 1
    scale = XD ** -0.5 * XD ** -0.5
    dve_per_body = 9

    def __init__(self, nc, G, W):
        super().__init__(nc, G, W)
        self.plan = Plan(XH, {1: ["project"]},
                         {3: ["ctx0", "ctx1"], 4: ["lat"], 5: ["q0"], 6: ["q1", "k0"], 7: ["k1", "k2"],
                          8: ["k3", "v0"], 9: ["v1", "v2", "v3"]},
                         {0: ["stats"], 1: ["again"], 2: ["scale"]})

    def allocate(self, sb, sem):
        self.norm, self.norm2 = self.allocate_norm(sb, sem), self.allocate_norm(sb, sem, "2")
        self.out_norm = self.allocate_norm(sb, sem, "3")
        self.cstats, self.cmv = sb("cstats", [P, CC, 6]), sb("cmv", [P, CC, 2])
        self.cvar, self.crstd = sb("cvar", [P, CC]), sb("crstd", [P, CC])
        self.cvar_ready, self.crstd_ready = sem("cvar_ready"), sem("crstd_ready")
        self.ctx = [sb(f"ctx{i}", [P, CC, D]) for i in range(2)]
        self.ctx_loaded = [sem(f"ctx_loaded{i}") for i in range(2)]
        self.mask = [sb(f"mask{i}", [P, S2], U8) for i in range(2)]
        self.mask_loaded = [sem(f"mask_loaded{i}") for i in range(2)]
        self.keep = [sb(f"keep{i}", [P, XK]) for i in range(2)]
        self.xn, self.ctx_n = sb("xn", [P, D]), sb("ctx_n", [P, CC, D])
        self.kv = sb("kv", [P, DC, XK])
        self.q = [sb(f"q{i}", [P, 4, 2, T]) for i in range(2)]
        self.k = [sb(f"k{i}", [P, 4, XK]) for i in range(2)]
        self.v = [sb(f"v{i}", [P, XC, XH * XD]) for i in range(2)]
        self.ones = sb("ones", [P, XD])
        self.out2 = sb("out2", [P, D])
        self.xn_ready, self.ctx_ready, self.normed_ready = sem("xn_ready"), sem("ctx_ready"), sem("normed_ready")
        self.sums_read, self.set_up = sem("sums_read"), sem("set_up")

    def sync(self, sp):
        load_context(self, sp, lambda before: sp.wait_ge(self.ctx_ready, before + 1), self.G["t"]["mask"])

    def pool_start(self, pool, chain):
        for i in range(2):
            pool.memset(self.keep[i][:, S2:XK - 1], BIG).then_inc(self.set_up, 1)
            pool.memset(self.keep[i][:, XK - 1:XK], -BIG).then_inc(self.set_up, 1)
            pool.memset(self.q[i][:], 0.0).then_inc(self.set_up, 1)
        pool.memset(self.kv[:, :, XK - 1:XK], 0.0).then_inc(self.set_up, 1)
        pool.memset(self.ones[:], 1.0).then_inc(self.set_up, 1)

    def pool(self, pool, name, b, par, chain):
        if name == "stats":
            self.norm_power(pool, self.norm, b)
            pool.wait_ge(self.cvar_ready, b + 1)
            self.nc.gpsimd.tensor_tensor(self.crstd[0:CK, :], self.cvar[0:CK, :], self.G["half"][0:CK, 0:CC],
                                         ALU.pow).then_inc(self.crstd_ready, 1)
        elif name == "again":
            self.norm_power(pool, self.norm2, b)
        elif name == "project":
            self.norm_power(pool, self.out_norm, b)

    def pe(self, pe, name, b, par, c, body):
        nc, ring, W = self.nc, self.ring, self.W
        if name in ("ctx0", "ctx1"):
            f = int(name[3])
            bank = ring.claim(pe, c, body)
            pe.wait_ge(self.ctx_ready, b + 1)
            for i in range(CC):
                ins = nc.tensor.transpose(bank[:, i * CK:(i + 1) * CK], self.ctx_n[0:CK, i, f * P:(f + 1) * P],
                                          self.const("ident", CK)[:, 0:CK])
            ring.filled(ins, c)
        elif name == "lat":
            self.pe_transpose(pe, name, b, c, body, self.xn, self.xn_ready, b + 1)
        elif name in ("q0", "q1"):
            bank = ring.claim(pe, c, body)
            if name == "q0":
                self.ready(pe, "lat", b, c)
            for i in range(2):
                m = 2 * int(name[1]) + i
                for f in range(DC):
                    ins = nc.tensor.matmul(bank[:, i * T:(i + 1) * T], W["xq"][:, f, m * P:(m + 1) * P],
                                           self.kv[:, f, S2:S2 + T], start=(f == 0), stop=(f == DC - 1))
            ring.filled(ins, c)
        elif name in ("k0", "k1", "k2", "k3"):
            bank = ring.claim(pe, c, body)
            m = int(name[1])
            if m == 0:
                self.ready(pe, "ctx0", b, c)
                self.ready(pe, "ctx1", b, c)
            for f in range(DC):
                ins = nc.tensor.matmul(bank[:, 0:XK], W["xkv"][:, f, m * P:(m + 1) * P], self.kv[:, f, :],
                                       start=(f == 0), stop=(f == DC - 1))
            ring.filled(ins, c)
        elif name[0] == "v":
            bank = ring.claim(pe, c, body)
            i = int(name[1])
            for f in range(DC):
                ins = nc.tensor.matmul(bank[0:XCK, :], self.kv[:, f, i * XCK:(i + 1) * XCK], W["xkv"][:, f, 512:1024],
                                       start=(f == 0), stop=(f == DC - 1))
            ring.filled(ins, c)
        elif name == "project":
            bank = ring.claim(pe, c, body)
            pe.wait_ge(self.normed_ready, b + 1)
            for m in range(4):
                ins = nc.tensor.matmul(bank[0:T, 0:D], self.normed[:, m * T:(m + 1) * T], W["xo"][:, m, :],
                                       start=(m == 0), stop=(m == 3))
            ring.filled(ins, c)

    def pe_scores(self, pe, b, u, par, bank):
        if u == 0:
            self.ready(pe, "k3", b)
        return self.nc.tensor.matmul(bank[0:T, 0:XK], self.q[par][:, u // 2, u % 2, :], self.k[par][:, u // 2, :],
                                     start=True, stop=True)

    def pe_values(self, pe, b, u, par, probs, out):
        if u == 0:
            self.ready(pe, "v2", b)
            self.ready(pe, "v3", b)
        for i in range(XC):
            ins = self.nc.tensor.matmul(out[XD * (u % 2):XD * (u % 2 + 1), (u // 2) * T:(u // 2 + 1) * T],
                                        self.v[par][0:XCK, i, u * XD:(u + 1) * XD], probs[0:XCK, i * T:(i + 1) * T],
                                        start=(i == 0), stop=(i == XC - 1))
        return ins

    def act(self, act, name, b, par, c, body):
        nc, ring, W = self.nc, self.ring, self.W
        if name in ("ctx0", "ctx1"):
            f = int(name[3])
            bank = ring.take(act, c, body)
            ring.freed(nc.scalar.activation(self.kv[:, f, 0:S2], bank[:, 0:S2], ACT.Identity,
                                            bias=W["lnx"][:, 1, f:f + 1], scale=W["lnx"][:, 0, f:f + 1]), c)
        elif name == "lat":
            bank = ring.take(act, c, body)
            for f in range(DC):
                ins = nc.scalar.activation(self.kv[:, f, S2:S2 + T], bank[:, f * T:(f + 1) * T], ACT.Identity,
                                           bias=W["lnl"][:, 1, f:f + 1], scale=W["lnl"][:, 0, f:f + 1])
            ring.freed(ins, c)
        elif name in ("q0", "q1"):
            bank = ring.take(act, c, body)
            m = 2 * int(name[1])
            for i in range(2):
                half = slice(XD * i, XD * (i + 1))
                ins = nc.scalar.activation(self.q[par][half, m:m + 2, i, :],
                                           bank[half, 0:2 * T].rearrange("p (m t) -> p m t", m=2), ACT.Copy)
            ring.freed(ins, c)
        elif name in ("k0", "k1", "k2", "k3"):
            self.copy_out(act, c, body, self.k[par][:, int(name[1]), :], lambda bank: bank[:, 0:XK])
        elif name[0] == "v":
            self.copy_out(act, c, body, self.v[par][0:XCK, int(name[1]), :], lambda bank: bank[0:XCK, :])

    def act_start(self, act):
        act.wait_ge(self.set_up, 8)

    def dve_bound(self, dve, u, par, b, hold, bank):
        return self.nc.vector.scalar_tensor_tensor(hold, bank, -BIG, self.keep[par][0:T, :].unsqueeze(1),
                                                   ALU.max, ALU.min)

    def dve_start(self, dve, chain):
        dve.wait_ge(self.set_up, 8)

    def dve(self, dve, name, b, par, c, body, chain):
        nc, ring, X = self.nc, self.ring, self.X
        ctx = self.ctx[par]
        if name == "stats":
            self.norm_stats(self.norm, X[0:T, b, :], chain)
            dve.wait_ge(self.ctx_loaded[par], loads(b, par))
            for i in range(CC):
                ins = nc.vector.bn_stats(self.cstats[0:CK, i, :], ctx[0:CK, i, :])
            chain.link_apart(ins)
            for i in range(CC):
                ins = nc.vector.bn_aggr(self.cmv[0:CK, i, :], self.cstats[0:CK, i, :])
            chain.link(ins)
            nc.vector.tensor_scalar(self.cvar[0:CK, :], self.cmv[0:CK, :, 1], EPS, None,
                                    ALU.add).then_inc(self.cvar_ready, 1)
            dve.wait_ge(self.mask_loaded[par], loads(b, par))
            chain.link(nc.vector.tensor_scalar(self.keep[par][0:T, 0:S2], self.mask[par][0:T, :], 2 * BIG, -BIG,
                                               ALU.mult, ALU.add))
        elif name == "again":
            chain.link(self.norm_scale(dve, self.norm, b, self.xn[0:T, :], X[0:T, b, :]))
            self.norm_stats(self.norm2, self.xn[0:T, :], chain)
            dve.wait_ge(self.crstd_ready, b + 1)
            for i in range(CC):
                ins = nc.vector.tensor_scalar(self.ctx_n[0:CK, i, :], ctx[0:CK, i, :], self.cmv[0:CK, i, 0:1],
                                              self.crstd[0:CK, i:i + 1], ALU.subtract, ALU.mult)
            ins.then_inc(self.ctx_ready, 1)
        elif name == "scale":
            self.norm_scale(dve, self.norm2, b, self.xn[0:T, :], self.xn[0:T, :]).then_inc(self.xn_ready, 1)
        elif name == "project":
            bank = ring.take(dve, c, body)
            self.norm_stats(self.out_norm, bank[0:T, 0:D], chain)
            dve.wait_ge(self.out_norm.rstd_ready, b + 1)
            n = self.out_norm
            ring.freed(nc.vector.tensor_scalar(self.out2[0:T, :], bank[0:T, 0:D], n.mv[0:T, 0:1], n.rstd[0:T, :],
                                               ALU.subtract, ALU.mult), c)
            ring.emptied(dve, c, body)
            lno = self.W["lno"]
            chain.link(nc.vector.tensor_tensor(self.out2[0:T, :], self.out2[0:T, :], lno[0:T, 0, :], ALU.mult))
            chain.link(nc.vector.tensor_tensor(self.out2[0:T, :], self.out2[0:T, :], lno[0:T, 1, :], ALU.add))
            chain.link(nc.vector.tensor_tensor(X[0:T, b, :], X[0:T, b, :], self.out2[0:T, :], ALU.add))

    def dve_finish(self, dve, b):
        dve.wait_ge(self.sums_done, (b + 1) * XH)
        self.nc.vector.reciprocal(self.inverse[:, :], self.denominators[:, 0:4 * T]).then_inc(self.sums_read, 1)
        dve.wait_ge(self.heads_read, b + 1)
        dve.wait_ge(self.sums_read, b + 1)
        self.nc.vector.tensor_tensor(self.normed[:, :], self.out_sb[:, :], self.inverse[:, :],
                                     ALU.mult).then_inc(self.normed_ready, 1)


def load_context(phase, sp, before_reuse, masks=None):
    ctx = phase.G["t"]["ctx_1024"]

    def load(b, par, before):
        if before is not None:
            before_reuse(before)
        sp.dma_start(phase.ctx[par][0:CK, :, :],
                     ctx[b].rearrange("(c p) d -> p c d", p=CK)).then_inc(phase.ctx_loaded[par], 16)
        if masks is not None:
            sp.dma_start(phase.mask[par][0:T, :], masks[b].partition_broadcast(T)).then_inc(phase.mask_loaded[par], 16)

    load(0, 0, None)
    load(1, 1, None)
    load(2, 0, 0)
    load(3, 1, 1)
    if phase.NB > 4:
        with sp.Fori(0, (phase.NB - 4) // 2) as it:
            load(it * 2 + 4, 0, it * 2 + 2)
            load(it * 2 + 5, 1, it * 2 + 3)


def loads(b, par):
    if isinstance(b, int):
        return 16 * (b // 2 + 1)
    return (b - par) * 8 + 16


class RotaryAttention(Phase):
    tag = "a1"
    width, ck, nt, heads = HS * T, T, HS, HS
    scale = 24 ** -0.5
    dve_per_body = 4

    def __init__(self, nc, G, W):
        super().__init__(nc, G, W)
        self.plan = Plan(4, {1: ["denominators"], 2: ["project"]},
                         {2: ["xT", "c"], 3: ["kr", "q"], 4: ["turnq", "turnk"], 5: ["kc", "v"]},
                         {0: ["stats"], 1: ["scale"]})

    def allocate(self, sb, sem):
        self.norm = self.allocate_norm(sb, sem)
        self.xn, self.xT = sb("xn", [P, D]), sb("xT", [P, DC, T])
        self.c, self.kr, self.q_raw = sb("c", [P, T]), sb("kr", [P, T]), sb("q_raw", [P, HG, T])
        self.q_plain, self.q_turned = sb("q_plain", [P, HG, T]), sb("q_turned", [P, HG, T])
        self.kr_plain, self.kr_turned = sb("kr_plain", [P, T]), sb("kr_turned", [P, T])
        self.q = [sb(f"q{i}", [P, HG, HS, T]) for i in range(2)]
        self.k = [sb(f"k{i}", [P, HG, T]) for i in range(2)]
        self.v = [sb(f"v{i}", [P, H, SLOT]) for i in range(2)]
        self.xn_ready, self.normed_ready = sem("xn_ready"), sem("normed_ready")
        self.plain_ready, self.q_ready, self.set_up = sem("plain_ready"), sem("q_ready"), sem("set_up")

    def act_start(self, act):
        act.wait_ge(self.set_up, 2)

    def dve_start(self, dve, chain):
        for i in range(2):
            self.nc.vector.memset(self.v[i][:], 1.0).then_inc(self.set_up, 1)

    def pool(self, pool, name, b, par, chain):
        if name == "stats":
            self.norm_power(pool, self.norm, b)
        elif name == "q":
            self.ready(pool, "q", b)
            self.nc.gpsimd.tensor_tensor(self.q_plain[:], self.q_raw[:], bc(self.const("cosA"), 1, HG),
                                         ALU.mult).then_inc(self.plain_ready, 1)

    def pe(self, pe, name, b, par, c, body):
        nc, ring, W = self.nc, self.ring, self.W
        if name == "xT":
            self.pe_transpose(pe, name, b, c, body, self.xn, self.xn_ready, b + 1)
        elif name in ("c", "kr"):
            bank = ring.claim(pe, c, body)
            if name == "c":
                self.ready(pe, "xT", b, c)
            for f in range(DC):
                ins = nc.tensor.matmul(bank[:, 0:T], W["a" + name][:, f, :], self.xT[:, f, :],
                                       start=(f == 0), stop=(f == DC - 1))
            ring.filled(ins, c)
        elif name in ("q", "kc"):
            bank = ring.claim(pe, c, body)
            if name == "q":
                self.ready(pe, "c", b, c)
            for g in range(HG):
                ins = nc.tensor.matmul(bank[:, g * T:(g + 1) * T], W["a" + name][:, g * P:(g + 1) * P], self.c[:, :],
                                       start=True, stop=True)
            ring.filled(ins, c)
        elif name in ("turnq", "turnk"):
            bank = ring.claim(pe, c, body)
            self.ready(pe, "q" if name == "turnq" else "kr", b, c)
            src = self.q_raw[:].rearrange("p g t -> p (g t)") if name == "turnq" else self.kr[:, :]
            ring.filled(nc.tensor.matmul(bank[:, 0:src.shape[1]], self.const("turnA"), src, start=True, stop=True), c)
        elif name == "v":
            bank = ring.claim(pe, c, body)
            ring.filled(nc.tensor.matmul(bank[0:T, 0:D], self.c[:, :], W["av"][:, :], start=True, stop=True), c)
        else:
            self.end_pe(pe, name, b, par, c, body, W["ao"])

    def pe_scores(self, pe, b, u, par, bank):
        if u == 0:
            pe.wait_ge(self.q_ready, b + 1)
            self.ready(pe, "kc", b)
        for a in range(HS):
            ins = self.nc.tensor.matmul(bank[0:T, a * T:(a + 1) * T], self.q[par][:, u, a, :], self.k[par][:, u, :],
                                        start=True, stop=True)
        return ins

    def act(self, act, name, b, par, c, body):
        if name == "xT":
            self.copy_out(act, c, body, self.xT[:].rearrange("p f t -> p (f t)"), lambda bank: bank[:, 0:DC * T])
        elif name in ("c", "kr"):
            self.copy_out(act, c, body, {"c": self.c, "kr": self.kr}[name][:, :], lambda bank: bank[:, 0:T])
        elif name == "q":
            self.copy_out(act, c, body, self.q_raw[:].rearrange("p g t -> p (g t)"), lambda bank: bank[:, 0:HG * T])
        elif name == "v":
            self.copy_out(act, c, body, self.v[par][0:T, :, 0:HD],
                          lambda bank: bank[0:T, 0:D].rearrange("t (h d) -> t h d", h=H))

    def dve_bound(self, dve, u, par, b, hold, bank):
        return self.nc.vector.scalar_tensor_tensor(hold, bank, -80.0, bc(self.const("keep1", T), 1, HS),
                                                   ALU.max, ALU.min)

    def dve(self, dve, name, b, par, c, body, chain):
        nc, ring, X, const = self.nc, self.ring, self.X, self.const
        if name == "stats":
            self.norm_stats(self.norm, X[0:T, b, :], chain)
        elif name == "scale":
            self.norm_scale(dve, self.norm, b, self.xn[0:T, :], X[0:T, b, :]).then_inc(self.xn_ready, 1)
        elif name == "turnq":
            bank = ring.take(dve, c, body)
            ring.freed(nc.vector.tensor_tensor(self.q_turned[:], bank[:, 0:HG * T].rearrange("p (g t) -> p g t", g=HG),
                                               bc(const("sinA"), 1, HG), ALU.mult), c)
            ring.emptied(dve, c, body)
            dve.wait_ge(self.plain_ready, b + 1)
            chain.link(nc.vector.tensor_tensor(self.q_turned[:], self.q_turned[:], self.q_plain[:], ALU.add))
            self.widen(self.q[par][:], self.q_turned[:].rearrange("p g t -> p (g t)"), const("mask4"), HG, HS,
                       T).then_inc(self.q_ready, 1)
        elif name == "turnk":
            chain.link(nc.vector.tensor_tensor(self.kr_plain[:, :], self.kr[:, :], const("cosA"), ALU.mult))
            bank = ring.take(dve, c, body)
            ring.freed(nc.vector.tensor_tensor(self.kr_turned[:, :], bank[:, 0:T], const("sinA"), ALU.mult), c)
            ring.emptied(dve, c, body)
            chain.link(nc.vector.tensor_tensor(self.kr_turned[:, :], self.kr_turned[:, :], self.kr_plain[:, :],
                                               ALU.add))
        elif name == "kc":
            bank = ring.take(dve, c, body)
            ring.freed(nc.vector.tensor_tensor(self.k[par][:], bank[:, 0:HG * T].rearrange("p (g t) -> p g t", g=HG),
                                               bc(self.kr_turned[:, :], 1, HG), ALU.add), c)
        else:
            self.end_dve(dve, name, b, par, c, body, chain)


class ContextAttention(Phase):
    tag = "x1"
    bounds = False
    width, ck, nt, heads = S2, CK, CC, 1
    scale = HD ** -0.5
    dve_per_body = 2

    def __init__(self, nc, G, W):
        super().__init__(nc, G, W)
        self.plan = Plan(H, {1: ["denominators"], 2: ["project"]},
                         {4: ["ctx0"], 5: ["ctx1"], 6: ["xT"], 7: ["q"], 8: ["turnq"], 9: ["k0"], 10: ["k1"],
                          12: ["turnk0"], 13: ["turnk1"], 15: ["v0"], 16: ["v1"], 17: ["v2"]},
                         {0: ["stats"], 2: ["scale"]})

    def allocate(self, sb, sem):
        self.norm = self.allocate_norm(sb, sem)
        self.ctx = [sb(f"ctx{i}", [P, CC, D]) for i in range(2)]
        self.ctx_loaded = [sem(f"ctx_loaded{i}") for i in range(2)]
        self.ctxT = sb("ctxT", [P, DC, S2])
        self.xn, self.xT = sb("xn", [P, D]), sb("xT", [P, DC, T])
        self.q_raw, self.k_raw = sb("q_raw", [P, DC, T]), sb("k_raw", [P, DC, S2])
        self.q_plain, self.k_plain = sb("q_plain", [P, DC, T]), sb("k_plain", [P, DC, S2])
        self.q_turned, self.k_turned = sb("q_turned", [P, DC, T]), sb("k_turned", [P, DC, S2])
        self.q = [sb(f"q{i}", [P, DC, 8, T]) for i in range(2)]
        self.k = [sb(f"k{i}", [P, DC, S2]) for i in range(2)]
        self.v = [sb(f"v{i}", [P, CC, H, SLOT]) for i in range(2)]
        self.xn_ready, self.normed_ready = sem("xn_ready"), sem("normed_ready")
        self.q_plain_ready, self.k_plain_ready = sem("q_plain_ready"), sem("k_plain_ready")
        self.q_ready, self.k_ready, self.set_up = sem("q_ready"), sem("k_ready"), sem("set_up")

    def sync(self, sp):
        load_context(self, sp, lambda before: self.ready(sp, "ctx1", before))

    def act_start(self, act):
        act.wait_ge(self.set_up, 2)

    def dve_start(self, dve, chain):
        for i in range(2):
            self.nc.vector.memset(self.v[i][:], 1.0).then_inc(self.set_up, 1)

    def pool(self, pool, name, b, par, chain):
        nc = self.nc
        if name == "stats":
            self.norm_power(pool, self.norm, b)
        elif name == "q":
            self.ready(pool, "q", b)
            nc.gpsimd.tensor_tensor(self.q_plain[:], self.q_raw[:], bc(self.const("cosX")[:, 0:T], 1, DC),
                                    ALU.mult).then_inc(self.q_plain_ready, 1)
        elif name in ("k0", "k1"):
            self.ready(pool, name, b)
            g = int(name[1])
            nc.gpsimd.tensor_tensor(self.k_plain[:, g, :], self.k_raw[:, g, :], self.const("cosX"),
                                    ALU.mult).then_inc(self.k_plain_ready, 1)

    def pe(self, pe, name, b, par, c, body):
        nc, ring, W = self.nc, self.ring, self.W
        if name in ("ctx0", "ctx1"):
            f = int(name[3])
            bank = ring.claim(pe, c, body)
            if f == 0:
                pe.wait_ge(self.ctx_loaded[par], loads(b, par))
            for i in range(CC):
                ins = nc.tensor.transpose(bank[:, i * CK:(i + 1) * CK], self.ctx[par][0:CK, i, f * P:(f + 1) * P],
                                          self.const("ident", CK)[:, 0:CK])
            ring.filled(ins, c)
        elif name == "xT":
            self.pe_transpose(pe, name, b, c, body, self.xn, self.xn_ready, b + 1)
        elif name == "q":
            self.pe_columns(pe, c, body, W["cq"], self.xT, b, "xT")
        elif name in ("k0", "k1"):
            bank = ring.claim(pe, c, body)
            g = int(name[1])
            if g == 0:
                self.ready(pe, "ctx0", b, c)
                self.ready(pe, "ctx1", b, c)
            for f in range(DC):
                ins = nc.tensor.matmul(bank[:, 0:S2], W["ck"][:, f, g * P:(g + 1) * P], self.ctxT[:, f, :],
                                       start=(f == 0), stop=(f == DC - 1))
            ring.filled(ins, c)
        elif name == "turnq":
            bank = ring.claim(pe, c, body)
            self.ready(pe, "q", b, c)
            ring.filled(nc.tensor.matmul(bank[:, 0:DC * T], self.const("turnX"),
                                         self.q_raw[:].rearrange("p g t -> p (g t)"), start=True, stop=True), c)
        elif name in ("turnk0", "turnk1"):
            bank = ring.claim(pe, c, body)
            g = int(name[5])
            self.ready(pe, "k" + name[5], b, c)
            ring.filled(nc.tensor.matmul(bank[:, 0:S2], self.const("turnX"), self.k_raw[:, g, :],
                                         start=True, stop=True), c)
        elif name[0] == "v":
            i = int(name[1])
            self.pe_rows(pe, c, body, self.ctxT[:, :, i * CK:(i + 1) * CK], W["cv"], CK)
        else:
            self.end_pe(pe, name, b, par, c, body, W["co"])

    def pe_scores(self, pe, b, u, par, bank):
        if u == 0:
            pe.wait_ge(self.q_ready, b + 1)
            pe.wait_ge(self.k_ready, b + 1)
        return self.nc.tensor.matmul(bank[0:T, 0:S2], self.q[par][:, u // 8, u % 8, :], self.k[par][:, u // 8, :],
                                     start=True, stop=True)

    def pe_values(self, pe, b, u, par, probs, out):
        if u == 0:
            self.ready(pe, "v1", b)
            self.ready(pe, "v2", b)
        a, g = u % HS, u // HS
        for i in range(CC):
            ins = self.nc.tensor.matmul(out[SLOT * a:SLOT * (a + 1), g * T:(g + 1) * T], self.v[par][0:CK, i, u, :],
                                        probs[0:CK, i * T:(i + 1) * T], start=(i == 0), stop=(i == CC - 1))
        return ins

    def act(self, act, name, b, par, c, body):
        if name in ("ctx0", "ctx1"):
            self.copy_out(act, c, body, self.ctxT[:, int(name[3]), :], lambda bank: bank[:, 0:S2])
        elif name == "xT":
            self.copy_out(act, c, body, self.xT[:].rearrange("p f t -> p (f t)"), lambda bank: bank[:, 0:DC * T])
        elif name == "q":
            self.copy_out(act, c, body, self.q_raw[:].rearrange("p f t -> p (f t)"), lambda bank: bank[:, 0:DC * T])
        elif name in ("k0", "k1"):
            self.copy_out(act, c, body, self.k_raw[:, int(name[1]), :], lambda bank: bank[:, 0:S2])
        elif name[0] == "v":
            self.copy_out(act, c, body, self.v[par][0:CK, int(name[1]), :, 0:HD],
                          lambda bank: bank[0:CK, 0:D].rearrange("t (h d) -> t h d", h=H))

    def dve(self, dve, name, b, par, c, body, chain):
        nc, ring, X, const = self.nc, self.ring, self.X, self.const
        if name == "stats":
            self.norm_stats(self.norm, X[0:T, b, :], chain)
        elif name == "scale":
            self.norm_scale(dve, self.norm, b, self.xn[0:T, :], X[0:T, b, :]).then_inc(self.xn_ready, 1)
        elif name == "turnq":
            bank = ring.take(dve, c, body)
            ring.freed(nc.vector.tensor_tensor(self.q_turned[:], bank[:, 0:DC * T].rearrange("p (g t) -> p g t", g=DC),
                                               bc(const("sinX")[:, 0:T], 1, DC), ALU.mult), c)
            ring.emptied(dve, c, body)
            dve.wait_ge(self.q_plain_ready, b + 1)
            chain.link(nc.vector.tensor_tensor(self.q_turned[:], self.q_turned[:], self.q_plain[:], ALU.add))
            self.widen(self.q[par][:], self.q_turned[:].rearrange("p g t -> p (g t)"), const("mask8"), DC, 8,
                       T).then_inc(self.q_ready, 1)
        elif name in ("turnk0", "turnk1"):
            g = int(name[5])
            bank = ring.take(dve, c, body)
            ring.freed(nc.vector.tensor_tensor(self.k_turned[:, g, :], bank[:, 0:S2], const("sinX"), ALU.mult), c)
            ring.emptied(dve, c, body)
            dve.wait_ge(self.k_plain_ready, b * 2 + g + 1)
            ins = nc.vector.tensor_tensor(self.k[par][:, g, :], self.k_turned[:, g, :], self.k_plain[:, g, :],
                                          ALU.add)
            if g == DC - 1:
                ins.then_inc(self.k_ready, 1)
        else:
            self.end_dve(dve, name, b, par, c, body, chain)


class RelativeAttention(CausalAttention):
    tag = "r1"
    scale = HD ** -0.5
    dve_per_body = 3
    PAIRS = 8

    def __init__(self, nc, G, W):
        super().__init__(nc, G, W)
        self.plan = Plan(4, {1: ["denominators"], 2: ["project"]},
                         {2: ["xT", "q"], 3: ["p0", "p1", "p2", "p3"], 4: ["p4", "p5", "p6", "p7"], 5: ["k", "v"]},
                         {0: ["stats"], 1: ["again"], 2: ["scale"]})

    def allocate(self, sb, sem):
        super().allocate(sb, sem)
        self.norm2 = self.allocate_norm(sb, sem, "2")
        self.set_up = sem("set_up")
        self.by_position = sb("by_position", [P, H, RPW])
        self.bias = [sb(f"bias{i}", [P, H, T]) for i in range(2)]
        self.scratch = [self.nc.dram_tensor(f"by_position_{i}", [T, H, RPW], F32).ap() for i in range(2)]
        self.by_position_ready = sem("by_position_ready")
        self.written, self.bias_loaded = sem("written"), [sem(f"bias_loaded{i}") for i in range(2)]

    def sync(self, sp):
        def shift(b, par, first):
            sp.wait_ge(self.by_position_ready, b + 1)
            sp.dma_start(self.scratch[par], self.by_position[0:T, :, :]).then_inc(self.written, 16)
            if not first:
                sp.wait_ge(self.scores_free, b * 4 - 4)
            sp.wait_ge(self.written, b * 16 + 16)
            s = self.scratch[par]
            src = bass.AP(s.tensor, s.offset + T - 1, [(H * RPW - 1, T), (RPW, H), (1, T)])
            sp.dma_start(self.bias[par][0:T, :, :], src).then_inc(self.bias_loaded[par], 16)

        shift(0, 0, True)
        shift(1, 1, True)
        with sp.Fori(0, (self.NB - 2) // 2) as it:
            shift(it * 2 + 2, 0, False)
            shift(it * 2 + 3, 1, False)

    def act_start(self, act):
        act.wait_ge(self.set_up, 2)

    def dve_start(self, dve, chain):
        for i in range(2):
            self.nc.vector.memset(self.v[i][:], 1.0).then_inc(self.set_up, 1)

    def pool(self, pool, name, b, par, chain):
        if name == "stats":
            self.norm_power(pool, self.norm, b)
        elif name == "again":
            self.norm_power(pool, self.norm2, b)

    def pe(self, pe, name, b, par, c, body):
        nc, ring, W = self.nc, self.ring, self.W
        if name == "xT":
            self.pe_transpose(pe, name, b, c, body, self.xn, self.xn_ready, b + 1)
        elif name in ("q", "k"):
            self.pe_columns(pe, c, body, W["r" + name], self.xT, b, "xT" if name == "q" else None)
        elif name == "v":
            self.pe_rows(pe, c, body, self.xT, W["rv"], T)
        elif name[0] == "p" and name != "project":
            bank = ring.claim(pe, c, body)
            if name == "p0":
                self.ready(pe, "q", b, c)
            for i in range(2):
                h = 2 * int(name[1]) + i
                ins = nc.tensor.matmul(bank[0:T, i * RPW:(i + 1) * RPW], self.q[par][:, h // 8, h % 8, :],
                                       W["pT"][:, h // 8, :], start=True, stop=True)
            ring.filled(ins, c)
        else:
            self.end_pe(pe, name, b, par, c, body, W["ro"])

    def act(self, act, name, b, par, c, body):
        nc, ring = self.nc, self.ring
        if name == "xT":
            ln = self.W["rln"]
            bank = ring.take(act, c, body)
            for f in range(DC):
                ins = nc.scalar.activation(self.xT[:, f, :], bank[:, f * T:(f + 1) * T], ACT.Identity,
                                           bias=ln[:, 1, f:f + 1], scale=ln[:, 0, f:f + 1])
            ring.freed(ins, c)
        elif name == "k":
            self.copy_out(act, c, body, self.k[par][:].rearrange("p f t -> p (f t)"), lambda bank: bank[:, 0:DC * T])
        elif name == "v":
            self.copy_out(act, c, body, self.v[par][0:T, :, 0:HD],
                          lambda bank: bank[0:T, 0:D].rearrange("t (h d) -> t h d", h=H))
        elif name[0] == "p" and name not in ("project",):
            i = int(name[1])
            if i == 0:
                at_least(act, self.written, b * 16)
            self.copy_out(act, c, body, self.by_position[0:T, 2 * i:2 * i + 2, :].rearrange("t h r -> t (h r)"),
                          lambda bank: bank[0:T, 0:2 * RPW])
            if i == self.PAIRS - 1:
                self.ready(act, "p6", b)
                self.ready(act, "p7", b)
                act.sem_inc(self.by_position_ready, 1)

    def dve_bound(self, dve, u, par, b, hold, bank):
        if u == 0:
            dve.wait_ge(self.bias_loaded[par], loads(b, par))
        return self.nc.vector.tensor_tensor(hold, bank, self.bias[par][0:T, HS * u:HS * (u + 1), :], ALU.add)

    def dve(self, dve, name, b, par, c, body, chain):
        nc, ring, X, S = self.nc, self.ring, self.X, self.G["S2"]
        if name == "stats":
            self.norm_stats(self.norm, X[0:T, b, :], chain)
        elif name == "again":
            chain.link(self.norm_scale(dve, self.norm, b, S[0:T, b, :], X[0:T, b, :]))
            nc.vector.tensor_tensor(X[0:T, b, :], X[0:T, b, :], S[0:T, b, :], ALU.add)
            self.norm_stats(self.norm2, S[0:T, b, :], chain)
        elif name == "scale":
            self.norm_scale(dve, self.norm2, b, self.xn[0:T, :], S[0:T, b, :]).then_inc(self.xn_ready, 1)
        elif name == "q":
            bank = ring.take(dve, c, body)
            ring.freed(self.widen(self.q[par][:], bank[:, 0:DC * T], self.const("mask8"), DC, 8, T), c)
        elif name == "project":
            bank = ring.take(dve, c, body)
            nc.vector.tensor_tensor(S[0:T, b, :], bank[0:T, 0:D], S[0:T, b, :], ALU.add)
            ring.freed(nc.vector.tensor_tensor(X[0:T, b, :], bank[0:T, 0:D], X[0:T, b, :], ALU.add), c)
        elif name == "denominators":
            self.end_dve(dve, name, b, par, c, body, chain)


def load_layer1(nc, G, stack):
    t = G["t"]
    sb, _, _ = G["alloc"](stack, "w1")
    W = dict(ac=sb("ac", [P, DC, P]), akr=sb("akr", [P, DC, P]), aq=sb("aq", [P, H * SLOT]),
             akc=sb("akc", [P, H * SLOT]), av=sb("av", [P, D]), ao=sb("ao", [P, HG, D]),
             cq=sb("cq", [P, DC, D]), ck=sb("ck", [P, DC, D]), cv=sb("cv", [P, DC, D]), co=sb("co", [P, HG, D]),
             rq=sb("rq", [P, DC, D]), rk=sb("rk", [P, DC, D]), rv=sb("rv", [P, DC, D]), ro=sb("ro", [P, HG, D]),
             rln=sb("rln", [P, 2, DC]), pT=sb("pT", [P, DC, RPW]))
    R = 64
    rows = lambda name: t[name].rearrange("(c p) n -> p c n", p=P)
    with ExitStack() as own:
        sbt, psum, sem = G["alloc"](own, "p1")
        wp = sbt("wp", [P, DC, D])
        loads = [(W["ac"][:, :, 0:R], rows("L1_attn_W_DQ")), (W["ac"][:, :, R:2 * R], rows("L1_attn_W_DKV")),
                 (W["cq"][:], rows("x_qT")), (W["ck"][:], rows("x_kT")), (W["cv"][:], rows("x_vT")),
                 (W["rq"][:], rows("L1_ffn_wq")), (W["rk"][:], rows("L1_ffn_wk")), (W["rv"][:], rows("L1_ffn_wv")),
                 (wp[:], rows("L1_ffn_wp"))] + columns(W["rln"], t["L1_ffn_ln1_g"], t["L1_ffn_ln1_b"])
        heads = lambda tile, a, b: tile[a:b, :].rearrange("p (h s) -> p h s", s=SLOT)
        slots = [(heads(W["aq"], 0, R)[:, :, 0:HD], t["L1_attn_W_UQ"].rearrange("r (h d) -> r h d", h=H)),
                 (heads(W["aq"], 0, R)[:, :, HD:HD + 8], t["L1_attn_W_QR"].rearrange("r (h d) -> r h d", h=H)),
                 (heads(W["akc"], R, 2 * R)[:, :, 0:HD], t["L1_attn_W_UK"].rearrange("r (h d) -> r h d", h=H)),
                 (W["av"][R:2 * R, :], t["L1_attn_W_UV"]),
                 (W["co"][HD:HD + 1, 0, :], t["L1_xattn_bo"].rearrange("(a n) -> a n", a=1))]
        for a in range(HS):
            s = slice(SLOT * a, SLOT * a + HD)
            slots += [(W["akr"][:, :, SLOT * a + HD:SLOT * a + HD + 8], rows("L1_attn_W_KR")),
                      (W["ao"][s, :, :], rows_in_slots(t["L1_attn_W_O"])[a]),
                      (W["co"][s, :, :], rows_in_slots(t["x_oT"])[a]),
                      (W["ro"][s, :, :], rows_in_slots(t["L1_ffn_wo"])[a])]
        load_all(nc, G, "l1", loads, [W[n] for n in ("akr", "aq", "akc", "av", "ao", "co", "ro")], slots)
        banks = [psum("bank0"), psum("bank1")]
        made = sem("made")
        block = own.enter_context(nc.Block())
        pe_table = G["const"]("pe").rearrange("p (f r) -> p f r", f=DC)

        @block.tensor
        def _(pe):
            for g in range(DC):
                for f in range(DC):
                    ins = nc.tensor.matmul(banks[g][:, 0:RPW], wp[:, f, g * P:(g + 1) * P], pe_table[:, f, :],
                                           start=(f == 0), stop=(f == DC - 1))
                ins.then_inc(made, 1)

        @block.vector
        def _(dve):
            for g in range(DC):
                dve.wait_ge(made, g + 1)
                nc.vector.tensor_copy(W["pT"][:, g, :], banks[g][:, 0:RPW])
    return W


def run_attention(nc, G, kind, W):
    with ExitStack() as stack:
        attention(nc, G, stack, kind(nc, G, W))


def load_experts(nc, G, stack, layer):
    t = G["t"]
    E = (8, 32)[layer]
    sb, _, _ = G["alloc"](stack, f"e{layer}")
    M = dict(layer=layer, E=E, up=sb("up", [P, DC, E, P]), down=sb("down", [P, E, D]), route=sb("route", [P, DC, E]))
    if layer == 0:
        M.update(b1=sb("b1", [P, E]), b2=sb("b2", [E, D]), rb=sb("rb", [P, E]))
        loads = [(M["up"][:, c, :, :], t["L0_ffn_W1"].rearrange("e (c p) f -> c p e f", p=P)[c]) for c in range(DC)]
        loads += [(M["down"][:], t["L0_ffn_W2"].rearrange("e f d -> f e d")),
                  (M["route"][:], t["L0_ffn_router_w"].rearrange("(c p) e -> p c e", p=P)),
                  (M["rb"][:], t["L0_ffn_router_b"].partition_broadcast(P)),
                  (M["b1"][:], t["b1T"]), (M["b2"][:], t["L0_ffn_b2"])]
    else:
        M.update(ln=sb("ln", [P, 2, DC]))
        loads = [(M["up"][:, c, :, :], t["L1_ffn_keys"].rearrange("e (c p) f -> c p e f", p=P)[c]) for c in range(DC)]
        loads += [(M["down"][:], t["L1_ffn_values"].rearrange("e f d -> f e d")),
                  (M["route"][:], t["L1_ffn_sel_w"].rearrange("(c p) e -> p c e", p=P))]
        loads += columns(M["ln"], t["L1_ffn_ln2_g"], t["L1_ffn_ln2_b"])
    load_all(nc, G, f"le{layer}", loads)
    return M


def columns(tile, gain, bias):
    return [(tile[:, i, c:c + 1], v.rearrange("(c p a) -> c p a", p=P, a=1)[c])
            for i, v in enumerate((gain, bias)) for c in range(DC)]


def load_all(nc, G, tag, loads, zero=(), slots=()):
    with ExitStack() as own:
        _, _, sem = G["alloc"](own, tag)
        by_sp, by_act, zeroed = sem("by_sp"), sem("by_act"), sem("zeroed")
        block = own.enter_context(nc.Block())

        @block.sync
        def _(sp):
            for dst, src in loads[0::2]:
                sp.dma_start(dst, src).then_inc(by_sp, 16)
            sp.wait_ge(by_sp, 16 * len(loads[0::2]))

        @block.gpsimd
        def _(pool):
            for tile in zero:
                pool.memset(tile[:], 0.0).then_inc(zeroed, 1)

        @block.scalar
        def _(act):
            for dst, src in loads[1::2]:
                act.dma_start(dst, src).then_inc(by_act, 16)
            if zero:
                act.wait_ge(zeroed, len(zero))
            for dst, src in slots:
                act.dma_start(dst, src).then_inc(by_act, 16)
            act.wait_ge(by_act, 16 * (len(loads[1::2]) + len(slots)))


def experts(nc, G, M):
    layer, E = M["layer"], M["E"]
    K = (2, 4)[layer]
    NB, X, const = G["NB"], G["X"], G["const"]
    SRC = (X, G.get("S2"))[layer]
    Q = 4
    NC = NB // Q
    with ExitStack() as stack:
        sb, psum, sem = G["alloc"](stack, f"m{layer}")
        names = (["xT0", "xT1", "route", "gates", "bias0", "bias1"], ["xT0", "xT1", "route0", "route1"])[layer]
        LA = len(names)
        ring = Ring([psum("ring0"), psum("ring1")], [sem("ring_full0"), sem("ring_full1")],
                    [sem("ring_free0"), sem("ring_free1")], LA, 0)
        hidden_bank = [psum("hidden_bank0"), psum("hidden_bank1")]
        out_bank = [psum(f"out{i}") for i in range(4)]
        stats, mv = sb("stats", [P, Q, 6]), sb("mv", [P, Q, 2])
        var, rstd = sb("var", [P, Q]), sb("rstd", [P, Q])
        xn = sb("xn", [P, Q, D])
        xT = [sb(f"xT{i}", [P, DC, Q * T]) for i in range(2)]
        hidden = [sb(f"hidden{i}", [P, Q * T]) for i in range(2)]
        score, score_in = sb("score", [P, Q, E]), sb("score_in", [P, Q, E])
        peak, total, tops, above = sb("peak", [P, Q]), sb("total", [P, Q]), sb("tops", [P, Q, 8]), sb("above", [P, Q])
        more, equal, run, again = sb("more", [P, Q, E]), sb("equal", [P, Q, E]), sb("run", [P, Q, E]), sb("again", [P, Q, E])
        gate = [sb(f"gate{i}", [P, Q, E]) for i in range(2)]
        gatesT = sb("gatesT", [P, Q * T])
        var_ready, rstd_ready, xn_ready = sem("var_ready"), sem("rstd_ready"), sem("xn_ready")
        logits_ready, score_ready, gate_ready = sem("logits_ready"), sem("score_ready"), sem("gate_ready")
        hidden_full, hidden_ready = sem("hidden_full"), sem("hidden_ready")
        out_full, added = sem("out_full"), sem("added")
        restart_set, chain_sem, once = sem("restart_set"), sem("chain"), sem("once")
        restart = sb("restart", [P, Q, E])
        block = stack.enter_context(nc.Block())

        at = ({0: ["stats"], 1: ["scale"], 2: ["xT0"], 3: ["xT1"], 4: ["route"], 6: ["gates"], 7: ["bias0", "bias1"]},
              {0: ["stats"], 2: ["scale"], 4: ["xT0"], 6: ["xT1"], 8: ["route0"], 9: ["route1"]})[layer]
        order = sum((at[s] for s in sorted(at)), [])

        def spot(name, c):
            j = names.index(name)
            return (j, 0) if isinstance(c, int) and c == 0 else (LA + j, c - 1)

        def first(c):
            return isinstance(c, int) and c == 0

        def last(c):
            return isinstance(c, int) and c == NC - 1

        def driver(eng, piece, work, chain=None):
            for name in order:
                piece(name, 0, 0)

            def body(c, par):
                for e in range(E):
                    work(c, par, e)
                    if not last(c):
                        for name in at.get(e, ()):
                            piece(name, c + 1, 1 - par)
            over(eng, NC, body, chain)

        @block.gpsimd
        def _(pool):
            pool.memset(restart[:], 1.0).then_inc(restart_set, 1)
            pool.wait_ge(restart_set, 1)
            pool.memset(restart[:, :, 0:1], 0.0).then_inc(restart_set, 1)

            def piece(name, c, par):
                if name == "stats":
                    pool.wait_ge(var_ready, c + 1)
                    nc.gpsimd.tensor_tensor(rstd[0:T, :], var[0:T, :], G["half"][0:T, 0:Q],
                                            ALU.pow).then_inc(rstd_ready, 1)
            driver(pool, piece, lambda c, par, e: None)

        @block.tensor
        def _(pe):
            def piece(name, c, par):
                if name in ("xT0", "xT1"):
                    f = int(name[2])
                    bank = ring.claim(pe, *spot(name, c))
                    pe.wait_ge(xn_ready, c + 1)
                    for i in range(Q):
                        ins = nc.tensor.transpose(bank[:, i * T:(i + 1) * T], xn[0:T, i, f * P:(f + 1) * P],
                                                  const("ident", T)[:, 0:T])
                    ring.filled(ins, spot(name, c)[0])
                elif name in ("route", "route0", "route1"):
                    which = range(Q) if name == "route" else range(2 * int(name[5]), 2 * int(name[5]) + 2)
                    bank = ring.claim(pe, *spot(name, c))
                    if name != "route1":
                        ring.emptied(pe, *spot("xT1", c))
                    for i in which:
                        for f in range(DC):
                            ins = nc.tensor.matmul(bank[0:T, (i - which[0]) * E:(i - which[0] + 1) * E],
                                                   xT[par][:, f, i * T:(i + 1) * T], M["route"][:, f, :],
                                                   start=(f == 0), stop=(f == DC - 1))
                    ring.filled(ins, spot(name, c)[0])
                elif name == "gates":
                    bank = ring.claim(pe, *spot(name, c))
                    pe.wait_ge(gate_ready, c + 1)
                    for i in range(Q):
                        ins = nc.tensor.transpose(bank[0:E, i * T:(i + 1) * T], gate[par][0:T, i, :],
                                                  const("ident", T)[:, 0:T])
                    ring.filled(ins, spot(name, c)[0])
                elif name in ("bias0", "bias1"):
                    bank = ring.claim(pe, *spot(name, c))
                    if name == "bias0":
                        ring.emptied(pe, *spot("gates", c))
                    for i in range(2):
                        j = 2 * int(name[4]) + i
                        ins = nc.tensor.matmul(bank[0:T, i * D:(i + 1) * D], gatesT[0:E, j * T:(j + 1) * T],
                                               M["b2"][:, :], start=True, stop=True)
                    ring.filled(ins, spot(name, c)[0])

            def up(c, par, e):
                n = c * E + e
                if e == 0:
                    ring.emptied(pe, *spot("xT0", c))
                    ring.emptied(pe, *spot("xT1", c))
                at_least(pe, hidden_ready, n - 1)
                for f in range(DC):
                    ins = nc.tensor.matmul(hidden_bank[e % 2][:, 0:Q * T], M["up"][:, f, e, :], xT[par][:, f, :],
                                           start=(f == 0), stop=(f == DC - 1))
                ins.then_inc(hidden_full, 1)

            def down(c, e):
                n = c * E + e
                pe.wait_ge(hidden_ready, n + 1)
                for i in range(Q):
                    if i % 2 == 0:
                        at_least(pe, added, (n - 2) * Q + i + 2)
                    ins = nc.tensor.matmul(out_bank[2 * (e % 2) + i // 2][0:T, (i % 2) * D:(i % 2 + 1) * D],
                                           hidden[e % 2][:, i * T:(i + 1) * T], M["down"][:, e, :],
                                           start=True, stop=True)
                    if i % 2:
                        ins.then_inc(out_full, 1)

            def work(c, par, e):
                if e == 0:
                    up(c, par, 0)
                if e + 1 < E:
                    up(c, par, e + 1)
                down(c, e)
            driver(pe, piece, work)

        @block.scalar
        def _(act):
            def piece(name, c, par):
                if name in ("xT0", "xT1"):
                    bank = ring.take(act, *spot(name, c))
                    f = int(name[2])
                    if layer == 0:
                        ins = nc.scalar.activation(xT[par][:, f, :], bank[:, 0:Q * T], ACT.Copy)
                    else:
                        ins = nc.scalar.activation(xT[par][:, f, :], bank[:, 0:Q * T], ACT.Identity,
                                                   bias=M["ln"][:, 1, f:f + 1], scale=M["ln"][:, 0, f:f + 1])
                    ring.freed(ins, spot(name, c)[0])
                elif name == "route":
                    act.wait_ge(logits_ready, c + 1)
                    nc.scalar.activation(score[0:T, :, :], score[0:T, :, :], ACT.Exp).then_inc(score_ready, 1)
                elif name in ("route0", "route1"):
                    bank = ring.take(act, *spot(name, c))
                    if name == "route0":
                        at_least(act, gate_ready, c)
                    i = 2 * int(name[5])
                    ring.freed(nc.scalar.activation(score[0:T, i:i + 2, :].rearrange("t q e -> t (q e)"),
                                                    bank[0:T, 0:2 * E], ACT.Sigmoid), spot(name, c)[0])
                elif name == "gates":
                    bank = ring.take(act, *spot(name, c))
                    ring.freed(nc.scalar.activation(gatesT[0:E, :], bank[0:E, 0:Q * T], ACT.Copy), spot(name, c)[0])

            def work(c, par, e):
                def hide(e):
                    n = c * E + e
                    act.wait_ge(hidden_full, n + 1)
                    at_least(act, out_full, 2 * (n - 1))
                    if layer == 0:
                        ins = nc.scalar.activation(hidden[e % 2][:, :], hidden_bank[e % 2][:, 0:Q * T], ACT.Gelu,
                                                   bias=M["b1"][:, e:e + 1])
                    else:
                        ins = nc.scalar.activation(hidden[e % 2][:, :], hidden_bank[e % 2][:, 0:Q * T], ACT.Relu)
                    ins.then_inc(hidden_ready, 1)
                if e == 0:
                    hide(0)
                if e + 1 < E:
                    hide(e + 1)
            driver(act, piece, work)

        @block.vector
        def _(dve):
            chain = Chain(dve, chain_sem, (15, 9)[layer], once=once)
            dve.wait_ge(restart_set, 2)

            def flat(a):
                return a[0:T, :, :].rearrange("t q e -> t (q e)")

            def choose(c, par, score=score):
                kth = tops[0:T, :, K - 1]
                for i in range(Q):
                    ins = nc.vector.max(tops[0:T, i, :], score[0:T, i, :])
                chain.link(ins)
                chain.link(nc.vector.tensor_tensor(more[0:T, :, :], score[0:T, :, :], bc(kth, 2, E), ALU.is_gt))
                chain.link(nc.vector.tensor_tensor(equal[0:T, :, :], score[0:T, :, :], bc(kth, 2, E), ALU.is_equal))
                chain.link(nc.vector.tensor_reduce(above[0:T, :], more[0:T, :, :], AX_X, ALU.add))
                chain.link(nc.vector.tensor_tensor_scan(flat(run), flat(restart), flat(equal), 0.0, ALU.mult, ALU.add))
                chain.link(nc.vector.tensor_tensor(run[0:T, :, :], run[0:T, :, :], bc(above[0:T, :], 2, E), ALU.add))
                chain.link(nc.vector.scalar_tensor_tensor(flat(again), flat(run), float(K), flat(equal),
                                                          ALU.is_le, ALU.mult))
                chain.link(nc.vector.tensor_tensor(more[0:T, :, :], more[0:T, :, :], again[0:T, :, :], ALU.add))

            def piece(name, c, par):
                if name == "stats":
                    for i in range(Q):
                        ins = nc.vector.bn_stats(stats[0:T, i, :], SRC[0:T, c * Q + i, :])
                    chain.link_apart(ins)
                    for i in range(Q):
                        ins = nc.vector.bn_aggr(mv[0:T, i, :], stats[0:T, i, :])
                    chain.link(ins)
                    nc.vector.tensor_scalar(var[0:T, :], mv[0:T, :, 1], EPS, None, ALU.add).then_inc(var_ready, 1)
                elif name == "scale":
                    dve.wait_ge(rstd_ready, c + 1)
                    for i in range(Q):
                        ins = nc.vector.tensor_scalar(xn[0:T, i, :], SRC[0:T, c * Q + i, :], mv[0:T, i, 0:1],
                                                      rstd[0:T, i:i + 1], ALU.subtract, ALU.mult)
                    ins.then_inc(xn_ready, 1)
                elif name == "route":
                    bank = ring.take(dve, *spot(name, c))
                    ring.freed(nc.vector.tensor_tensor(score[0:T, :, :],
                                                       bank[0:T, 0:Q * E].rearrange("t (q e) -> t q e", e=E),
                                                       bc(M["rb"][0:T, :], 1, Q), ALU.add), spot(name, c)[0])
                    ring.emptied(dve, *spot(name, c))
                    chain.link(nc.vector.tensor_reduce(peak[0:T, :], score[0:T, :, :], AX_X, ALU.max))
                    nc.vector.tensor_tensor(score[0:T, :, :], score[0:T, :, :], bc(peak[0:T, :], 2, E),
                                            ALU.subtract).then_inc(logits_ready, 1)
                    dve.wait_ge(score_ready, c + 1)
                    chain.link(nc.vector.tensor_reduce(total[0:T, :], score[0:T, :, :], AX_X, ALU.add))
                    chain.link(nc.vector.reciprocal(total[0:T, :], total[0:T, :]))
                    chain.link_apart(nc.vector.tensor_tensor(score[0:T, :, :], score[0:T, :, :],
                                                             bc(total[0:T, :], 2, E), ALU.mult))
                    choose(c, par)
                    g = gate[par]
                    chain.link(nc.vector.tensor_tensor(more[0:T, :, :], more[0:T, :, :], score[0:T, :, :], ALU.mult))
                    chain.link(nc.vector.tensor_reduce(total[0:T, :], more[0:T, :, :], AX_X, ALU.add))
                    chain.link(nc.vector.reciprocal(total[0:T, :], total[0:T, :]))
                    nc.vector.tensor_tensor(g[0:T, :, :], more[0:T, :, :], bc(total[0:T, :], 2, E),
                                            ALU.mult).then_inc(gate_ready, 1)
                elif name == "route1":
                    ring.emptied(dve, *spot("route0", c))
                    ring.emptied(dve, *spot("route1", c))
                    chain.link_apart(nc.vector.tensor_copy(score_in[0:T, :, :], score[0:T, :, :]))
                    choose(c, par, score_in)
                    nc.vector.tensor_tensor(gate[par][0:T, :, :], more[0:T, :, :], score[0:T, :, :],
                                            ALU.mult).then_inc(gate_ready, 1)
                elif name in ("bias0", "bias1"):
                    bank = ring.take(dve, *spot(name, c))
                    i = c * Q + 2 * int(name[4])
                    if isinstance(c, int):
                        view = X[0:T, i:i + 2, :]
                    else:
                        view = X[0:T, bass.ds(i, 2), :]
                    ring.freed(nc.vector.tensor_tensor(view, bank[0:T, :].rearrange("t (q d) -> t q d", q=2), view,
                                                       ALU.add), spot(name, c)[0])

            def work(c, par, e):
                n = c * E + e
                if e == 0:
                    dve.wait_ge(gate_ready, c + 1)
                    if layer == 0:
                        ring.emptied(dve, *spot("bias0", c))
                        ring.emptied(dve, *spot("bias1", c))
                for i in range(Q):
                    if i % 2 == 0:
                        dve.wait_ge(out_full, 2 * n + i // 2 + 1)
                    at_least(dve, added, n * Q + i - (Q - 1))
                    row = X[0:T, c * Q + i, :]
                    nc.vector.scalar_tensor_tensor(row, out_bank[2 * (e % 2) + i // 2][0:T, (i % 2) * D:(i % 2 + 1) * D],
                                                   gate[par][0:T, i, e:e + 1], row, ALU.mult,
                                                   ALU.add).then_inc(added, 1)
            driver(dve, piece, work, chain)


_TRANSPOSED = {"v_wT": "L0_attn_v_w", "o_wT": "L0_attn_o_w", "x_qT": "L1_xattn_Wq", "x_kT": "L1_xattn_Wk",
               "x_vT": "L1_xattn_Wv", "x_oT": "L1_xattn_Wo"}


def kernel(**inputs):
    import concourse.bacc as _bacc
    from concourse.bass_utils import run_bass_kernel_spmd as _run

    nc = _bacc.Bacc("TRN2", target_bir_lowering=False, num_devices=1)
    arrays, t = {}, {}

    def give(name, a):
        arrays[f"in_{name}"] = a
        t[name] = nc.dram_tensor(f"in_{name}", a.shape, mybir.dt.from_np(a.dtype), kind="ExternalInput").ap()

    taken = set(_TRANSPOSED.values()) | {"L0_attn_q_a", "L0_attn_k_a", "L0_ffn_b1", "mask_BxS2_bk1"}
    for name, a in inputs.items():
        if name not in taken:
            give(name, np.ascontiguousarray(a))
    for name, source in _TRANSPOSED.items():
        give(name, np.ascontiguousarray(np.asarray(inputs[source]).T))
    for n in "qk":
        give(f"{n}_aT", np.ascontiguousarray(np.asarray(inputs[f"L0_attn_{n}_a"]).transpose(0, 2, 1)))
    give("b1T", np.ascontiguousarray(np.asarray(inputs["L0_ffn_b1"]).T))
    give("mask", np.ascontiguousarray(inputs["mask_BxS2_bk1"]))
    give("constants", constants())
    x = inputs["x"]
    t["out"] = nc.dram_tensor("out", x.shape, F32, kind="ExternalOutput").ap()
    decoder(nc, t)
    r = _run(nc, [arrays], core_ids=[0])
    return r.results[0]["out"]
```

```python
from contextlib import ExitStack

import numpy as np

import concourse.bass as bass
from concourse import mybir

F32 = mybir.dt.float32
U8 = mybir.dt.uint8
ACT = mybir.ActivationFunctionType
ALU = mybir.AluOpType
AX_X = mybir.AxisListType.X

P = 128
T = 112
D = 256
DC = D // P
H = 16
HD = D // H
SLOT = 32
HS = P // SLOT
HG = H // HS
S2 = 375
CC = 3
CK = S2 // CC
XH, XD = 8, 64
XK = 488
XC = 4
XCK = XK // XC
RP = 2 * T - 1
RPW = RP + 1
EPS = 1e-5
BIG = 1.5e38

CONST = {}
_at = 0
for _name, _width in (("ident", P), ("mask8", 8), ("mask4", 4), ("keep0", T), ("keep1", T),
                      ("turnX", P), ("cosX", S2), ("sinX", S2), ("turnA", P), ("cosA", T), ("sinA", T),
                      ("pe", DC * RPW)):
    CONST[_name] = (_at, _width)
    _at += _width
CONST_W = _at


def constants():
    c = np.zeros((P, CONST_W), np.float32)

    def put(name, a):
        at, width = CONST[name]
        c[:a.shape[0], at:at + width] = a

    put("ident", np.eye(P, dtype=np.float32))
    put("mask8", np.kron(np.eye(8), np.ones((16, 1))))
    put("mask4", np.kron(np.eye(4), np.ones((32, 1))))
    causal = np.tril(np.ones((T, T), bool))
    put("keep0", np.where(causal, BIG, -BIG))
    put("keep1", np.where(causal, 80.0, -1e30))
    inv = (1.0 / np.float32(10000.0) ** (np.arange(0, HD, 2, dtype=np.float32) / np.float32(HD))).astype(np.float32)
    ang = (np.arange(S2, dtype=np.float32)[:, None] * inv[None, :]).astype(np.float32)
    put("cosX", np.tile(np.concatenate([np.cos(ang), np.cos(ang)], 1).T, (P // HD, 1)))
    put("sinX", np.tile(np.concatenate([np.sin(ang), np.sin(ang)], 1).T, (P // HD, 1)))
    turn = np.zeros((P, P))
    for h in range(P // HD):
        for d in range(HD // 2):
            turn[HD * h + d + 8, HD * h + d] = -1.0
            turn[HD * h + d, HD * h + d + 8] = 1.0
    put("turnX", turn)
    inv = (np.float32(10000.0) ** (-np.arange(0, 8, 2, dtype=np.float32) / np.float32(8))).astype(np.float32)
    ang = (np.arange(T, dtype=np.float32)[:, None] * inv[None, :]).astype(np.float32)
    cos, sin, turn = np.ones((P, T)), np.zeros((P, T)), np.zeros((P, P))
    for a in range(HS):
        for r in range(8):
            cos[SLOT * a + 16 + r] = np.cos(ang[:, r // 2])
            sin[SLOT * a + 16 + r] = np.sin(ang[:, r // 2])
        for r in range(0, 8, 2):
            turn[SLOT * a + 17 + r, SLOT * a + 16 + r] = -1.0
            turn[SLOT * a + 16 + r, SLOT * a + 17 + r] = 1.0
    put("cosA", cos)
    put("sinA", sin)
    put("turnA", turn)
    pos = np.arange(-(T - 1), T, dtype=np.float32)
    inv = (1.0 / np.float32(10000.0) ** (np.arange(0, D, 2, dtype=np.float32) / np.float32(D))).astype(np.float32)
    ang = (pos[None, :] * inv[:, None]).astype(np.float32)
    pe = np.zeros((P, DC, RPW))
    pe[:, 0, :RP] = np.sin(ang)
    pe[:, 1, :RP] = np.cos(ang)
    put("pe", pe.reshape(P, -1))
    return c


def bc(ap, axis, n):
    v = ap.unsqueeze(axis)
    shape = list(v.shape)
    shape[axis] = n
    return v.to_broadcast(shape)


class Chain:

    def __init__(self, eng, sem, once=None):
        self.eng, self.sem, self.once = eng, sem, once
        self.base = self.n = self.k = 0

    def start(self, b):
        if isinstance(b, int):
            self.base = self.n
        else:
            self.base = self.loop + (b - self.first) * self.per
        self.k = 0

    def enter(self, first=1):
        self.loop, self.first, self.per = self.n, first, self.k

    def leave(self, bodies):
        self.n = self.loop + bodies * self.per

    def inc(self, ins):
        ins.then_inc(self.sem, 1)
        self.k += 1
        self.n += 1
        return self.base + self.k

    def link(self, ins):
        self.eng.wait_ge(self.sem, self.inc(ins))

    def link_apart(self, ins):
        ins.then_inc(self.once, 1)
        self.eng.wait_ge(self.once, 1)
        self.eng.sem_clear(self.once)


def over(eng, n, body, chain=None):
    if chain:
        chain.start(0)
    body(0, 0)
    if chain:
        chain.enter()
    with eng.Fori(0, (n - 2) // 2) as it:
        for k in (0, 1):
            b = it * 2 + (1 + k)
            if chain:
                chain.start(b)
            body(b, (1 + k) % 2)
            if chain:
                assert chain.k == chain.per, (chain.k, chain.per)
    if chain:
        chain.leave(n - 2)
        chain.start(n - 1)
    body(n - 1, (n - 1) % 2)


def at_least(eng, sem, n):
    if not isinstance(n, int) or n > 0:
        eng.wait_ge(sem, n)


class Ring:

    def __init__(self, banks, full, free, n):
        assert n % 2 == 0
        self.banks, self.full, self.free, self.n = banks, full, free, n

    def count(self, c, e):
        return c // 2 + e * (self.n // 2)

    def claim(self, pe, c, e):
        at_least(pe, self.free[c % 2], self.count(c, e))
        return self.banks[c % 2]

    def filled(self, ins, c):
        ins.then_inc(self.full[c % 2], 1)

    def skip(self, pe, c, e):
        self.claim(pe, c, e)
        pe.sem_inc(self.full[c % 2], 1)
        pe.sem_inc(self.free[c % 2], 1)

    def take(self, eng, c, e):
        eng.wait_ge(self.full[c % 2], self.count(c, e) + 1)
        return self.banks[c % 2]

    def freed(self, ins, c):
        ins.then_inc(self.free[c % 2], 1)

    def emptied(self, eng, c, e):
        eng.wait_ge(self.free[c % 2], self.count(c, e) + 1)


def decoder(nc, t):
    NB = t["x"].shape[0]
    whole = ExitStack()
    with whole:
        def allocators(stack, tag):
            def sb(name, shape, dt=F32):
                return stack.enter_context(nc.sbuf_tensor(f"{tag}_{name}", shape, dt))

            def psum(name, shape=(P, 512)):
                return stack.enter_context(nc.psum_tensor(f"{tag}_{name}", list(shape), F32))

            sems = []

            def release():
                if sems:
                    nc.clear_and_free_semaphores(sems)
                    nc.all_engine_barrier()

            stack.callback(release)

            def sem(name):
                sems.append(nc.alloc_semaphore(f"{tag}_{name}"))
                return sems[-1]
            return sb, psum, sem

        sb, _, _ = allocators(whole, "g")
        X = sb("residual", [P, NB, D])
        C = sb("constants", [P, CONST_W])
        half = sb("minus_half", [P, 4])

        def const(name, parts=P):
            at, width = CONST[name]
            return C[0:parts, at:at + width]

        G = dict(NB=NB, X=X, constants=C, const=const, half=half, alloc=allocators, t=t)

        with ExitStack() as layer1:
            W1, ahead = layer1_weights(nc, G, layer1)
            with ExitStack() as ffn:
                M, first = expert_weights(nc, G, ffn, 0)
                with ExitStack() as layer0:
                    W = load_layer0(nc, G, layer0, [first, ahead])
                    run_attention(nc, G, CausalAttention, W)
                    run_attention(nc, G, LatentAttention, W)
                experts(nc, G, M)
            finish_layer1(nc, G, W1, ahead)
            run_attention(nc, G, RotaryAttention, W1)
            run_attention(nc, G, ContextAttention, W1)
            G["S2"] = allocators(layer1, "l1")[0]("stream2", [P, NB, D])
            run_attention(nc, G, RelativeAttention, W1)
            experts(nc, G, expert_weights(nc, G, layer1, 1)[0])


def rows_in_slots(w):
    return w.rearrange("(g a d) n -> a d g n", g=HG, a=HS)


def load_layer0(nc, G, stack, background):
    t, NB = G["t"], G["NB"]
    sb, _, sem = G["alloc"](stack, "w0")
    W = dict(wq=sb("wq", [P, DC, D]), wk=sb("wk", [P, DC, D]), wv=sb("wv", [P, DC, D]),
             wo=sb("wo", [P, HG, D]), vb=sb("vb", [P, D]),
             xq=sb("xq", [P, DC, 512]), xkv=sb("xkv", [P, DC, 1024]), xo=sb("xo", [P, 4, D]),
             lnx=sb("lnx", [P, 2, DC]), lnl=sb("lnl", [P, 2, DC]), lno=sb("lno", [P, 2, D]))
    cross = [(W[key][:], t[f"L0_xattn_{name}"].rearrange("(c p) n -> p c n", p=P))
             for key, name in (("xq", "Wq"), ("xkv", "Wkv"), ("xo", "Wo"))]
    cross += columns(W["lnx"], t["L0_xattn_ln_x_g"], t["L0_xattn_ln_x_b"])
    cross += columns(W["lnl"], t["L0_xattn_ln_l_g"], t["L0_xattn_ln_l_b"])
    cross += [(W["lno"][:, i, :], t[f"L0_xattn_ln_o_{gb}"].partition_broadcast(P)) for i, gb in enumerate("gb")]
    W["cross"] = dict(loads=cross, zero=[], loaded=sem("cross_loaded"))
    background = W["background"] = [W["cross"]] + background
    with ExitStack() as own:
        sbt, psum, sem = G["alloc"](own, "p0")
        low = {n: (sbt(f"{n}a", [P, H // 2, D]), sbt(f"{n}b", [P, H // 2, 2 * HD])) for n in ("q", "k")}
        bank = [psum(f"bank{i}") for i in range(4)]
        zeroed, loaded, folded, copied = sem("zeroed"), sem("loaded"), sem("folded"), sem("copied")
        small, low_zeroed = sem("small"), sem("low_zeroed")
        block = own.enter_context(nc.Block())

        @block.sync
        def _(sp):
            for n in ("q", "k"):
                sp.dma_start(low[n][0][:], t[f"{n}_aT"].rearrange("(g i) r d -> (i r) g d", i=2)).then_inc(loaded, 16)
            sp.wait_ge(low_zeroed, 2)
            for n in ("q", "k"):
                for i in range(2):
                    sp.dma_start(low[n][1][64 * i:64 * (i + 1), :, HD * i:HD * (i + 1)],
                                 t[f"L0_attn_{n}_b"].rearrange("(g i) r d -> i r g d", i=2)[i]).then_inc(loaded, 16)
            q = NB // 4
            for i in range(4):
                sp.dma_start(G["X"][0:T, i * q:(i + 1) * q, :],
                             t["x"].rearrange("b t d -> t b d")[:, i * q:(i + 1) * q, :]).then_inc(small, 16)
            sp.wait_ge(small, 64)

        @block.scalar
        def _(act):
            loads = [(G["constants"][:], t["constants"]),
                     (W["wv"][:], t["v_wT"].rearrange("(c p) n -> p c n", p=P)),
                     (W["vb"][:], t["L0_attn_v_b"].partition_broadcast(P))]
            for dst, src in loads:
                act.dma_start(dst, src).then_inc(copied, 16)
            n = 16 * len(loads)
            act.wait_ge(zeroed, 1)
            for a in range(HS):
                act.dma_start(W["wo"][SLOT * a:SLOT * a + HD, :, :], rows_in_slots(t["o_wT"])[a]).then_inc(copied, 16)
                n += 16
            act.dma_start(W["wo"][HD:HD + 1, 0, :], t["L0_attn_o_b"].rearrange("(a n) -> a n", a=1)).then_inc(copied, 16)
            n += 16
            act.wait_ge(copied, n)

        @block.gpsimd
        def _(pool):
            for n in ("q", "k"):
                pool.memset(low[n][1][:], 0.0).then_inc(low_zeroed, 1)
            pool.memset(W["wo"][:], 0.0).then_inc(zeroed, 1)
            pool.memset(G["half"][:], -0.5).then_inc(zeroed, 1)
            for later in background:
                for tile in later["zero"]:
                    pool.memset(tile[:], 0.0).then_inc(later["zeroed"], 1)
            pool.wait_ge(zeroed, 2)

        @block.tensor
        def _(pe):
            pe.wait_ge(loaded, 96)
            for i, n in enumerate("qk"):
                for c in range(DC):
                    for g in range(H // 2):
                        last = nc.tensor.matmul(bank[2 * i + c][:, g * 2 * HD:(g + 1) * 2 * HD],
                                                low[n][0][:, g, c * P:(c + 1) * P], low[n][1][:, g, :],
                                                start=True, stop=True)
                    last.then_inc(folded, 1)

        @block.vector
        def _(dve):
            for i, n in enumerate("qk"):
                for c in range(DC):
                    dve.wait_ge(folded, 2 * i + c + 1)
                    nc.vector.tensor_copy(W["w" + n][:, c, :], bank[2 * i + c][:, 0:D])
    return W


class Plan:
    NORMALISE, PREPARE, ATTEND, FINISH = range(4)
    BANKLESS = ("stats", "again", "scale")

    def __init__(self, units, normalise, steps, late=()):
        self.units, self.steps = units, steps
        names = [name for s in range(units) for name in steps.get(s, ())]
        self.age = {name: self.NORMALISE if name in normalise or name in self.BANKLESS else
                    self.FINISH + (name in late) if name in ("spread", "project") else self.PREPARE for name in names}
        self.order = [name for name in names if name not in self.BANKLESS]
        self.n = len(self.order)
        assert self.n % 2 == 0, self.n

    def spot_of(self, name, b):
        return self.order.index(name), b + self.age[name]


AHEAD = 4
BEHIND = 4


def frames(eng, NB, body, chain=None):
    def run(e, k):
        if chain:
            chain.start(e)
        body(e, k % 2)

    for e in range(AHEAD):
        run(e, e)
    if NB > AHEAD:
        if chain:
            chain.enter(AHEAD)
        with eng.Fori(0, (NB - AHEAD) // 2) as it:
            for k in (0, 1):
                run(it * 2 + (AHEAD + k), k)
        if chain:
            chain.leave(NB - AHEAD)
    for e in range(NB, NB + BEHIND):
        run(e, e)


def attention(nc, G, stack, cfg):
    NB, const = G["NB"], G["const"]
    plan = cfg.plan
    U = plan.units
    sb, psum, sem = G["alloc"](stack, cfg.tag)
    scores = [psum("scores0"), psum("scores1")]
    flipped = [psum("flipped0"), psum("flipped1")]
    heads_out = cfg.heads_out = [psum("heads_out0"), psum("heads_out1")]
    ring = cfg.ring = Ring([psum("ring0"), psum("ring1")], [sem("ring_full0"), sem("ring_full1")],
                           [sem("ring_free0"), sem("ring_free1")], plan.n)
    width, ck, nt, nh = cfg.width, cfg.ck, cfg.nt, cfg.heads
    wk = width // nh
    bounded = [sb("bounded0", [P, width]), sb("bounded1", [P, width])]
    top, minus_top = sb("top", [P, 2, nh]), sb("minus_top", [P, 2, nh])
    probs = [sb("probs0", [P, width]), sb("probs1", [P, width])]
    together = cfg.together
    NT = 2 * together
    probsT = [sb(f"probsT{i}", [P, nt * T]) for i in range(NT)]
    sums = [sb("sums0", [P, U * nh]), sb("sums1", [P, U * nh])]
    inverse = sb("inverse", [P, U * nh])
    inverse_wide = cfg.inverse_wide = sb("inverse_wide", [P, 4 * P])
    cfg.inverse_rows, cfg.normed = sb("inverse_rows", [P, 4 * T]), sb("normed", [P, 4 * T])

    scored, scores_free, maxed, tops_ready = sem("scored"), sem("scores_free"), sem("maxed"), sem("tops_ready")
    exped, turned, copied, valued = sem("exped"), sem("turned"), sem("copied"), sem("valued")
    inverse_ready = sem("inverse_ready")
    dve_chain, dve_once, pool_chain = sem("dve_chain"), sem("dve_once"), sem("pool_chain")
    wide_ready = sem("wide_ready")
    cfg.normed_ready = sem("normed_ready")
    cfg.scores_free, cfg.valued, cfg.wide_ready = scores_free, valued, wide_ready
    cfg.allocate(sb, sem)
    block = stack.enter_context(nc.Block())

    def missing(b):
        return isinstance(b, int) and not 0 <= b < NB

    def unit(e, s, lag):
        b, u = (e - 2, s - lag) if s >= lag else (e - 3, s - lag + U)
        return None if missing(b) else (b, u, b * U + u)

    def pieces(part, e, par, s, *more, skip=None):
        for name in plan.steps.get(s, ()):
            age = plan.age[name]
            b = e - age
            c = None if name in plan.BANKLESS else plan.order.index(name)
            if not missing(b):
                part(name, b, (par + age) % 2, c, e, *more)
            elif skip and c is not None:
                skip(c, e)

    @block.sync
    def _(sp):
        cfg.sync(sp)

    @block.gpsimd
    def _(pool):
        chain = Chain(pool, pool_chain)
        cfg.pool_start(pool, chain)

        def body(e, par):
            for s in range(U):
                pieces(lambda name, b, par, c, e: cfg.pool(pool, name, b, par, chain), e, par, s)
        frames(pool, NB, body)

    @block.tensor
    def _(pe):
        cfg.pe_start(pe)

        def body(e, par):
            for s in range(U):
                if unit(e, s, 0):
                    b, u, n = unit(e, s, 0)
                    at_least(pe, scores_free if cfg.bounds else exped, n - 1)
                    cfg.pe_scores(pe, b, u, par, scores[u % 2]).then_inc(scored, 1)
                if unit(e, s, 2):
                    b, u, n = unit(e, s, 2)
                    pe.wait_ge(exped, n + 1)
                    at_least(pe, copied, n - 1)
                    for i in range(nt):
                        ins = nc.tensor.transpose(flipped[u % 2][0:ck, i * T:(i + 1) * T],
                                                  probs[u % 2][0:T, i * ck:(i + 1) * ck], const("ident", T)[:, 0:T])
                    ins.then_inc(turned, 1)
                if unit(e, s, 3) and (s - 2) % together == 0:
                    b, u, n = unit(e, s, 3)
                    vpar = par if s >= 3 else 1 - par
                    pe.wait_ge(copied, n + 1)
                    if u == together - 1:
                        at_least(pe, cfg.normed_ready, b - 1)
                    for v in range(u - together + 1, u + 1):
                        ins = cfg.pe_values(pe, b, v, vpar, probsT[v % NT], heads_out[vpar])
                    ins.then_inc(valued, together)
                pieces(lambda name, b, par, c, e: c is None or cfg.pe(pe, name, b, par, c, e), e, par, s,
                       skip=lambda c, e: ring.skip(pe, c, e))
        frames(pe, NB, body)

    @block.scalar
    def _(act):
        cfg.act_start(act)

        def body(e, par):
            for s in range(U):
                if unit(e, s, 2):
                    b, u, n = unit(e, s, 2)
                    act.wait_ge(turned, n + 1)
                    at_least(act, valued, n - NT + 1)
                    nc.scalar.activation(probsT[u % NT][0:ck, :], flipped[u % 2][0:ck, 0:nt * T],
                                         ACT.Copy).then_inc(copied, 1)
                if unit(e, s, cfg.exp_lag):
                    b, u, n = unit(e, s, cfg.exp_lag)
                    spar = par if s >= cfg.exp_lag else 1 - par
                    act.wait_ge(tops_ready, n + 1)
                    at_least(act, turned, n - 1)
                    if u == 0:
                        at_least(act, inverse_ready, b - 1)
                    src = bounded[u % 2] if cfg.bounds else scores[u % 2]
                    for h in range(nh):
                        cols = slice(h * wk, (h + 1) * wk)
                        ins = nc.scalar.activation(probs[u % 2][0:T, cols], src[0:T, cols], ACT.Exp, scale=cfg.scale,
                                                   bias=minus_top[0:T, u % 2, h:h + 1],
                                                   accum_out=sums[spar][0:T, u * nh + h:u * nh + h + 1])
                    ins.then_inc(exped, 1)
                if s == 2 and not missing(e - 3):
                    act.wait_ge(inverse_ready, e - 3 + 1)
                    cfg.reuse(act, "spread", e - 3)
                    nc.scalar.activation(inverse_wide[0:T, :].rearrange("t (h r) -> t h r", h=U * nh),
                                         bc(inverse[0:T, :], 2, 4 * P // (U * nh)), ACT.Copy).then_inc(wide_ready, 1)
                pieces(lambda name, b, par, c, e: cfg.end_act(act, name, b, c, e) if name in ("spread", "project")
                       else cfg.act(act, name, b, par, c, e), e, par, s)
        frames(act, NB, body)

    @block.vector
    def _(dve):
        chain = Chain(dve, dve_chain, once=dve_once)
        cfg.dve_start(dve, chain)

        def body(e, par):
            for s in range(U):
                if unit(e, s, 0):
                    b, u, n = unit(e, s, 0)
                    hold = bounded[u % 2][0:T, :].rearrange("p (h k) -> p h k", h=nh)
                    bank = scores[u % 2][0:T, 0:width].rearrange("p (h k) -> p h k", h=nh)
                    dve.wait_ge(scored, n + 1)
                    if cfg.bounds:
                        at_least(dve, exped, n - 1)
                        cfg.dve_bound(dve, u, par, b, hold, bank).then_inc(scores_free, 1)
                        dve.wait_ge(scores_free, n + 1)
                    nc.vector.tensor_reduce(top[0:T, u % 2, :], hold if cfg.bounds else bank, AX_X,
                                            ALU.max).then_inc(maxed, 1)
                    dve.wait_ge(maxed, n + 1)
                    if not cfg.bounds:
                        at_least(dve, exped, n - 1)
                    nc.vector.tensor_scalar(minus_top[0:T, u % 2, :], top[0:T, u % 2, :], -cfg.scale, None,
                                            ALU.mult).then_inc(tops_ready, 1)
                if s == 1 and not missing(e - 3):
                    b = e - 3
                    dve.wait_ge(exped, (b + 1) * U)
                    nc.vector.reciprocal(inverse[0:T, :], sums[1 - par][0:T, :]).then_inc(inverse_ready, 1)
                pieces(lambda *a: cfg.dve(dve, *a), e, par, s, chain)
        frames(dve, NB, body, chain)


class Norm:

    def __init__(self, sb, sem, tag):
        self.stats, self.mv = sb(f"stats{tag}", [P, 6]), sb(f"mv{tag}", [P, 2])
        self.var, self.rstd = sb(f"var{tag}", [P, 1]), sb(f"rstd{tag}", [P, 1])
        self.var_ready, self.rstd_ready = sem(f"var_ready{tag}"), sem(f"rstd_ready{tag}")


class Phase:
    pairs = False
    bounds = True
    scale = 1.0
    together = 1
    exp_lag = 1

    def __init__(self, nc, G, W):
        self.nc, self.G, self.W = nc, G, W
        self.X, self.const = G["X"], G["const"]
        self.NB = G["NB"]

    def sync(self, sp):
        pass

    def pool_start(self, pool, chain):
        pass

    def dve_start(self, dve, chain):
        pass

    def act_start(self, act):
        pass

    def pe_start(self, pe):
        pass

    def allocate_norm(self, sb, sem, tag=""):
        return Norm(sb, sem, tag)

    def norm_stats(self, n, src, chain):
        nc = self.nc
        chain.link_apart(nc.vector.bn_stats(n.stats[0:T, :], src))
        chain.link(nc.vector.bn_aggr(n.mv[0:T, :], n.stats[0:T, :]))
        nc.vector.tensor_scalar(n.var[0:T, :], n.mv[0:T, 1:2], EPS, None, ALU.add).then_inc(n.var_ready, 1)

    def norm_power(self, pool, n, b):
        pool.wait_ge(n.var_ready, b + 1)
        self.nc.gpsimd.tensor_tensor(n.rstd[0:T, :], n.var[0:T, :], self.G["half"][0:T, 0:1],
                                     ALU.pow).then_inc(n.rstd_ready, 1)

    def norm_scale(self, dve, n, b, dst, src):
        dve.wait_ge(n.rstd_ready, b + 1)
        return self.nc.vector.tensor_scalar(dst, src, n.mv[0:T, 0:1], n.rstd[0:T, :], ALU.subtract, ALU.mult)

    def end_pe(self, pe, name, b, par, c, e, wo):
        nc, ring = self.nc, self.ring
        bank = ring.claim(pe, c, e)
        if name == "spread":
            pe.wait_ge(self.wide_ready, b + 1)
            for g in range(4):
                ins = nc.tensor.transpose(bank[:, g * T:(g + 1) * T], self.inverse_wide[0:T, g * P:(g + 1) * P],
                                          self.const("ident", T)[:, 0:T])
        else:
            pe.wait_ge(self.normed_ready, b + 1)
            for g in range(4):
                ins = nc.tensor.matmul(bank[0:T, 0:D], self.normed[:, g * T:(g + 1) * T], wo[:, g, :],
                                       start=(g == 0), stop=(g == 3))
        ring.filled(ins, c)

    def end_act(self, act, name, b, c, e):
        if name == "spread":
            at_least(act, self.normed_ready, b)
            self.copy_out(act, c, e, self.inverse_rows[:, :], lambda bank: bank[:, 0:4 * T])

    def end_dve(self, dve, name, b, par, c, e):
        nc, ring = self.nc, self.ring
        if name == "spread":
            ring.emptied(dve, c, e)
            dve.wait_ge(self.valued, (b + 1) * self.plan.units)
            nc.vector.tensor_tensor(self.normed[:, :], self.heads_out[par][:, 0:4 * T], self.inverse_rows[:, :],
                                    ALU.mult).then_inc(self.normed_ready, 1)
        elif name == "project":
            bank = ring.take(dve, c, e)
            ring.freed(nc.vector.tensor_tensor(self.X[0:T, b, :], bank[0:T, 0:D], self.X[0:T, b, :], ALU.add), c)

    def reuse(self, eng, name, b):
        if not isinstance(b, int) or b > 0:
            self.ready(eng, name, b - 1)

    def widen(self, dst, src, mask, groups, heads, width):
        return self.nc.vector.tensor_tensor(
            dst, bc(src.rearrange("p (g t) -> p g t", g=groups), 2, heads),
            bc(bc(mask, 1, groups), 3, width), ALU.mult)

    def ready(self, eng, name, b, claimed=None):
        c, body = self.plan.spot_of(name, b)
        if claimed is None or (claimed - c) % 2:
            self.ring.emptied(eng, c, body)

    def pe_values(self, pe, b, u, par, probs, out):
        if u == 0:
            self.ready(pe, "v", b)
        for a in range(HS):
            h = HS * u + a
            ins = self.nc.tensor.matmul(out[SLOT * a:SLOT * (a + 1), u * T:(u + 1) * T], self.v[par][0:T, h, :],
                                        probs[0:T, a * T:(a + 1) * T], start=True, stop=True)
        return ins

    def pe_transpose(self, pe, name, b, c, body, src, ready, n):
        bank = self.ring.claim(pe, c, body)
        pe.wait_ge(ready, n)
        for f in range(DC):
            ins = self.nc.tensor.transpose(bank[:, f * T:(f + 1) * T], src[0:T, f * P:(f + 1) * P],
                                           self.const("ident", T)[:, 0:T])
        self.ring.filled(ins, c)

    def pe_columns(self, pe, c, body, w, xT, b, wait):
        bank = self.ring.claim(pe, c, body)
        if wait:
            self.ready(pe, wait, b, c)
        for g in range(DC):
            for f in range(DC):
                ins = self.nc.tensor.matmul(bank[:, g * T:(g + 1) * T], w[:, f, g * P:(g + 1) * P], xT[:, f, :],
                                            start=(f == 0), stop=(f == DC - 1))
        self.ring.filled(ins, c)

    def pe_rows(self, pe, c, body, xT, w, rows):
        bank = self.ring.claim(pe, c, body)
        for f in range(DC):
            ins = self.nc.tensor.matmul(bank[0:rows, 0:w.shape[2]], xT[:, f, :], w[:, f, :],
                                        start=(f == 0), stop=(f == DC - 1))
        self.ring.filled(ins, c)

    def copy_out(self, act, c, body, dst, src_of):
        bank = self.ring.take(act, c, body)
        self.ring.freed(self.nc.scalar.activation(dst, src_of(bank), ACT.Copy), c)


class CausalAttention(Phase):
    tag = "a0"
    width, ck, nt, heads = HS * T, T, HS, HS
    scale = HD ** -0.5

    def __init__(self, nc, G, W):
        super().__init__(nc, G, W)
        self.plan = Plan(4, ["xT"], {0: ["q"], 1: ["stats", "scale", "k"], 2: ["v", "project"], 3: ["spread", "xT"]},
                         late=["project"])

    def allocate(self, sb, sem):
        self.norm = self.allocate_norm(sb, sem)
        self.xn, self.xT = sb("xn", [P, D]), sb("xT", [P, DC, T])
        self.q = [sb(f"q{i}", [P, DC, 8, T]) for i in range(2)]
        self.k = [sb(f"k{i}", [P, DC, T]) for i in range(2)]
        self.v = [sb(f"v{i}", [P, H, SLOT]) for i in range(2)]
        self.xn_ready = sem("xn_ready")

    def sync(self, sp):
        for later in self.W["background"]:
            if later["zero"]:
                sp.wait_ge(later["zeroed"], len(later["zero"]))
            for dst, src in later["loads"]:
                sp.dma_start(dst, src).then_inc(later["loaded"], 16)

    def dve_start(self, dve, chain):
        for i in range(2):
            chain.link(self.nc.vector.memset(self.v[i][:], 1.0))

    def pool(self, pool, name, b, par, chain):
        if name == "stats":
            self.norm_power(pool, self.norm, b)

    def pe(self, pe, name, b, par, c, body):
        W = self.W
        if name == "xT":
            self.pe_transpose(pe, name, b, c, body, self.xn, self.xn_ready, b + 1)
        elif name in ("q", "k"):
            self.pe_columns(pe, c, body, W["w" + name], self.xT, b, "xT")
        elif name == "v":
            self.pe_rows(pe, c, body, self.xT, W["wv"], T)
        else:
            self.end_pe(pe, name, b, par, c, body, W["wo"])

    def pe_scores(self, pe, b, u, par, bank):
        if u == 0:
            self.ready(pe, "q", b)
            self.ready(pe, "k", b)
        for a in range(HS):
            h = HS * u + a
            ins = self.nc.tensor.matmul(bank[0:T, a * T:(a + 1) * T], self.q[par][:, h // 8, h % 8, :],
                                        self.k[par][:, h // 8, :], start=True, stop=True)
        return ins

    def act(self, act, name, b, par, c, body):
        if name == "xT":
            self.copy_out(act, c, body, self.xT[:].rearrange("p f t -> p (f t)"), lambda bank: bank[:, 0:DC * T])
        elif name == "k":
            self.copy_out(act, c, body, self.k[par][:].rearrange("p f t -> p (f t)"), lambda bank: bank[:, 0:DC * T])

    def dve_bound(self, dve, u, par, b, hold, bank):
        return self.nc.vector.scalar_tensor_tensor(hold, bank, -BIG, bc(self.const("keep0", T), 1, HS),
                                                   ALU.max, ALU.min)

    def dve(self, dve, name, b, par, c, body, chain):
        nc, ring, X = self.nc, self.ring, self.X
        if name == "stats":
            self.norm_stats(self.norm, X[0:T, b, :], chain)
        elif name == "scale":
            self.reuse(dve, "xT", b)
            self.norm_scale(dve, self.norm, b, self.xn[0:T, :], X[0:T, b, :]).then_inc(self.xn_ready, 1)
        elif name == "q":
            bank = ring.take(dve, c, body)
            ring.freed(self.widen(self.q[par][:], bank[:, 0:DC * T], self.const("mask8"), DC, 8, T), c)
        elif name == "v":
            bank = ring.take(dve, c, body)
            ring.freed(nc.vector.tensor_tensor(self.v[par][0:T, :, 0:HD],
                                               bank[0:T, 0:D].rearrange("t (h d) -> t h d", h=H),
                                               self.W["vb"][0:T, :].rearrange("t (h d) -> t h d", h=H), ALU.add), c)
        else:
            self.end_dve(dve, name, b, par, c, body)


class LatentAttention(Phase):
    tag = "x0"
    pairs = True
    width, ck, nt, heads = XK, XCK, XC, 1
    scale = XD ** -0.5 * XD ** -0.5

    def __init__(self, nc, G, W):
        super().__init__(nc, G, W)
        self.plan = Plan(XH, ["ctx0", "ctx1", "lat"],
                         {0: ["stats", "q"], 1: ["again", "k0"], 2: ["k1"], 3: ["scale", "k2", "spread"],
                          4: ["k3", "v0"], 5: ["project", "v1"], 6: ["v2", "v3"], 7: ["lat", "ctx0", "ctx1"]})

    def allocate(self, sb, sem):
        self.norm, self.norm2 = self.allocate_norm(sb, sem), self.allocate_norm(sb, sem, "2")
        self.out_norm = self.allocate_norm(sb, sem, "3")
        self.cstats, self.cmv = sb("cstats", [P, CC, 6]), sb("cmv", [P, CC, 2])
        self.cvar, self.crstd = sb("cvar", [P, CC]), sb("crstd", [P, CC])
        self.cvar_ready, self.crstd_ready = sem("cvar_ready"), sem("crstd_ready")
        self.ctx = [sb(f"ctx{i}", [P, CC, D]) for i in range(2)]
        self.ctx_loaded = [sem(f"ctx_loaded{i}") for i in range(2)]
        self.mask = [sb(f"mask{i}", [P, S2], U8) for i in range(2)]
        self.mask_loaded = [sem(f"mask_loaded{i}") for i in range(2)]
        self.keep = [sb(f"keep{i}", [P, XK]) for i in range(2)]
        self.xn, self.ctx_n = sb("xn", [P, D]), sb("ctx_n", [P, CC, D])
        self.kv = sb("kv", [P, DC, XK])
        self.q = [sb(f"q{i}", [P, 4, 2, T]) for i in range(2)]
        self.k = [sb(f"k{i}", [P, 4, XK]) for i in range(2)]
        self.v = [sb(f"v{i}", [P, XC, XH * XD]) for i in range(2)]
        self.out2 = sb("out2", [P, D])
        self.xn_ready, self.ctx_ready = sem("xn_ready"), sem("ctx_ready")
        self.mask_used, self.set_up = sem("mask_used"), sem("set_up")

    def sync(self, sp):
        def used(before):
            sp.wait_ge(self.ctx_ready, before + 1)
            sp.wait_ge(self.mask_used, before + 1)
        load_context(self, sp, used, self.G["t"]["mask"])

    def pool_start(self, pool, chain):
        for i in range(2):
            pool.memset(self.keep[i][:, S2:XK - 1], BIG).then_inc(self.set_up, 1)
            pool.memset(self.keep[i][:, XK - 1:XK], -BIG).then_inc(self.set_up, 1)
            pool.memset(self.q[i][:], 0.0).then_inc(self.set_up, 1)
        pool.memset(self.kv[:, :, XK - 1:XK], 0.0).then_inc(self.set_up, 1)

    def pool(self, pool, name, b, par, chain):
        if name == "stats":
            self.norm_power(pool, self.norm, b)
            pool.wait_ge(self.cvar_ready, b + 1)
            self.nc.gpsimd.tensor_tensor(self.crstd[0:CK, :], self.cvar[0:CK, :], self.G["half"][0:CK, 0:CC],
                                         ALU.pow).then_inc(self.crstd_ready, 1)
        elif name == "again":
            self.norm_power(pool, self.norm2, b)
        elif name == "project":
            self.norm_power(pool, self.out_norm, b)

    def pe(self, pe, name, b, par, c, body):
        nc, ring, W = self.nc, self.ring, self.W
        if name in ("ctx0", "ctx1"):
            f = int(name[3])
            bank = ring.claim(pe, c, body)
            pe.wait_ge(self.ctx_ready, b + 1)
            for i in range(CC):
                ins = nc.tensor.transpose(bank[:, i * CK:(i + 1) * CK], self.ctx_n[0:CK, i, f * P:(f + 1) * P],
                                          self.const("ident", CK)[:, 0:CK])
            ring.filled(ins, c)
        elif name == "lat":
            self.pe_transpose(pe, name, b, c, body, self.xn, self.xn_ready, b + 1)
        elif name == "q":
            bank = ring.claim(pe, c, body)
            self.ready(pe, "lat", b, c)
            for m in range(4):
                for f in range(DC):
                    ins = nc.tensor.matmul(bank[:, m * T:(m + 1) * T], W["xq"][:, f, m * P:(m + 1) * P],
                                           self.kv[:, f, S2:S2 + T], start=(f == 0), stop=(f == DC - 1))
            ring.filled(ins, c)
        elif name in ("k0", "k1", "k2", "k3"):
            bank = ring.claim(pe, c, body)
            m = int(name[1])
            if m == 0:
                self.ready(pe, "ctx0", b, c)
                self.ready(pe, "ctx1", b, c)
            for f in range(DC):
                ins = nc.tensor.matmul(bank[:, 0:XK], W["xkv"][:, f, m * P:(m + 1) * P], self.kv[:, f, :],
                                       start=(f == 0), stop=(f == DC - 1))
            ring.filled(ins, c)
        elif name[0] == "v":
            bank = ring.claim(pe, c, body)
            i = int(name[1])
            for f in range(DC):
                ins = nc.tensor.matmul(bank[0:XCK, :], self.kv[:, f, i * XCK:(i + 1) * XCK], W["xkv"][:, f, 512:1024],
                                       start=(f == 0), stop=(f == DC - 1))
            ring.filled(ins, c)
        else:
            self.end_pe(pe, name, b, par, c, body, W["xo"])

    def pe_scores(self, pe, b, u, par, bank):
        if u == 0:
            self.ready(pe, "k3", b)
        return self.nc.tensor.matmul(bank[0:T, 0:XK], self.q[par][:, u // 2, u % 2, :], self.k[par][:, u // 2, :],
                                     start=True, stop=True)

    def pe_values(self, pe, b, u, par, probs, out):
        if u == 0:
            self.ready(pe, "v2", b)
            self.ready(pe, "v3", b)
        for i in range(XC):
            ins = self.nc.tensor.matmul(out[XD * (u % 2):XD * (u % 2 + 1), (u // 2) * T:(u // 2 + 1) * T],
                                        self.v[par][0:XCK, i, u * XD:(u + 1) * XD], probs[0:XCK, i * T:(i + 1) * T],
                                        start=(i == 0), stop=(i == XC - 1))
        return ins

    def act(self, act, name, b, par, c, body):
        nc, ring, W = self.nc, self.ring, self.W
        if name in ("ctx0", "ctx1"):
            f = int(name[3])
            bank = ring.take(act, c, body)
            ring.freed(nc.scalar.activation(self.kv[:, f, 0:S2], bank[:, 0:S2], ACT.Identity,
                                            bias=W["lnx"][:, 1, f:f + 1], scale=W["lnx"][:, 0, f:f + 1]), c)
        elif name == "lat":
            bank = ring.take(act, c, body)
            for f in range(DC):
                ins = nc.scalar.activation(self.kv[:, f, S2:S2 + T], bank[:, f * T:(f + 1) * T], ACT.Identity,
                                           bias=W["lnl"][:, 1, f:f + 1], scale=W["lnl"][:, 0, f:f + 1])
            ring.freed(ins, c)
        elif name == "q":
            bank = ring.take(act, c, body)
            for i in range(2):
                half = slice(XD * i, XD * (i + 1))
                ins = nc.scalar.activation(self.q[par][half, :, i, :],
                                           bank[half, 0:4 * T].rearrange("p (m t) -> p m t", m=4), ACT.Copy)
            ring.freed(ins, c)
        elif name in ("k0", "k1", "k2", "k3"):
            self.copy_out(act, c, body, self.k[par][:, int(name[1]), :], lambda bank: bank[:, 0:XK])
        elif name[0] == "v":
            self.copy_out(act, c, body, self.v[par][0:XCK, int(name[1]), :], lambda bank: bank[0:XCK, :])

    def arrived(self, eng):
        eng.wait_ge(self.W["cross"]["loaded"], 16 * len(self.W["cross"]["loads"]))

    def pe_start(self, pe):
        self.arrived(pe)

    def act_start(self, act):
        self.arrived(act)
        act.wait_ge(self.set_up, 7)

    def dve_bound(self, dve, u, par, b, hold, bank):
        return self.nc.vector.scalar_tensor_tensor(hold, bank, -BIG, self.keep[par][0:T, :].unsqueeze(1),
                                                   ALU.max, ALU.min)

    def dve_start(self, dve, chain):
        self.arrived(dve)
        dve.wait_ge(self.set_up, 7)

    def dve(self, dve, name, b, par, c, body, chain):
        nc, ring, X = self.nc, self.ring, self.X
        ctx = self.ctx[par]
        if name == "stats":
            self.norm_stats(self.norm, X[0:T, b, :], chain)
            dve.wait_ge(self.ctx_loaded[par], loads(b, par))
            for i in range(CC):
                ins = nc.vector.bn_stats(self.cstats[0:CK, i, :], ctx[0:CK, i, :])
            chain.link_apart(ins)
            for i in range(CC):
                ins = nc.vector.bn_aggr(self.cmv[0:CK, i, :], self.cstats[0:CK, i, :])
            chain.link(ins)
            nc.vector.tensor_scalar(self.cvar[0:CK, :], self.cmv[0:CK, :, 1], EPS, None,
                                    ALU.add).then_inc(self.cvar_ready, 1)
        elif name == "k0":
            dve.wait_ge(self.mask_loaded[par], loads(b, par))
            nc.vector.tensor_scalar(self.keep[par][0:T, 0:S2], self.mask[par][0:T, :], 2 * BIG, -BIG,
                                    ALU.mult, ALU.add).then_inc(self.mask_used, 1)
            dve.wait_ge(self.mask_used, b + 1)
        elif name == "again":
            self.reuse(dve, "lat", b)
            chain.link(self.norm_scale(dve, self.norm, b, self.xn[0:T, :], X[0:T, b, :]))
            self.norm_stats(self.norm2, self.xn[0:T, :], chain)
            self.reuse(dve, "ctx0", b)
            self.reuse(dve, "ctx1", b)
            dve.wait_ge(self.crstd_ready, b + 1)
            for i in range(CC):
                ins = nc.vector.tensor_scalar(self.ctx_n[0:CK, i, :], ctx[0:CK, i, :], self.cmv[0:CK, i, 0:1],
                                              self.crstd[0:CK, i:i + 1], ALU.subtract, ALU.mult)
            ins.then_inc(self.ctx_ready, 1)
        elif name == "scale":
            self.norm_scale(dve, self.norm2, b, self.xn[0:T, :], self.xn[0:T, :]).then_inc(self.xn_ready, 1)
        elif name == "project":
            bank = ring.take(dve, c, body)
            self.norm_stats(self.out_norm, bank[0:T, 0:D], chain)
            dve.wait_ge(self.out_norm.rstd_ready, b + 1)
            n = self.out_norm
            ring.freed(nc.vector.tensor_scalar(self.out2[0:T, :], bank[0:T, 0:D], n.mv[0:T, 0:1], n.rstd[0:T, :],
                                               ALU.subtract, ALU.mult), c)
            ring.emptied(dve, c, body)
            lno = self.W["lno"]
            chain.link(nc.vector.tensor_tensor(self.out2[0:T, :], self.out2[0:T, :], lno[0:T, 0, :], ALU.mult))
            chain.link(nc.vector.tensor_tensor(self.out2[0:T, :], self.out2[0:T, :], lno[0:T, 1, :], ALU.add))
            chain.link(nc.vector.tensor_tensor(X[0:T, b, :], X[0:T, b, :], self.out2[0:T, :], ALU.add))
        elif name == "spread":
            self.end_dve(dve, name, b, par, c, body)


def load_context(phase, sp, before_reuse, masks=None):
    ctx = phase.G["t"]["ctx_1024"]

    def load(b, par, before):
        if before is not None:
            before_reuse(before)
        sp.dma_start(phase.ctx[par][0:CK, :, :],
                     ctx[b].rearrange("(c p) d -> p c d", p=CK)).then_inc(phase.ctx_loaded[par], 16)
        if masks is not None:
            sp.dma_start(phase.mask[par][0:T, :], masks[b].partition_broadcast(T)).then_inc(phase.mask_loaded[par], 16)

    load(0, 0, None)
    load(1, 1, None)
    load(2, 0, 0)
    load(3, 1, 1)
    if phase.NB > 4:
        with sp.Fori(0, (phase.NB - 4) // 2) as it:
            load(it * 2 + 4, 0, it * 2 + 2)
            load(it * 2 + 5, 1, it * 2 + 3)


def loads(b, par):
    if isinstance(b, int):
        return 16 * (b // 2 + 1)
    return (b - par) * 8 + 16


class RotaryAttention(Phase):
    tag = "a1"
    width, ck, nt, heads = HS * T, T, HS, HS
    scale = 24 ** -0.5

    def __init__(self, nc, G, W):
        super().__init__(nc, G, W)
        self.plan = Plan(4, ["xT", "c", "kr"],
                         {0: ["stats", "turnk", "q"], 1: ["scale", "project", "turnq"], 2: ["xT", "kc"],
                          3: ["kr", "v", "c", "spread"]}, late=["project"])

    def allocate(self, sb, sem):
        self.norm = self.allocate_norm(sb, sem)
        self.xn, self.xT = sb("xn", [P, D]), sb("xT", [P, DC, T])
        self.c, self.kr, self.q_raw = sb("c", [P, T]), sb("kr", [P, T]), sb("q_raw", [P, HG, T])
        self.q_plain, self.q_turned = sb("q_plain", [P, HG, T]), sb("q_turned", [P, HG, T])
        self.kr_plain, self.kr_turned = sb("kr_plain", [P, T]), sb("kr_turned", [P, T])
        self.q = [sb(f"q{i}", [P, HG, HS, T]) for i in range(2)]
        self.k = [sb(f"k{i}", [P, HG, T]) for i in range(2)]
        self.v = [sb(f"v{i}", [P, H, SLOT]) for i in range(2)]
        self.xn_ready = sem("xn_ready")
        self.plain_ready, self.q_ready, self.set_up = sem("plain_ready"), sem("q_ready"), sem("set_up")

    def act_start(self, act):
        act.wait_ge(self.set_up, 2)

    def dve_start(self, dve, chain):
        for i in range(2):
            self.nc.vector.memset(self.v[i][:], 1.0).then_inc(self.set_up, 1)

    def pool(self, pool, name, b, par, chain):
        if name == "stats":
            self.norm_power(pool, self.norm, b)
        elif name == "q":
            self.ready(pool, "q", b)
            self.nc.gpsimd.tensor_tensor(self.q_plain[:], self.q_raw[:], bc(self.const("cosA"), 1, HG),
                                         ALU.mult).then_inc(self.plain_ready, 1)

    def pe(self, pe, name, b, par, c, body):
        nc, ring, W = self.nc, self.ring, self.W
        if name == "xT":
            self.pe_transpose(pe, name, b, c, body, self.xn, self.xn_ready, b + 1)
        elif name in ("c", "kr"):
            bank = ring.claim(pe, c, body)
            if name == "c":
                self.ready(pe, "xT", b, c)
            for f in range(DC):
                ins = nc.tensor.matmul(bank[:, 0:T], W["a" + name][:, f, :], self.xT[:, f, :],
                                       start=(f == 0), stop=(f == DC - 1))
            ring.filled(ins, c)
        elif name in ("q", "kc"):
            bank = ring.claim(pe, c, body)
            if name == "q":
                self.ready(pe, "c", b, c)
            for g in range(HG):
                ins = nc.tensor.matmul(bank[:, g * T:(g + 1) * T], W["a" + name][:, g * P:(g + 1) * P], self.c[:, :],
                                       start=True, stop=True)
            ring.filled(ins, c)
        elif name in ("turnq", "turnk"):
            bank = ring.claim(pe, c, body)
            self.ready(pe, "q" if name == "turnq" else "kr", b, c)
            src = self.q_raw[:].rearrange("p g t -> p (g t)") if name == "turnq" else self.kr[:, :]
            ring.filled(nc.tensor.matmul(bank[:, 0:src.shape[1]], self.const("turnA"), src, start=True, stop=True), c)
        elif name == "v":
            bank = ring.claim(pe, c, body)
            ring.filled(nc.tensor.matmul(bank[0:T, 0:D], self.c[:, :], W["av"][:, :], start=True, stop=True), c)
        else:
            self.end_pe(pe, name, b, par, c, body, W["ao"])

    def pe_scores(self, pe, b, u, par, bank):
        if u == 0:
            pe.wait_ge(self.q_ready, b + 1)
            self.ready(pe, "kc", b)
        for a in range(HS):
            ins = self.nc.tensor.matmul(bank[0:T, a * T:(a + 1) * T], self.q[par][:, u, a, :], self.k[par][:, u, :],
                                        start=True, stop=True)
        return ins

    def act(self, act, name, b, par, c, body):
        if name == "xT":
            self.copy_out(act, c, body, self.xT[:].rearrange("p f t -> p (f t)"), lambda bank: bank[:, 0:DC * T])
        elif name in ("c", "kr"):
            if name == "kr":
                self.reuse(act, "turnk", b)
            self.copy_out(act, c, body, {"c": self.c, "kr": self.kr}[name][:, :], lambda bank: bank[:, 0:T])
        elif name == "q":
            self.copy_out(act, c, body, self.q_raw[:].rearrange("p g t -> p (g t)"), lambda bank: bank[:, 0:HG * T])
        elif name == "v":
            self.copy_out(act, c, body, self.v[par][0:T, :, 0:HD],
                          lambda bank: bank[0:T, 0:D].rearrange("t (h d) -> t h d", h=H))

    def dve_bound(self, dve, u, par, b, hold, bank):
        return self.nc.vector.scalar_tensor_tensor(hold, bank, -80.0, bc(self.const("keep1", T), 1, HS),
                                                   ALU.max, ALU.min)

    def dve(self, dve, name, b, par, c, body, chain):
        nc, ring, X, const = self.nc, self.ring, self.X, self.const
        if name == "stats":
            self.norm_stats(self.norm, X[0:T, b, :], chain)
        elif name == "scale":
            self.reuse(dve, "xT", b)
            self.norm_scale(dve, self.norm, b, self.xn[0:T, :], X[0:T, b, :]).then_inc(self.xn_ready, 1)
        elif name == "turnq":
            bank = ring.take(dve, c, body)
            ring.freed(nc.vector.tensor_tensor(self.q_turned[:], bank[:, 0:HG * T].rearrange("p (g t) -> p g t", g=HG),
                                               bc(const("sinA"), 1, HG), ALU.mult), c)
            ring.emptied(dve, c, body)
            dve.wait_ge(self.plain_ready, b + 1)
            chain.link(nc.vector.tensor_tensor(self.q_turned[:], self.q_turned[:], self.q_plain[:], ALU.add))
            self.widen(self.q[par][:], self.q_turned[:].rearrange("p g t -> p (g t)"), const("mask4"), HG, HS,
                       T).then_inc(self.q_ready, 1)
        elif name == "turnk":
            bank = ring.take(dve, c, body)
            chain.link(nc.vector.tensor_tensor(self.kr_plain[:, :], self.kr[:, :], const("cosA"), ALU.mult))
            ring.freed(nc.vector.tensor_tensor(self.kr_turned[:, :], bank[:, 0:T], const("sinA"), ALU.mult), c)
            ring.emptied(dve, c, body)
            chain.link(nc.vector.tensor_tensor(self.kr_turned[:, :], self.kr_turned[:, :], self.kr_plain[:, :],
                                               ALU.add))
        elif name == "kc":
            bank = ring.take(dve, c, body)
            ring.freed(nc.vector.tensor_tensor(self.k[par][:], bank[:, 0:HG * T].rearrange("p (g t) -> p g t", g=HG),
                                               bc(self.kr_turned[:, :], 1, HG), ALU.add), c)
        else:
            self.end_dve(dve, name, b, par, c, body)


class ContextAttention(Phase):
    tag = "x1"
    bounds = False
    together = HS
    exp_lag = 0
    width, ck, nt, heads = S2, CK, CC, 1
    scale = HD ** -0.5

    def __init__(self, nc, G, W):
        super().__init__(nc, G, W)
        self.plan = Plan(H, ["xT", "ctx0", "ctx1"],
                         {0: ["stats", "k0"], 1: ["k1"], 2: ["scale"], 3: ["spread"], 4: ["turnk0"],
                          5: ["turnk1"], 6: ["q"], 7: ["project"], 8: ["turnq"], 9: ["v0"], 10: ["v1"], 11: ["v2"],
                          13: ["xT"], 14: ["ctx0"], 15: ["ctx1"]})

    def allocate(self, sb, sem):
        self.norm = self.allocate_norm(sb, sem)
        self.ctx = [sb(f"ctx{i}", [P, CC, D]) for i in range(2)]
        self.ctx_loaded = [sem(f"ctx_loaded{i}") for i in range(2)]
        self.ctxT = sb("ctxT", [P, DC, S2])
        self.xn, self.xT = sb("xn", [P, D]), sb("xT", [P, DC, T])
        self.q_raw, self.k_raw = sb("q_raw", [P, DC, T]), sb("k_raw", [P, DC, S2])
        self.q_plain, self.k_plain = sb("q_plain", [P, DC, T]), sb("k_plain", [P, DC, S2])
        self.q_turned, self.k_turned = sb("q_turned", [P, DC, T]), sb("k_turned", [P, DC, S2])
        self.q = [sb(f"q{i}", [P, DC, 8, T]) for i in range(2)]
        self.k = [sb(f"k{i}", [P, DC, S2]) for i in range(2)]
        self.v = [sb(f"v{i}", [P, CC, H, SLOT]) for i in range(2)]
        self.xn_ready = sem("xn_ready")
        self.q_plain_ready, self.k_plain_ready = sem("q_plain_ready"), sem("k_plain_ready")
        self.q_ready, self.k_ready, self.set_up = sem("q_ready"), sem("k_ready"), sem("set_up")

    def sync(self, sp):
        load_context(self, sp, lambda before: self.ready(sp, "ctx1", before))

    def act_start(self, act):
        act.wait_ge(self.set_up, 2)

    def dve_start(self, dve, chain):
        for i in range(2):
            self.nc.vector.memset(self.v[i][:], 1.0).then_inc(self.set_up, 1)

    def pool(self, pool, name, b, par, chain):
        nc = self.nc
        if name == "stats":
            self.norm_power(pool, self.norm, b)
        elif name == "q":
            self.ready(pool, "q", b)
            nc.gpsimd.tensor_tensor(self.q_plain[:], self.q_raw[:], bc(self.const("cosX")[:, 0:T], 1, DC),
                                    ALU.mult).then_inc(self.q_plain_ready, 1)
        elif name in ("k0", "k1"):
            self.ready(pool, name, b)
            g = int(name[1])
            nc.gpsimd.tensor_tensor(self.k_plain[:, g, :], self.k_raw[:, g, :], self.const("cosX"),
                                    ALU.mult).then_inc(self.k_plain_ready, 1)

    def pe(self, pe, name, b, par, c, body):
        nc, ring, W = self.nc, self.ring, self.W
        if name in ("ctx0", "ctx1"):
            f = int(name[3])
            bank = ring.claim(pe, c, body)
            if f == 0:
                pe.wait_ge(self.ctx_loaded[par], loads(b, par))
            for i in range(CC):
                ins = nc.tensor.transpose(bank[:, i * CK:(i + 1) * CK], self.ctx[par][0:CK, i, f * P:(f + 1) * P],
                                          self.const("ident", CK)[:, 0:CK])
            ring.filled(ins, c)
        elif name == "xT":
            self.pe_transpose(pe, name, b, c, body, self.xn, self.xn_ready, b + 1)
        elif name == "q":
            self.pe_columns(pe, c, body, W["cq"], self.xT, b, "xT")
        elif name in ("k0", "k1"):
            bank = ring.claim(pe, c, body)
            g = int(name[1])
            if g == 0:
                self.ready(pe, "ctx0", b, c)
                self.ready(pe, "ctx1", b, c)
            for f in range(DC):
                ins = nc.tensor.matmul(bank[:, 0:S2], W["ck"][:, f, g * P:(g + 1) * P], self.ctxT[:, f, :],
                                       start=(f == 0), stop=(f == DC - 1))
            ring.filled(ins, c)
        elif name == "turnq":
            bank = ring.claim(pe, c, body)
            self.ready(pe, "q", b, c)
            ring.filled(nc.tensor.matmul(bank[:, 0:DC * T], self.const("turnX"),
                                         self.q_raw[:].rearrange("p g t -> p (g t)"), start=True, stop=True), c)
        elif name in ("turnk0", "turnk1"):
            bank = ring.claim(pe, c, body)
            g = int(name[5])
            self.ready(pe, "k" + name[5], b, c)
            ring.filled(nc.tensor.matmul(bank[:, 0:S2], self.const("turnX"), self.k_raw[:, g, :],
                                         start=True, stop=True), c)
        elif name[0] == "v":
            i = int(name[1])
            self.pe_rows(pe, c, body, self.ctxT[:, :, i * CK:(i + 1) * CK], W["cv"], CK)
        else:
            self.end_pe(pe, name, b, par, c, body, W["co"])

    def pe_scores(self, pe, b, u, par, bank):
        if u == 0:
            pe.wait_ge(self.q_ready, b + 1)
            pe.wait_ge(self.k_ready, b + 1)
        return self.nc.tensor.matmul(bank[0:T, 0:S2], self.q[par][:, u // 8, u % 8, :], self.k[par][:, u // 8, :],
                                     start=True, stop=True)

    def pe_values(self, pe, b, u, par, probs, out):
        if u == 0:
            self.ready(pe, "v1", b)
            self.ready(pe, "v2", b)
        a, g = u % HS, u // HS
        for i in range(CC):
            ins = self.nc.tensor.matmul(out[SLOT * a:SLOT * (a + 1), g * T:(g + 1) * T], self.v[par][0:CK, i, u, :],
                                        probs[0:CK, i * T:(i + 1) * T], start=(i == 0), stop=(i == CC - 1))
        return ins

    def act(self, act, name, b, par, c, body):
        if name in ("ctx0", "ctx1"):
            self.copy_out(act, c, body, self.ctxT[:, int(name[3]), :], lambda bank: bank[:, 0:S2])
        elif name == "xT":
            self.copy_out(act, c, body, self.xT[:].rearrange("p f t -> p (f t)"), lambda bank: bank[:, 0:DC * T])
        elif name == "q":
            self.copy_out(act, c, body, self.q_raw[:].rearrange("p f t -> p (f t)"), lambda bank: bank[:, 0:DC * T])
        elif name in ("k0", "k1"):
            self.copy_out(act, c, body, self.k_raw[:, int(name[1]), :], lambda bank: bank[:, 0:S2])
        elif name[0] == "v":
            self.copy_out(act, c, body, self.v[par][0:CK, int(name[1]), :, 0:HD],
                          lambda bank: bank[0:CK, 0:D].rearrange("t (h d) -> t h d", h=H))

    def dve(self, dve, name, b, par, c, body, chain):
        nc, ring, X, const = self.nc, self.ring, self.X, self.const
        if name == "stats":
            self.norm_stats(self.norm, X[0:T, b, :], chain)
        elif name == "scale":
            self.reuse(dve, "xT", b)
            self.norm_scale(dve, self.norm, b, self.xn[0:T, :], X[0:T, b, :]).then_inc(self.xn_ready, 1)
        elif name == "turnq":
            bank = ring.take(dve, c, body)
            ring.freed(nc.vector.tensor_tensor(self.q_turned[:], bank[:, 0:DC * T].rearrange("p (g t) -> p g t", g=DC),
                                               bc(const("sinX")[:, 0:T], 1, DC), ALU.mult), c)
            ring.emptied(dve, c, body)
            dve.wait_ge(self.q_plain_ready, b + 1)
            chain.link(nc.vector.tensor_tensor(self.q_turned[:], self.q_turned[:], self.q_plain[:], ALU.add))
            self.widen(self.q[par][:], self.q_turned[:].rearrange("p g t -> p (g t)"), const("mask8"), DC, 8,
                       T).then_inc(self.q_ready, 1)
        elif name in ("turnk0", "turnk1"):
            g = int(name[5])
            bank = ring.take(dve, c, body)
            ring.freed(nc.vector.tensor_tensor(self.k_turned[:, g, :], bank[:, 0:S2], const("sinX"), ALU.mult), c)
            ring.emptied(dve, c, body)
            dve.wait_ge(self.k_plain_ready, b * 2 + g + 1)
            ins = nc.vector.tensor_tensor(self.k[par][:, g, :], self.k_turned[:, g, :], self.k_plain[:, g, :],
                                          ALU.add)
            if g == DC - 1:
                ins.then_inc(self.k_ready, 1)
        else:
            self.end_dve(dve, name, b, par, c, body)


class RelativeAttention(CausalAttention):
    tag = "r1"
    scale = HD ** -0.5

    def __init__(self, nc, G, W):
        super().__init__(nc, G, W)
        self.plan = Plan(4, ["xT"],
                         {0: ["q", "stats", "k"], 1: ["p0", "again", "p2", "p1", "project"],
                          2: ["p3", "p5", "p4", "scale", "v", "p6", "xT"], 3: ["p7", "spread"]}, late=["project"])

    def allocate(self, sb, sem):
        super().allocate(sb, sem)
        self.norm2 = self.allocate_norm(sb, sem, "2")
        self.set_up = sem("set_up")
        self.by_position = sb("by_position", [P, H, RPW])
        self.bias = [sb(f"bias{i}", [P, H, T]) for i in range(2)]
        self.scratch = [[self.nc.dram_tensor(f"by_position_{i}_{u}", [T, HS, RPW], F32).ap() for u in range(HG)]
                        for i in range(2)]
        self.by_position_ready = [sem(f"by_position_ready{u}") for u in range(HG)]
        self.written = [sem(f"written{u}") for u in range(HG)]
        self.bias_loaded = [[sem(f"bias_loaded{i}_{u}") for u in range(HG)] for i in range(2)]

    def sync(self, sp):
        def shift(b, par):
            if not isinstance(b, int):
                sp.wait_ge(self.scores_free, (b - 1) * HG)
            for u in range(HG + 1):
                if u < HG:
                    sp.wait_ge(self.by_position_ready[u], b * 16 + 16)
                    sp.dma_start(self.scratch[par][u],
                                 self.by_position[0:T, HS * u:HS * (u + 1), :]).then_inc(self.written[u], 16)
                if u > 0:
                    sp.wait_ge(self.written[u - 1], b * 16 + 16)
                    s = self.scratch[par][u - 1]
                    src = bass.AP(s.tensor, s.offset + T - 1, [(HS * RPW - 1, T), (RPW, HS), (1, T)])
                    sp.dma_start(self.bias[par][0:T, HS * (u - 1):HS * u, :],
                                 src).then_inc(self.bias_loaded[par][u - 1], 16)

        shift(0, 0)
        shift(1, 1)
        with sp.Fori(0, (self.NB - 2) // 2) as it:
            shift(it * 2 + 2, 0)
            shift(it * 2 + 3, 1)

    def act_start(self, act):
        act.wait_ge(self.set_up, 2)

    def dve_start(self, dve, chain):
        for i in range(2):
            self.nc.vector.memset(self.v[i][:], 1.0).then_inc(self.set_up, 1)

    def pool(self, pool, name, b, par, chain):
        if name == "stats":
            self.norm_power(pool, self.norm, b)
        elif name == "again":
            self.norm_power(pool, self.norm2, b)
        elif name in ("p1", "p3", "p5", "p7"):
            i = int(name[1])
            self.ready(pool, f"p{i - 1}", b)
            self.ready(pool, name, b)
            pool.sem_inc(self.by_position_ready[i // 2], 16)

    def pe(self, pe, name, b, par, c, body):
        nc, ring, W = self.nc, self.ring, self.W
        if name == "xT":
            self.pe_transpose(pe, name, b, c, body, self.xn, self.xn_ready, b + 1)
        elif name in ("q", "k"):
            self.pe_columns(pe, c, body, W["r" + name], self.xT, b, "xT" if name == "q" else None)
        elif name == "v":
            self.pe_rows(pe, c, body, self.xT, W["rv"], T)
        elif name[0] == "p" and name != "project":
            bank = ring.claim(pe, c, body)
            if name == "p0":
                self.ready(pe, "q", b, c)
            for i in range(2):
                h = 2 * int(name[1]) + i
                ins = nc.tensor.matmul(bank[0:T, i * RPW:(i + 1) * RPW], self.q[par][:, h // 8, h % 8, :],
                                       W["pT"][:, h // 8, :], start=True, stop=True)
            ring.filled(ins, c)
        else:
            self.end_pe(pe, name, b, par, c, body, W["ro"])

    def act(self, act, name, b, par, c, body):
        nc, ring = self.nc, self.ring
        if name == "xT":
            ln = self.W["rln"]
            bank = ring.take(act, c, body)
            for f in range(DC):
                ins = nc.scalar.activation(self.xT[:, f, :], bank[:, f * T:(f + 1) * T], ACT.Identity,
                                           bias=ln[:, 1, f:f + 1], scale=ln[:, 0, f:f + 1])
            ring.freed(ins, c)
        elif name == "k":
            self.copy_out(act, c, body, self.k[par][:].rearrange("p f t -> p (f t)"), lambda bank: bank[:, 0:DC * T])
        elif name == "v":
            self.copy_out(act, c, body, self.v[par][0:T, :, 0:HD],
                          lambda bank: bank[0:T, 0:D].rearrange("t (h d) -> t h d", h=H))
        elif name[0] == "p" and int(name[1]) % 2 == 0:
            i = int(name[1])
            at_least(act, self.written[i // 2], b * 16)
            self.copy_out(act, c, body, self.position_rows(i), lambda bank: bank[0:T, 0:2 * RPW])

    def position_rows(self, i):
        return self.by_position[0:T, 2 * i:2 * i + 2, :].rearrange("t h r -> t (h r)")

    def dve_bound(self, dve, u, par, b, hold, bank):
        dve.wait_ge(self.bias_loaded[par][u], loads(b, par))
        return self.nc.vector.tensor_tensor(hold, bank, self.bias[par][0:T, HS * u:HS * (u + 1), :], ALU.add)

    def dve(self, dve, name, b, par, c, body, chain):
        nc, ring, X, S = self.nc, self.ring, self.X, self.G["S2"]
        if name == "stats":
            self.norm_stats(self.norm, X[0:T, b, :], chain)
        elif name == "again":
            chain.link(self.norm_scale(dve, self.norm, b, S[0:T, b, :], X[0:T, b, :]))
            nc.vector.tensor_tensor(X[0:T, b, :], X[0:T, b, :], S[0:T, b, :], ALU.add)
            self.norm_stats(self.norm2, S[0:T, b, :], chain)
        elif name == "scale":
            self.reuse(dve, "xT", b)
            self.norm_scale(dve, self.norm2, b, self.xn[0:T, :], S[0:T, b, :]).then_inc(self.xn_ready, 1)
        elif name == "q":
            bank = ring.take(dve, c, body)
            ring.freed(self.widen(self.q[par][:], bank[:, 0:DC * T], self.const("mask8"), DC, 8, T), c)
        elif name in ("p1", "p3", "p5", "p7"):
            i = int(name[1])
            at_least(dve, self.written[i // 2], b * 16)
            bank = ring.take(dve, c, body)
            ring.freed(nc.vector.tensor_copy(self.position_rows(i), bank[0:T, 0:2 * RPW]), c)
        elif name == "project":
            bank = ring.take(dve, c, body)
            nc.vector.tensor_tensor(S[0:T, b, :], bank[0:T, 0:D], S[0:T, b, :], ALU.add)
            ring.freed(nc.vector.tensor_tensor(X[0:T, b, :], bank[0:T, 0:D], X[0:T, b, :], ALU.add), c)
        elif name == "spread":
            self.end_dve(dve, name, b, par, c, body)


def layer1_weights(nc, G, stack):
    t = G["t"]
    sb, _, sem = G["alloc"](stack, "w1")
    W = dict(ac=sb("ac", [P, DC, P]), akr=sb("akr", [P, DC, P]), aq=sb("aq", [P, H * SLOT]),
             akc=sb("akc", [P, H * SLOT]), av=sb("av", [P, D]), ao=sb("ao", [P, HG, D]),
             cq=sb("cq", [P, DC, D]), ck=sb("ck", [P, DC, D]), cv=sb("cv", [P, DC, D]), co=sb("co", [P, HG, D]),
             rq=sb("rq", [P, DC, D]), rk=sb("rk", [P, DC, D]), rv=sb("rv", [P, DC, D]), ro=sb("ro", [P, HG, D]),
             rln=sb("rln", [P, 2, DC]), pT=sb("pT", [P, DC, RPW]), wp=sb("wp", [P, DC, D]))
    R = 64
    rows = lambda name: t[name].rearrange("(c p) n -> p c n", p=P)
    loads = [(W["ac"][:, :, 0:R], rows("L1_attn_W_DQ")), (W["ac"][:, :, R:2 * R], rows("L1_attn_W_DKV")),
             (W["cq"][:], rows("x_qT")), (W["ck"][:], rows("x_kT")), (W["cv"][:], rows("x_vT")),
             (W["rq"][:], rows("L1_ffn_wq")), (W["rk"][:], rows("L1_ffn_wk")), (W["rv"][:], rows("L1_ffn_wv")),
             (W["wp"][:], rows("L1_ffn_wp"))] + columns(W["rln"], t["L1_ffn_ln1_g"], t["L1_ffn_ln1_b"])
    heads = lambda tile, a, b: tile[a:b, :].rearrange("p (h s) -> p h s", s=SLOT)
    slots = [(heads(W["aq"], 0, R)[:, :, 0:HD], t["L1_attn_W_UQ"].rearrange("r (h d) -> r h d", h=H)),
             (heads(W["aq"], 0, R)[:, :, HD:HD + 8], t["L1_attn_W_QR"].rearrange("r (h d) -> r h d", h=H)),
             (heads(W["akc"], R, 2 * R)[:, :, 0:HD], t["L1_attn_W_UK"].rearrange("r (h d) -> r h d", h=H)),
             (W["av"][R:2 * R, :], t["L1_attn_W_UV"]),
             (W["co"][HD:HD + 1, 0, :], t["L1_xattn_bo"].rearrange("(a n) -> a n", a=1))]
    for a in range(HS):
        s = slice(SLOT * a, SLOT * a + HD)
        slots += [(W["akr"][:, :, SLOT * a + HD:SLOT * a + HD + 8], rows("L1_attn_W_KR")),
                  (W["ao"][s, :, :], rows_in_slots(t["L1_attn_W_O"])[a]),
                  (W["co"][s, :, :], rows_in_slots(t["x_oT"])[a]),
                  (W["ro"][s, :, :], rows_in_slots(t["L1_ffn_wo"])[a])]
    return W, dict(loads=loads + slots, zero=[W[n] for n in ("akr", "aq", "akc", "av", "ao", "co", "ro")],
                   zeroed=sem("zeroed"), loaded=sem("loaded"))


def finish_layer1(nc, G, W, ahead):
    with ExitStack() as own:
        _, psum, sem = G["alloc"](own, "p1")
        banks = [psum("bank0"), psum("bank1")]
        made = sem("made")
        block = own.enter_context(nc.Block())
        pe_table = G["const"]("pe").rearrange("p (f r) -> p f r", f=DC)

        @block.tensor
        def _(pe):
            pe.wait_ge(ahead["loaded"], 16 * len(ahead["loads"]))
            for g in range(DC):
                for f in range(DC):
                    ins = nc.tensor.matmul(banks[g][:, 0:RPW], W["wp"][:, f, g * P:(g + 1) * P], pe_table[:, f, :],
                                           start=(f == 0), stop=(f == DC - 1))
                ins.then_inc(made, 1)

        @block.vector
        def _(dve):
            for g in range(DC):
                dve.wait_ge(made, g + 1)
                nc.vector.tensor_copy(W["pT"][:, g, :], banks[g][:, 0:RPW])


def run_attention(nc, G, kind, W):
    with ExitStack() as stack:
        attention(nc, G, stack, kind(nc, G, W))


def expert_weights(nc, G, stack, layer):
    t = G["t"]
    E = (8, 32)[layer]
    sb, _, sem = G["alloc"](stack, f"e{layer}")
    M = dict(layer=layer, E=E, up=sb("up", [P, DC, E, P]), down=sb("down", [P, E, D]), route=sb("route", [P, DC, E]))
    up, down, route = (("L0_ffn_W1", "L0_ffn_W2", "L0_ffn_router_w"), ("L1_ffn_keys", "L1_ffn_values", "L1_ffn_sel_w"))[layer]
    small = [(M["route"][:], t[route].rearrange("(c p) e -> p c e", p=P))]
    if layer == 0:
        M.update(b1=sb("b1", [P, E]), b2=sb("b2", [E, D]), rb=sb("rb", [P, E]))
        small += [(M["rb"][:], t["L0_ffn_router_b"].partition_broadcast(P)),
                  (M["b1"][:], t["b1T"]), (M["b2"][:], t["L0_ffn_b2"])]
    else:
        M.update(ln=sb("ln", [P, 2, DC]))
        small += columns(M["ln"], t["L1_ffn_ln2_g"], t["L1_ffn_ln2_b"])

    def some(a, b):
        return [(M["up"][:, c, a:b, :], t[up].rearrange("e (c p) f -> c p e f", p=P)[c][:, a:b, :]) for c in range(DC)] + \
               [(M["down"][:, a:b, :], t[down].rearrange("e f d -> f e d")[:, a:b, :])]

    M["group"] = 4
    M["groups"] = [dict(loads=some(a, a + 4), loaded=sem(f"loaded{a}")) for a in range(0, E, 4)]
    M["small"] = dict(loads=small, loaded=sem("small"))
    everything = dict(loads=small + some(0, E), zero=[], loaded=sem("everything"))
    M["everything"] = everything if layer == 0 else None
    return M, everything


def columns(tile, gain, bias):
    return [(tile[:, i, c:c + 1], v.rearrange("(c p a) -> c p a", p=P, a=1)[c])
            for i, v in enumerate((gain, bias)) for c in range(DC)]


def experts(nc, G, M):
    layer, E = M["layer"], M["E"]
    K = (2, 4)[layer]
    NB, X, const = G["NB"], G["X"], G["const"]
    SRC = (X, G.get("S2"))[layer]
    Q = 4
    NC = NB // Q
    with ExitStack() as stack:
        sb, psum, sem = G["alloc"](stack, f"m{layer}")
        names = (["xT0", "xT1", "route", "gates", "bias0", "bias1"], ["xT0", "xT1", "route0", "route1"])[layer]
        LA = len(names)
        ring = Ring([psum("ring0"), psum("ring1")], [sem("ring_full0"), sem("ring_full1")],
                    [sem("ring_free0"), sem("ring_free1")], LA)
        hidden_bank = [psum("hidden_bank0"), psum("hidden_bank1")]
        out_bank = [psum(f"out{i}") for i in range(4)]
        stats, mv = sb("stats", [P, Q, 6]), sb("mv", [P, Q, 2])
        var, rstd = sb("var", [P, Q]), sb("rstd", [P, Q])
        xn = sb("xn", [P, Q, D])
        xT = [sb(f"xT{i}", [P, DC, Q * T]) for i in range(2)]
        hidden = [sb(f"hidden{i}", [P, Q * T]) for i in range(2)]
        score, score_in = sb("score", [P, Q, E]), sb("score_in", [P, Q, E])
        peak, total, tops, above = sb("peak", [P, Q]), sb("total", [P, Q]), sb("tops", [P, Q, 8]), sb("above", [P, Q])
        more, equal, run, again = sb("more", [P, Q, E]), sb("equal", [P, Q, E]), sb("run", [P, Q, E]), sb("again", [P, Q, E])
        gate = [sb(f"gate{i}", [P, Q, E]) for i in range(2)]
        gatesT = sb("gatesT", [P, Q * T])
        var_ready, rstd_ready, xn_ready = sem("var_ready"), sem("rstd_ready"), sem("xn_ready")
        logits_ready, score_ready, gate_ready = sem("logits_ready"), sem("score_ready"), sem("gate_ready")
        hidden_full, hidden_ready = sem("hidden_full"), sem("hidden_ready")
        out_full, added = sem("out_full"), sem("added")
        restart_set, chain_sem, once, stored = sem("restart_set"), sem("chain"), sem("once"), sem("stored")
        restart = sb("restart", [P, Q, E])
        block = stack.enter_context(nc.Block())

        at = ({0: ["stats"], 1: ["scale"], 2: ["xT0"], 3: ["xT1"], 4: ["route"], 6: ["gates"], 7: ["bias0", "bias1"]},
              {0: ["stats"], 2: ["scale"], 4: ["xT0"], 6: ["xT1"], 8: ["route0"], 9: ["route1"]})[layer]
        order = sum((at[s] for s in sorted(at)), [])

        def spot(name, c):
            j = names.index(name)
            return (j, 0) if isinstance(c, int) and c == 0 else (LA + j, c - 1)

        def first(c):
            return isinstance(c, int) and c == 0

        def last(c):
            return isinstance(c, int) and c == NC - 1

        def driver(eng, piece, work, chain=None):
            for name in order:
                piece(name, 0, 0)

            def body(c, par):
                for e in range(E):
                    work(c, par, e)
                    if not last(c):
                        for name in at.get(e, ()):
                            piece(name, c + 1, 1 - par)
            over(eng, NC, body, chain)

        @block.sync
        def _(sp):
            if layer == 1:
                for part in [M["small"]] + M["groups"]:
                    for dst, src in part["loads"]:
                        sp.dma_start(dst, src).then_inc(part["loaded"], 16)
                for c in range(NC):
                    sp.wait_ge(added, (c + 1) * E * Q)
                    sp.dma_start(G["t"]["out"].rearrange("b t d -> t b d")[:, c * Q:(c + 1) * Q, :],
                                 X[0:T, c * Q:(c + 1) * Q, :]).then_inc(stored, 16)
                sp.wait_ge(stored, 16 * NC)

        def arrived(eng, part):
            eng.wait_ge(part["loaded"], 16 * len(part["loads"]))

        def small_arrived(eng):
            arrived(eng, M["everything"] if layer == 0 else M["small"])

        @block.gpsimd
        def _(pool):
            pool.memset(restart[:], 1.0).then_inc(restart_set, 1)
            pool.wait_ge(restart_set, 1)
            pool.memset(restart[:, :, 0:1], 0.0).then_inc(restart_set, 1)

            def piece(name, c, par):
                if name == "stats":
                    pool.wait_ge(var_ready, c + 1)
                    nc.gpsimd.tensor_tensor(rstd[0:T, :], var[0:T, :], G["half"][0:T, 0:Q],
                                            ALU.pow).then_inc(rstd_ready, 1)
            driver(pool, piece, lambda c, par, e: None)

        @block.tensor
        def _(pe):
            small_arrived(pe)

            def piece(name, c, par):
                if name in ("xT0", "xT1"):
                    f = int(name[2])
                    bank = ring.claim(pe, *spot(name, c))
                    pe.wait_ge(xn_ready, c + 1)
                    for i in range(Q):
                        ins = nc.tensor.transpose(bank[:, i * T:(i + 1) * T], xn[0:T, i, f * P:(f + 1) * P],
                                                  const("ident", T)[:, 0:T])
                    ring.filled(ins, spot(name, c)[0])
                elif name in ("route", "route0", "route1"):
                    which = range(Q) if name == "route" else range(2 * int(name[5]), 2 * int(name[5]) + 2)
                    bank = ring.claim(pe, *spot(name, c))
                    if name != "route1":
                        ring.emptied(pe, *spot("xT1", c))
                    for i in which:
                        for f in range(DC):
                            ins = nc.tensor.matmul(bank[0:T, (i - which[0]) * E:(i - which[0] + 1) * E],
                                                   xT[par][:, f, i * T:(i + 1) * T], M["route"][:, f, :],
                                                   start=(f == 0), stop=(f == DC - 1))
                    ring.filled(ins, spot(name, c)[0])
                elif name == "gates":
                    bank = ring.claim(pe, *spot(name, c))
                    pe.wait_ge(gate_ready, c + 1)
                    for i in range(Q):
                        ins = nc.tensor.transpose(bank[0:E, i * T:(i + 1) * T], gate[par][0:T, i, :],
                                                  const("ident", T)[:, 0:T])
                    ring.filled(ins, spot(name, c)[0])
                elif name in ("bias0", "bias1"):
                    bank = ring.claim(pe, *spot(name, c))
                    if name == "bias0":
                        ring.emptied(pe, *spot("gates", c))
                    for i in range(2):
                        j = 2 * int(name[4]) + i
                        ins = nc.tensor.matmul(bank[0:T, i * D:(i + 1) * D], gatesT[0:E, j * T:(j + 1) * T],
                                               M["b2"][:, :], start=True, stop=True)
                    ring.filled(ins, spot(name, c)[0])

            def up(c, par, e):
                n = c * E + e
                if layer == 1 and first(c) and e % M["group"] == 0:
                    arrived(pe, M["groups"][e // M["group"]])
                if e == 0:
                    ring.emptied(pe, *spot("xT0", c))
                    ring.emptied(pe, *spot("xT1", c))
                at_least(pe, hidden_ready, n - 1)
                for f in range(DC):
                    ins = nc.tensor.matmul(hidden_bank[e % 2][:, 0:Q * T], M["up"][:, f, e, :], xT[par][:, f, :],
                                           start=(f == 0), stop=(f == DC - 1))
                ins.then_inc(hidden_full, 1)

            def down(c, e):
                n = c * E + e
                pe.wait_ge(hidden_ready, n + 1)
                for i in range(Q):
                    if i % 2 == 0:
                        at_least(pe, added, (n - 2) * Q + i + 2)
                    ins = nc.tensor.matmul(out_bank[2 * (e % 2) + i // 2][0:T, (i % 2) * D:(i % 2 + 1) * D],
                                           hidden[e % 2][:, i * T:(i + 1) * T], M["down"][:, e, :],
                                           start=True, stop=True)
                    if i % 2:
                        ins.then_inc(out_full, 1)

            def work(c, par, e):
                if e == 0:
                    up(c, par, 0)
                if e + 1 < E:
                    up(c, par, e + 1)
                down(c, e)
            driver(pe, piece, work)

        @block.scalar
        def _(act):
            small_arrived(act)

            def piece(name, c, par):
                if name in ("xT0", "xT1"):
                    bank = ring.take(act, *spot(name, c))
                    f = int(name[2])
                    if layer == 0:
                        ins = nc.scalar.activation(xT[par][:, f, :], bank[:, 0:Q * T], ACT.Copy)
                    else:
                        ins = nc.scalar.activation(xT[par][:, f, :], bank[:, 0:Q * T], ACT.Identity,
                                                   bias=M["ln"][:, 1, f:f + 1], scale=M["ln"][:, 0, f:f + 1])
                    ring.freed(ins, spot(name, c)[0])
                elif name == "route":
                    act.wait_ge(logits_ready, c + 1)
                    nc.scalar.activation(score[0:T, :, :], score[0:T, :, :], ACT.Exp).then_inc(score_ready, 1)
                elif name in ("route0", "route1"):
                    bank = ring.take(act, *spot(name, c))
                    if name == "route0":
                        at_least(act, gate_ready, c)
                    i = 2 * int(name[5])
                    ring.freed(nc.scalar.activation(score[0:T, i:i + 2, :].rearrange("t q e -> t (q e)"),
                                                    bank[0:T, 0:2 * E], ACT.Sigmoid), spot(name, c)[0])
                elif name == "gates":
                    bank = ring.take(act, *spot(name, c))
                    ring.freed(nc.scalar.activation(gatesT[0:E, :], bank[0:E, 0:Q * T], ACT.Copy), spot(name, c)[0])

            def work(c, par, e):
                def hide(e):
                    n = c * E + e
                    act.wait_ge(hidden_full, n + 1)
                    at_least(act, out_full, 2 * (n - 1))
                    if layer == 0:
                        ins = nc.scalar.activation(hidden[e % 2][:, :], hidden_bank[e % 2][:, 0:Q * T], ACT.Gelu,
                                                   bias=M["b1"][:, e:e + 1])
                    else:
                        ins = nc.scalar.activation(hidden[e % 2][:, :], hidden_bank[e % 2][:, 0:Q * T], ACT.Relu)
                    ins.then_inc(hidden_ready, 1)
                if e == 0:
                    hide(0)
                if e + 1 < E:
                    hide(e + 1)
            driver(act, piece, work)

        @block.vector
        def _(dve):
            small_arrived(dve)
            chain = Chain(dve, chain_sem, once=once)
            dve.wait_ge(restart_set, 2)

            def flat(a):
                return a[0:T, :, :].rearrange("t q e -> t (q e)")

            def choose(c, par, score=score):
                kth = tops[0:T, :, K - 1]
                for i in range(Q):
                    ins = nc.vector.max(tops[0:T, i, :], score[0:T, i, :])
                chain.link(ins)
                chain.link(nc.vector.tensor_tensor(more[0:T, :, :], score[0:T, :, :], bc(kth, 2, E), ALU.is_gt))
                chain.link(nc.vector.tensor_tensor(equal[0:T, :, :], score[0:T, :, :], bc(kth, 2, E), ALU.is_equal))
                chain.link(nc.vector.tensor_reduce(above[0:T, :], more[0:T, :, :], AX_X, ALU.add))
                chain.link(nc.vector.tensor_tensor_scan(flat(run), flat(restart), flat(equal), 0.0, ALU.mult, ALU.add))
                chain.link(nc.vector.tensor_tensor(run[0:T, :, :], run[0:T, :, :], bc(above[0:T, :], 2, E), ALU.add))
                chain.link(nc.vector.scalar_tensor_tensor(flat(again), flat(run), float(K), flat(equal),
                                                          ALU.is_le, ALU.mult))
                chain.link(nc.vector.tensor_tensor(more[0:T, :, :], more[0:T, :, :], again[0:T, :, :], ALU.add))

            def piece(name, c, par):
                if name == "stats":
                    for i in range(Q):
                        ins = nc.vector.bn_stats(stats[0:T, i, :], SRC[0:T, c * Q + i, :])
                    chain.link_apart(ins)
                    for i in range(Q):
                        ins = nc.vector.bn_aggr(mv[0:T, i, :], stats[0:T, i, :])
                    chain.link(ins)
                    nc.vector.tensor_scalar(var[0:T, :], mv[0:T, :, 1], EPS, None, ALU.add).then_inc(var_ready, 1)
                elif name == "scale":
                    dve.wait_ge(rstd_ready, c + 1)
                    for i in range(Q):
                        ins = nc.vector.tensor_scalar(xn[0:T, i, :], SRC[0:T, c * Q + i, :], mv[0:T, i, 0:1],
                                                      rstd[0:T, i:i + 1], ALU.subtract, ALU.mult)
                    ins.then_inc(xn_ready, 1)
                elif name == "route":
                    bank = ring.take(dve, *spot(name, c))
                    ring.freed(nc.vector.tensor_tensor(score[0:T, :, :],
                                                       bank[0:T, 0:Q * E].rearrange("t (q e) -> t q e", e=E),
                                                       bc(M["rb"][0:T, :], 1, Q), ALU.add), spot(name, c)[0])
                    ring.emptied(dve, *spot(name, c))
                    chain.link(nc.vector.tensor_reduce(peak[0:T, :], score[0:T, :, :], AX_X, ALU.max))
                    nc.vector.tensor_tensor(score[0:T, :, :], score[0:T, :, :], bc(peak[0:T, :], 2, E),
                                            ALU.subtract).then_inc(logits_ready, 1)
                    dve.wait_ge(score_ready, c + 1)
                    chain.link(nc.vector.tensor_reduce(total[0:T, :], score[0:T, :, :], AX_X, ALU.add))
                    chain.link(nc.vector.reciprocal(total[0:T, :], total[0:T, :]))
                    chain.link_apart(nc.vector.tensor_tensor(score[0:T, :, :], score[0:T, :, :],
                                                             bc(total[0:T, :], 2, E), ALU.mult))
                    choose(c, par)
                    g = gate[par]
                    chain.link(nc.vector.tensor_tensor(more[0:T, :, :], more[0:T, :, :], score[0:T, :, :], ALU.mult))
                    chain.link(nc.vector.tensor_reduce(total[0:T, :], more[0:T, :, :], AX_X, ALU.add))
                    chain.link(nc.vector.reciprocal(total[0:T, :], total[0:T, :]))
                    nc.vector.tensor_tensor(g[0:T, :, :], more[0:T, :, :], bc(total[0:T, :], 2, E),
                                            ALU.mult).then_inc(gate_ready, 1)
                elif name == "route1":
                    ring.emptied(dve, *spot("route0", c))
                    ring.emptied(dve, *spot("route1", c))
                    chain.link_apart(nc.vector.tensor_copy(score_in[0:T, :, :], score[0:T, :, :]))
                    choose(c, par, score_in)
                    nc.vector.tensor_tensor(gate[par][0:T, :, :], more[0:T, :, :], score[0:T, :, :],
                                            ALU.mult).then_inc(gate_ready, 1)
                elif name in ("bias0", "bias1"):
                    bank = ring.take(dve, *spot(name, c))
                    i = c * Q + 2 * int(name[4])
                    if isinstance(c, int):
                        view = X[0:T, i:i + 2, :]
                    else:
                        view = X[0:T, bass.ds(i, 2), :]
                    ring.freed(nc.vector.tensor_tensor(view, bank[0:T, :].rearrange("t (q d) -> t q d", q=2), view,
                                                       ALU.add), spot(name, c)[0])

            def work(c, par, e):
                n = c * E + e
                if e == 0:
                    dve.wait_ge(gate_ready, c + 1)
                    if layer == 0:
                        ring.emptied(dve, *spot("bias0", c))
                        ring.emptied(dve, *spot("bias1", c))
                for i in range(Q):
                    if i % 2 == 0:
                        dve.wait_ge(out_full, 2 * n + i // 2 + 1)
                    at_least(dve, added, n * Q + i - (Q - 1))
                    row = X[0:T, c * Q + i, :]
                    nc.vector.scalar_tensor_tensor(row, out_bank[2 * (e % 2) + i // 2][0:T, (i % 2) * D:(i % 2 + 1) * D],
                                                   gate[par][0:T, i, e:e + 1], row, ALU.mult,
                                                   ALU.add).then_inc(added, 1)
            driver(dve, piece, work, chain)


_TRANSPOSED = {"v_wT": "L0_attn_v_w", "o_wT": "L0_attn_o_w", "x_qT": "L1_xattn_Wq", "x_kT": "L1_xattn_Wk",
               "x_vT": "L1_xattn_Wv", "x_oT": "L1_xattn_Wo"}


def kernel(**inputs):
    import concourse.bacc as _bacc
    from concourse.bass_utils import run_bass_kernel_spmd as _run

    nc = _bacc.Bacc("TRN2", target_bir_lowering=False, num_devices=1)
    arrays, t = {}, {}

    def give(name, a):
        arrays[f"in_{name}"] = a
        t[name] = nc.dram_tensor(f"in_{name}", a.shape, mybir.dt.from_np(a.dtype), kind="ExternalInput").ap()

    taken = set(_TRANSPOSED.values()) | {"L0_attn_q_a", "L0_attn_k_a", "L0_ffn_b1", "mask_BxS2_bk1"}
    for name, a in inputs.items():
        if name not in taken:
            give(name, np.ascontiguousarray(a))
    for name, source in _TRANSPOSED.items():
        give(name, np.ascontiguousarray(np.asarray(inputs[source]).T))
    for n in "qk":
        give(f"{n}_aT", np.ascontiguousarray(np.asarray(inputs[f"L0_attn_{n}_a"]).transpose(0, 2, 1)))
    give("b1T", np.ascontiguousarray(np.asarray(inputs["L0_ffn_b1"]).T))
    give("mask", np.ascontiguousarray(inputs["mask_BxS2_bk1"]))
    give("constants", constants())
    x = inputs["x"]
    t["out"] = nc.dram_tensor("out", x.shape, F32, kind="ExternalOutput").ap()
    decoder(nc, t)
    r = _run(nc, [arrays], core_ids=[0])
    return r.results[0]["out"]
```
